# Optimizing a Trainium2 kernel written in Bass

```python
import numpy as np
import jax
import jax.numpy as jnp

def _softmax(x, axis=-1):
    return jax.nn.softmax(x, axis=axis)

def _gelu(x):
    return jax.nn.gelu(x, approximate=True)

def _silu(x):
    return jax.nn.silu(x)

def _sigmoid(x):
    return jax.nn.sigmoid(x)

def _layernorm(x, axis=-1, eps=1e-05):
    m = jnp.mean(x, axis=axis, keepdims=True)
    v = jnp.var(x, axis=axis, keepdims=True)
    return (x - m) / jnp.sqrt(v + eps)

def _scatter_add(tgt, idx, src, axis=0):
    return tgt.at[idx].add(src)

def _segment_sum(src, seg, n):
    return jax.ops.segment_sum(src, seg, n)
kernel_name = 'mk_adaln_d2_jaxref_r8_fe3888'

def setup_inputs(seed: int=0):
    np.random.seed(seed)
    _w = jnp.asarray

    def _L0_attn_setup():
        import jax, jax.numpy as jnp
        import numpy as np
        import math
        B, T, DIM = (2, 256, 128)
        H, HD = (16, 64)
        WINDOW = 64
        EPS = 1e-06

        def get_alibi_slopes(n_heads):

            def _slopes_pow2(n):
                start = 2 ** (-2 ** (-(math.log2(n) - 3)))
                return [start * start ** i for i in range(n)]
            if math.log2(n_heads).is_integer():
                slopes = _slopes_pow2(n_heads)
            else:
                closest = 2 ** math.floor(math.log2(n_heads))
                slopes = _slopes_pow2(closest)
                extra = _slopes_pow2(2 * closest)
                slopes += extra[0::2][:n_heads - closest]
            return jnp.asarray(np.array(slopes, dtype=np.float32))

        def rmsnorm(x, w, eps=EPS):
            var = jnp.mean(jnp.square(x), axis=-1, keepdims=True)
            return x * jax.lax.rsqrt(var + eps) * w
        key = jax.random.key(seed)
        ks = jax.random.split(key, 8)
        s = 0.02
        return {'x': jax.random.normal(ks[0], (B, T, DIM), dtype=jnp.float32), 'wq': jax.random.normal(ks[1], (H * HD, DIM), dtype=jnp.float32) * s, 'wk': jax.random.normal(ks[2], (H * HD, DIM), dtype=jnp.float32) * s, 'wv': jax.random.normal(ks[3], (H * HD, DIM), dtype=jnp.float32) * s, 'wo': jax.random.normal(ks[4], (DIM, H * HD), dtype=jnp.float32) * s, 'q_norm_w': jnp.ones((H * HD,), dtype=jnp.float32), 'k_norm_w': jnp.ones((H * HD,), dtype=jnp.float32)}
    _L0_attn_in = _L0_attn_setup()

    def _L0_ffn_setup():
        import jax, jax.numpy as jnp
        import numpy as np
        D = 128
        E = 8
        K = 2
        DF = 512
        B, S = (2, 256)
        EPS_LN = 1e-05
        EPS_TOPK = 1e-08

        def _xavier(key, shape, fan_in, fan_out, dtype=jnp.float32):
            bound = float(np.sqrt(6.0 / (fan_in + fan_out)))
            return jax.random.uniform(key, shape, dtype, -bound, bound)
        key = jax.random.key(seed)
        kx, kg, k1, k2 = jax.random.split(key, 4)
        return {'x': jax.random.normal(kx, (B, S, D), jnp.float32), 'gamma': jnp.ones((D,), jnp.float32), 'beta': jnp.zeros((D,), jnp.float32), 'Wg': _xavier(kg, (E, D), D, E), 'bg': jnp.zeros((E,), jnp.float32), 'W1': _xavier(k1, (E, DF, D), D, DF), 'b1': jnp.zeros((E, DF), jnp.float32), 'W2': _xavier(k2, (E, D, DF), DF, D), 'b2': jnp.zeros((E, D), jnp.float32)}
    _L0_ffn_in = _L0_ffn_setup()
    _L0_c = _w((lambda *s: np.random.randn(*s).astype(np.float32) * 0.05)(4, 128))
    _L0_wmod = _w((lambda *s: np.random.randn(*s).astype(np.float32) * 0.05)(128, 6 * 128) * 128 ** (-0.5))

    def _L1_attn_setup():
        import jax, jax.numpy as jnp
        import numpy as np
        INDIM = 128
        NHEADS = 16
        DK = INDIM // NHEADS
        DV = INDIM // NHEADS
        B, S = (4, 256)
        key = jax.random.key(seed)
        ks = jax.random.split(key, 5)
        x = jax.random.normal(ks[0], (B, S, INDIM), dtype=jnp.float32)
        std_qk = np.sqrt(2.0 / (INDIM + DK)).astype(np.float32)
        std_v = np.sqrt(2.0 / (INDIM + DV)).astype(np.float32)
        Wq = jax.random.normal(ks[1], (NHEADS * DK, INDIM), dtype=jnp.float32) * std_qk
        Wk = jax.random.normal(ks[2], (NHEADS * DK, INDIM), dtype=jnp.float32) * std_qk
        Wv = jax.random.normal(ks[3], (NHEADS * DV, INDIM), dtype=jnp.float32) * std_v
        std_o = np.sqrt(2.0 / (NHEADS * DV + INDIM)).astype(np.float32)
        Wo = jax.random.normal(ks[4], (INDIM, NHEADS * DV), dtype=jnp.float32) * std_o
        bq = jnp.zeros((NHEADS * DK,), jnp.float32)
        bk = jnp.zeros((NHEADS * DK,), jnp.float32)
        bv = jnp.zeros((NHEADS * DV,), jnp.float32)
        bo = jnp.zeros((INDIM,), jnp.float32)
        return {'x': x, 'Wq': Wq, 'bq': bq, 'Wk': Wk, 'bk': bk, 'Wv': Wv, 'bv': bv, 'Wo': Wo, 'bo': bo}
    _L1_attn_in = _L1_attn_setup()

    def _L1_ffn_setup():
        import jax, jax.numpy as jnp
        import numpy as np
        EPS = 1e-05
        NUM_HEADS = 16
        NUM_KV_HEADS = 4
        NUM_EXPERTS = 8
        TOP_K = 2

        def _layernorm(x, w, b):
            mu = jnp.mean(x, axis=-1, keepdims=True)
            var = jnp.mean((x - mu) ** 2, axis=-1, keepdims=True)
            return (x - mu) * jax.lax.rsqrt(var + EPS) * w + b
        key = jax.random.key(seed)
        ks = jax.random.split(key, 8)
        S, B, H = (128, 4, 128)
        F = 256
        hd = H // NUM_HEADS
        qkv_out = (NUM_HEADS + 2 * NUM_KV_HEADS) * hd
        w_scale = 0.02
        return {'hidden_states': jax.random.normal(ks[0], (S, B, H), jnp.float32), 'ln1_weight': jnp.ones((H,), jnp.float32), 'ln1_bias': jnp.zeros((H,), jnp.float32), 'ln2_weight': jnp.ones((H,), jnp.float32), 'ln2_bias': jnp.zeros((H,), jnp.float32), 'qkv_weight': jax.random.normal(ks[1], (qkv_out, H), jnp.float32) * w_scale, 'proj_weight': jax.random.normal(ks[2], (H, H), jnp.float32) * w_scale, 'router_weight': jax.random.normal(ks[3], (NUM_EXPERTS, H), jnp.float32) * w_scale, 'moe_w1': jax.random.normal(ks[4], (NUM_EXPERTS, H, F), jnp.float32) * w_scale, 'moe_w2': jax.random.normal(ks[5], (NUM_EXPERTS, F, H), jnp.float32) * w_scale}
    _L1_ffn_in = _L1_ffn_setup()
    _L1_c = _w((lambda *s: np.random.randn(*s).astype(np.float32) * 0.05)(4, 128))
    _L1_wmod = _w((lambda *s: np.random.randn(*s).astype(np.float32) * 0.05)(128, 6 * 128) * 128 ** (-0.5))
    _d = {'L0_attn_x': _L0_attn_in['x'], 'L0_attn_wq': _L0_attn_in['wq'], 'L0_attn_wk': _L0_attn_in['wk'], 'L0_attn_wv': _L0_attn_in['wv'], 'L0_attn_wo': _L0_attn_in['wo'], 'L0_attn_q_norm_w': _L0_attn_in['q_norm_w'], 'L0_attn_k_norm_w': _L0_attn_in['k_norm_w'], 'L0_ffn_gamma': _L0_ffn_in['gamma'], 'L0_ffn_beta': _L0_ffn_in['beta'], 'L0_ffn_Wg': _L0_ffn_in['Wg'], 'L0_ffn_bg': _L0_ffn_in['bg'], 'L0_ffn_W1': _L0_ffn_in['W1'], 'L0_ffn_b1': _L0_ffn_in['b1'], 'L0_ffn_W2': _L0_ffn_in['W2'], 'L0_ffn_b2': _L0_ffn_in['b2'], 'L0_c': _L0_c, 'L0_wmod': _L0_wmod, 'L1_attn_Wq': _L1_attn_in['Wq'], 'L1_attn_bq': _L1_attn_in['bq'], 'L1_attn_Wk': _L1_attn_in['Wk'], 'L1_attn_bk': _L1_attn_in['bk'], 'L1_attn_Wv': _L1_attn_in['Wv'], 'L1_attn_bv': _L1_attn_in['bv'], 'L1_attn_Wo': _L1_attn_in['Wo'], 'L1_attn_bo': _L1_attn_in['bo'], 'L1_ffn_ln1_weight': _L1_ffn_in['ln1_weight'], 'L1_ffn_ln1_bias': _L1_ffn_in['ln1_bias'], 'L1_ffn_ln2_weight': _L1_ffn_in['ln2_weight'], 'L1_ffn_ln2_bias': _L1_ffn_in['ln2_bias'], 'L1_ffn_qkv_weight': _L1_ffn_in['qkv_weight'], 'L1_ffn_proj_weight': _L1_ffn_in['proj_weight'], 'L1_ffn_router_weight': _L1_ffn_in['router_weight'], 'L1_ffn_moe_w1': _L1_ffn_in['moe_w1'], 'L1_ffn_moe_w2': _L1_ffn_in['moe_w2'], 'L1_c': _L1_c, 'L1_wmod': _L1_wmod}
    _x0 = _d['L0_attn_x']
    _d['L0_attn_x'] = jax.random.normal(jax.random.fold_in(jax.random.key(seed), 1), (4, 1024, 128), dtype=_x0.dtype)
    del _x0
    return _d

def reference(L0_attn_x, L0_attn_wq, L0_attn_wk, L0_attn_wv, L0_attn_wo, L0_attn_q_norm_w, L0_attn_k_norm_w, L0_ffn_gamma, L0_ffn_beta, L0_ffn_Wg, L0_ffn_bg, L0_ffn_W1, L0_ffn_b1, L0_ffn_W2, L0_ffn_b2, L0_c, L0_wmod, L1_attn_Wq, L1_attn_bq, L1_attn_Wk, L1_attn_bk, L1_attn_Wv, L1_attn_bv, L1_attn_Wo, L1_attn_bo, L1_ffn_ln1_weight, L1_ffn_ln1_bias, L1_ffn_ln2_weight, L1_ffn_ln2_bias, L1_ffn_qkv_weight, L1_ffn_proj_weight, L1_ffn_router_weight, L1_ffn_moe_w1, L1_ffn_moe_w2, L1_c, L1_wmod):

    def _L0_attn_ref(x, wq, wk, wv, wo, q_norm_w, k_norm_w):
        import jax, jax.numpy as jnp
        import numpy as np
        import math
        B, T, DIM = (2, 256, 128)
        H, HD = (16, 64)
        WINDOW = 64
        EPS = 1e-06

        def get_alibi_slopes(n_heads):

            def _slopes_pow2(n):
                start = 2 ** (-2 ** (-(math.log2(n) - 3)))
                return [start * start ** i for i in range(n)]
            if math.log2(n_heads).is_integer():
                slopes = _slopes_pow2(n_heads)
            else:
                closest = 2 ** math.floor(math.log2(n_heads))
                slopes = _slopes_pow2(closest)
                extra = _slopes_pow2(2 * closest)
                slopes += extra[0::2][:n_heads - closest]
            return jnp.asarray(np.array(slopes, dtype=np.float32))

        def rmsnorm(x, w, eps=EPS):
            var = jnp.mean(jnp.square(x), axis=-1, keepdims=True)
            return x * jax.lax.rsqrt(var + eps) * w
        Bx, Tx, _ = x.shape
        scale = HD ** (-0.5)
        q = x @ wq.T
        k = x @ wk.T
        v = x @ wv.T
        q = rmsnorm(q, q_norm_w)
        k = rmsnorm(k, k_norm_w)
        q = q.reshape(Bx, Tx, H, HD).transpose(0, 2, 1, 3)
        k = k.reshape(Bx, Tx, H, HD).transpose(0, 2, 1, 3)
        v = v.reshape(Bx, Tx, H, HD).transpose(0, 2, 1, 3)
        scores = jnp.einsum('bhqd,bhkd->bhqk', q, k) * scale
        pos = jnp.arange(Tx)
        dist = pos[None, :] - pos[:, None]
        slopes = get_alibi_slopes(H)
        scores = scores + slopes[:, None, None] * dist[None, :, :].astype(jnp.float32)
        neg_inf = jnp.float32(-jnp.inf)
        causal = dist > 0
        if WINDOW > 0:
            causal = causal | (dist < -WINDOW)
        scores = jnp.where(causal[None, None], neg_inf, scores)
        weights = jax.nn.softmax(scores.astype(jnp.float32), axis=-1).astype(x.dtype)
        out = jnp.einsum('bhqk,bhkd->bhqd', weights, v)
        out = out.transpose(0, 2, 1, 3).reshape(Bx, Tx, H * HD)
        return out @ wo.T

    def _L0_ffn_ref(x, gamma, beta, Wg, bg, W1, b1, W2, b2):
        import jax, jax.numpy as jnp
        import numpy as np
        D = 128
        E = 8
        K = 2
        DF = 512
        B, S = (2, 256)
        EPS_LN = 1e-05
        EPS_TOPK = 1e-08

        def _xavier(key, shape, fan_in, fan_out, dtype=jnp.float32):
            bound = float(np.sqrt(6.0 / (fan_in + fan_out)))
            return jax.random.uniform(key, shape, dtype, -bound, bound)
        b, s, d = x.shape
        mu = jnp.mean(x, axis=-1, keepdims=True)
        var = jnp.mean((x - mu) ** 2, axis=-1, keepdims=True)
        xn = (x - mu) / jnp.sqrt(var + EPS_LN) * gamma + beta
        xf = xn.reshape(-1, d)
        logits = xf @ Wg.T + bg
        probs = jax.nn.softmax(logits, axis=-1)
        tp, ti = jax.lax.top_k(probs, K)
        tp = tp / (jnp.sum(tp, axis=-1, keepdims=True) + EPS_TOPK)
        w = jnp.sum(jax.nn.one_hot(ti, E, dtype=xf.dtype) * tp[..., None], axis=1)
        h = jax.nn.gelu(jnp.einsum('td,efd->tef', xf, W1) + b1, approximate=False)
        y = jnp.einsum('tef,edf->ted', h, W2) + b2
        out = jnp.einsum('ted,te->td', y, w)
        return x + out.reshape(b, s, d)

    def _L1_attn_ref(x, Wq, bq, Wk, bk, Wv, bv, Wo, bo):
        import jax, jax.numpy as jnp
        import numpy as np
        INDIM = 128
        NHEADS = 16
        DK = INDIM // NHEADS
        DV = INDIM // NHEADS
        B, S = (4, 256)
        b, s, _ = x.shape
        q = (x @ Wq.T + bq).reshape(b, s, NHEADS, DK)
        k = (x @ Wk.T + bk).reshape(b, s, NHEADS, DK)
        v = (x @ Wv.T + bv).reshape(b, s, NHEADS, DV)
        w = jnp.einsum('bshd,bzhd->bhsz', q, k)
        w = w / jnp.sqrt(jnp.float32(DV))
        w = jax.nn.softmax(w, axis=-1)
        vw = jnp.einsum('bhsz,bzhd->bshd', w, v)
        vw = vw.reshape(b, s, NHEADS * DV)
        out = vw @ Wo.T + bo
        return out

    def _L1_ffn_ref(hidden_states, ln1_weight, ln1_bias, ln2_weight, ln2_bias, qkv_weight, proj_weight, router_weight, moe_w1, moe_w2):
        import jax, jax.numpy as jnp
        import numpy as np
        EPS = 1e-05
        NUM_HEADS = 16
        NUM_KV_HEADS = 4
        NUM_EXPERTS = 8
        TOP_K = 2

        def _layernorm(x, w, b):
            mu = jnp.mean(x, axis=-1, keepdims=True)
            var = jnp.mean((x - mu) ** 2, axis=-1, keepdims=True)
            return (x - mu) * jax.lax.rsqrt(var + EPS) * w + b
        S, B, H = hidden_states.shape
        hd = H // NUM_HEADS
        rep = NUM_HEADS // NUM_KV_HEADS
        scale = 1.0 / hd ** 0.5
        ln1_out = _layernorm(hidden_states, ln1_weight, ln1_bias)
        qkv = jnp.einsum('sbh,oh->sbo', ln1_out, qkv_weight)
        q = qkv[..., :NUM_HEADS * hd].reshape(S, B, NUM_HEADS, hd)
        k = qkv[..., NUM_HEADS * hd:(NUM_HEADS + NUM_KV_HEADS) * hd].reshape(S, B, NUM_KV_HEADS, hd)
        v = qkv[..., (NUM_HEADS + NUM_KV_HEADS) * hd:].reshape(S, B, NUM_KV_HEADS, hd)
        k = jnp.repeat(k, rep, axis=2)
        v = jnp.repeat(v, rep, axis=2)
        scores = jnp.einsum('sbhd,tbhd->bhst', q, k) * scale
        causal = jnp.tril(jnp.ones((S, S), bool))
        scores = jnp.where(causal, scores, jnp.finfo(scores.dtype).min)
        probs = jax.nn.softmax(scores, axis=-1)
        attn = jnp.einsum('bhst,tbhd->sbhd', probs, v).reshape(S, B, H)
        proj_out = jnp.einsum('sbh,oh->sbo', attn, proj_weight)
        hidden_after_attn = hidden_states + proj_out
        ln2_out = _layernorm(hidden_after_attn, ln2_weight, ln2_bias)
        x = ln2_out.reshape(-1, H)
        logits = jnp.einsum('th,eh->te', x, router_weight)
        gate = jax.nn.softmax(logits, axis=-1)
        top_probs, top_idx = jax.lax.top_k(gate, TOP_K)
        h_mid = jax.nn.gelu(jnp.einsum('th,ehf->etf', x, moe_w1))
        expert_out = jnp.einsum('etf,efh->eth', h_mid, moe_w2)
        e_ids = jnp.arange(NUM_EXPERTS)[:, None, None]
        weights = jnp.sum(jnp.where(top_idx[None] == e_ids, top_probs[None], 0.0), axis=-1)
        moe_out = jnp.einsum('eth,et->th', expert_out, weights).reshape(S, B, H)
        return hidden_after_attn + moe_out
    x = L0_attn_x
    mod = (_silu(L0_c) @ L0_wmod).reshape(L0_c.shape[0], 6, 1, -1)
    sa, ca, ga, sb, cb, gb = (mod[:, 0], mod[:, 1], mod[:, 2], mod[:, 3], mod[:, 4], mod[:, 5])
    ga = (2 * (ga >= 0) - 1) * jnp.maximum(jnp.abs(ga), 0.25)
    gb = (2 * (gb >= 0) - 1) * jnp.maximum(jnp.abs(gb), 0.25)
    h = _layernorm(x, axis=-1) * (1 + ca) + sa
    x = x + ga * _L0_attn_ref(h, L0_attn_wq, L0_attn_wk, L0_attn_wv, L0_attn_wo, L0_attn_q_norm_w, L0_attn_k_norm_w)
    h = _layernorm(x, axis=-1) * (1 + cb) + sb
    x = x + gb * _L0_ffn_ref(h, L0_ffn_gamma, L0_ffn_beta, L0_ffn_Wg, L0_ffn_bg, L0_ffn_W1, L0_ffn_b1, L0_ffn_W2, L0_ffn_b2)
    mod = (_silu(L1_c) @ L1_wmod).reshape(L1_c.shape[0], 6, 1, -1)
    sa, ca, ga, sb, cb, gb = (mod[:, 0], mod[:, 1], mod[:, 2], mod[:, 3], mod[:, 4], mod[:, 5])
    ga = (2 * (ga >= 0) - 1) * jnp.maximum(jnp.abs(ga), 0.25)
    gb = (2 * (gb >= 0) - 1) * jnp.maximum(jnp.abs(gb), 0.25)
    h = _layernorm(x, axis=-1) * (1 + ca) + sa
    x = x + ga * _L1_attn_ref(h, L1_attn_Wq, L1_attn_bq, L1_attn_Wk, L1_attn_bk, L1_attn_Wv, L1_attn_bv, L1_attn_Wo, L1_attn_bo)
    h = _layernorm(x, axis=-1) * (1 + cb) + sb
    x = x + gb * _L1_ffn_ref(h, L1_ffn_ln1_weight, L1_ffn_ln1_bias, L1_ffn_ln2_weight, L1_ffn_ln2_bias, L1_ffn_qkv_weight, L1_ffn_proj_weight, L1_ffn_router_weight, L1_ffn_moe_w1, L1_ffn_moe_w2)
    return x

_drawn_inputs = setup_inputs


def setup_inputs(seed=0):
    import zlib

    import numpy as np

    out = dict(_drawn_inputs(seed))
    spreads = {'L0_attn_q_norm_w': (1.0, 0.6),
     'L0_attn_k_norm_w': (1.0, 0.6),
     'L0_ffn_gamma': (1.0, 0.2),
     'L0_ffn_beta': (0.0, 0.301),
     'L0_ffn_bg': (0.0, 0.517),
     'L0_ffn_b1': (0.0, 0.517),
     'L0_ffn_b2': (0.0, 0.426),
     'L1_attn_bq': (0.0, 0.8),
     'L1_attn_bk': (0.0, 0.8),
     'L1_attn_bv': (0.0, 0.301),
     'L1_attn_bo': (0.0, 0.348),
     'L1_ffn_ln1_weight': (1.0, 0.6),
     'L1_ffn_ln1_bias': (0.0, 0.8),
     'L1_ffn_ln2_weight': (1.0, 0.6),
     'L1_ffn_ln2_bias': (0.0, 0.8)}
    factors = {'L0_attn_wq': 5.09,
     'L0_attn_wk': 4.981,
     'L0_attn_wv': 3.728,
     'L0_attn_wo': 3.651,
     'L1_ffn_qkv_weight': 6.218,
     'L1_ffn_proj_weight': 6.074,
     'L1_ffn_router_weight': 8.0,
     'L1_ffn_moe_w1': 8.0,
     'L1_ffn_moe_w2': 8.0}
    for name, (base, spread) in spreads.items():
        noise = np.random.default_rng([zlib.crc32(name.encode()), seed]).standard_normal(out[name].shape)
        drawn = base * np.exp(spread * noise) if base else spread * noise
        out[name] = jnp.asarray(drawn.astype(out[name].dtype))
    for name, factor in factors.items():
        out[name] = (out[name] * factor).astype(out[name].dtype)
    return out
```

```python
from contextlib import ExitStack

import numpy as np

import concourse.bass as bass
from concourse import mybir

F32 = mybir.dt.float32
BF16 = mybir.dt.bfloat16
ALU = mybir.AluOpType
ACT = mybir.ActivationFunctionType
AX = mybir.AxisListType

P = 128
B, T, D = 4, 1024, 128
TPB = T // P
NT = B * TPB
CH = 512
NCH = B * T // CH
CPT = CH // P
LN_EPS = 1e-5
GATE_MIN = 0.25

H0, HD0, WIN = 16, 64, 64
PAIRS = H0 // 2
BLK = 64
NBLK = T // BLK
RMS_EPS = 1e-6
E = 8
F0, F1 = 512, 256
TOPK_EPS = 1e-8
H1, HD1 = 16, 8
QUADS = H1 // 4
KV2 = 4
QKV2 = H1 * HD1 + 2 * KV2 * HD1
Q_PART = (0, 0, 1, 1, 0, 2)
K_PART = (0, 1, 0, 1, 2, 0)
MROW = len(Q_PART) * HD1
KROWS = 96

SA, CA, GA, SB, CB, GB = range(6)


def bc(ap, axis, n):
    a = ap.unsqueeze(axis)
    shape = list(a.shape)
    shape[axis] = n
    return a.broadcast_to(shape)


class Core:

    def __init__(self, nc, ctx):
        self.nc, self.ctx = nc, ctx

    def sb(self, name, shape, dt=F32, ctx=None):
        return (ctx or self.ctx).enter_context(self.nc.sbuf_tensor(name, shape, dt))

    def ps(self, name, shape, ctx):
        return ctx.enter_context(self.nc.psum_tensor(name, shape, F32))

    def sems(self, ctx, prefix, *names):
        s = [self.nc.alloc_semaphore(f"{prefix}_{n}") for n in names]
        ctx.callback(self.clear, s)
        return s

    def clear(self, sems):
        self.nc.clear_and_free_semaphores(sems)
        self.nc.all_engine_barrier()

    def loop_sems(self, prefix, *names):
        s = [self.nc.alloc_semaphore(f"{prefix}_{n}") for n in names]
        numbers = [x.num for x in s]
        assert numbers == list(range(numbers[0], numbers[0] + len(s)))
        return s, range(numbers[0], numbers[0] + len(s))


def modulation_stage(nc, K, A):
    with ExitStack() as st:
        cT = K.sb("cT", [P, 2, B], ctx=st)
        wmod = K.sb("wmod", [P, 2, 6 * D], ctx=st)
        ex = K.sb("silu_exp", [P, 2, B], ctx=st)
        den = K.sb("silu_den", [P, 2, B], ctx=st)
        rec = K.sb("silu_rec", [P, 2, B], ctx=st)
        sil = K.sb("silu", [P, 2, B], ctx=st)
        silb = K.sb("silu_rows", [P, 2, B, P], ctx=st)
        sgn = K.sb("gate_sign", [P, 2, B, 2, D], ctx=st)
        mag = K.sb("gate_size", [P, 2, B, 2, D], ctx=st)
        colp = K.ps("mod_cols_ps", [P, 2, 6, B], st)
        rowp = [K.ps(f"mod_rows_ps{i}", [P, CH], st) for i in range(4)]
        (x_in, c_in, e_done, dve, cols_mm, rows_mm, rows_out) = K.sems(st, 
            "mod", "x_in", "c_in", "exp", "dve", "cols_mm", "rows_mm", "rows_out")
        half = 3 * D
        with nc.Block() as block:
            @block.sync
            def _(sp):
                for i, (c, w) in enumerate((("L0_c", "L0_wmod"), ("L1_c", "L1_wmod"))):
                    sp.dma_start(cT[:, i, :], A[c]).then_inc(c_in, 16)
                    sp.dma_start(wmod[:, i, :], A[w]).then_inc(c_in, 16)
                sp.dma_start(K.x[:], A["L0_attn_x"].rearrange("b (t p) d -> p (b t) d", p=P)).then_inc(x_in, 16)
                sp.dma_start(K.ident[:], A["identity"]).then_inc(x_in, 16)
                sp.wait_ge(x_in, 32)

            @block.scalar
            def _(act):
                act.wait_ge(c_in, 64)
                nc.scalar.activation(ex[:], cT[:], ACT.Exp, scale=-1.0).then_inc(e_done, 1)
                act.wait_ge(cols_mm, 1)
                nc.scalar.copy(K.mod_cols[:], colp[:]).then_inc(e_done, 1)

            @block.vector
            def _(dve_):
                v = nc.vector
                v.memset(K.neghalf[:], -0.5).then_inc(dve, 1)
                v.memset(K.ones[:], 1.0).then_inc(dve, 1)
                dve_.wait_ge(e_done, 1)
                v.tensor_scalar(den[:], ex[:], 1.0, None, ALU.add).then_inc(dve, 1)
                dve_.wait_ge(dve, 3)
                v.reciprocal(rec[:], den[:]).then_inc(dve, 1)
                dve_.wait_ge(dve, 4)
                v.tensor_tensor(sil[:], cT[:], rec[:], ALU.mult).then_inc(dve, 1)
                dve_.wait_ge(dve, 5)
                v.tensor_copy(silb[:], bc(sil[:], 3, P)).then_inc(dve, 1)
                for n in range(2 * B):
                    dve_.wait_ge(rows_mm, n + 1)
                    for j in range(2):
                        r = v.tensor_copy(K.mod_rows[:, n // B, n % B, 3 * j:3 * j + 3, :],
                                          rowp[2 * (n % 2) + j][:, 0:half].rearrange("p (c d) -> p c d", c=3))
                    r.then_inc(rows_out, 1)
                dve_.wait_ge(rows_out, 2 * B)
                dve_.wait_ge(e_done, 2)
                for c in (CA, CB):
                    v.tensor_scalar(K.mod_cols[:, :, c, :], K.mod_cols[:, :, c, :], 1.0, None, ALU.add)
                    for l in range(2):
                        v.tensor_scalar(K.mod_rows[:, l, :, c, :], K.mod_rows[:, l, :, c, :], 1.0, None, ALU.add)
                for l in range(2):
                    for i, c in enumerate((GA, GB)):
                        g = K.mod_rows[:, l, :, c, :]
                        v.tensor_scalar(sgn[:, l, :, i, :], g, 0.0, 2.0, ALU.is_ge, ALU.mult).then_inc(dve, 1)
                        v.scalar_tensor_tensor(out=mag[:, l, :, i, :], in0=g, scalar=-1.0, in1=g, op0=ALU.mult,
                                               op1=ALU.max).then_inc(dve, 1)
                dve_.wait_ge(dve, 14)
                v.tensor_scalar(sgn[:], sgn[:], 1.0, None, ALU.subtract).then_inc(dve, 1)
                dve_.wait_ge(dve, 15)
                for l in range(2):
                    for i, c in enumerate((GA, GB)):
                        v.scalar_tensor_tensor(out=K.mod_rows[:, l, :, c, :], in0=mag[:, l, :, i, :],
                                               scalar=GATE_MIN, in1=sgn[:, l, :, i, :], op0=ALU.max, op1=ALU.mult)

            @block.tensor
            def _(pe):
                pe.wait_ge(dve, 6)
                pe.wait_ge(c_in, 64)
                for l in range(2):
                    for c in range(6):
                        m = nc.tensor.matmul(colp[:, l, c, :], wmod[:, l, c * D:(c + 1) * D], sil[:, l, :],
                                             start=True, stop=True)
                m.then_inc(cols_mm, 1)
                for n in range(2 * B):
                    if n >= 2:
                        pe.wait_ge(rows_out, n - 1)
                    for j in range(2):
                        m = nc.tensor.matmul(rowp[2 * (n % 2) + j][:, 0:half], silb[:, n // B, n % B, :],
                                             wmod[:, n // B, j * half:(j + 1) * half], start=True, stop=True)
                    m.then_inc(rows_mm, 1)


def norm_stage(nc, K, name, src, to_T=None, rows=None):
    with ExitStack() as st:
        stats = K.sb(name + "_stats", [P, NT, 6], ctx=st)
        mv = K.sb(name + "_mv", [P, NT, 2], ctx=st)
        ve = K.sb(name + "_ve", [P, NT], ctx=st)
        rstd = K.sb(name + "_rstd", [P, NT], ctx=st)
        hat = K.sb(name + "_hat", [P, NT, D], ctx=st)
        hp = [K.ps(f"{name}_ps{i}", [P, CPT, P], st) for i in range(NCH)] if to_T else None
        (st_done, mv_done, rs_done, hat_done, row_done, turned) = K.sems(st, 
            name, "stats", "meanvar", "rstd", "hat", "rows", "turned")
        with nc.Block() as block:
            @block.vector
            def _(dve):
                v = nc.vector
                for b in range(B):
                    for t in range(b * TPB, (b + 1) * TPB):
                        v.bn_stats(stats[:, t, :], src[:, t, :]).then_inc(st_done, 1)
                    for t in range(b * TPB, (b + 1) * TPB):
                        dve.wait_ge(st_done, t + 1)
                        v.bn_aggr(mv[:, t, :], stats[:, t, :]).then_inc(mv_done, 1)
                for b in range(B):
                    dve.wait_ge(rs_done, 2 * (b + 1))
                    for t in range(b * TPB, (b + 1) * TPB):
                        v.tensor_scalar(hat[:, t, :], src[:, t, :], mv[:, t, 0:1], rstd[:, t:t + 1],
                                        ALU.subtract, ALU.mult).then_inc(hat_done, 1)
                    if rows:
                        scale, bias = rows
                        h, o = hat[:, b * TPB:(b + 1) * TPB, :], K.nat[:, b * TPB:(b + 1) * TPB, :]
                        dve.wait_ge(hat_done, (b + 1) * TPB)
                        v.tensor_tensor(h, h, bc(scale(b), 1, TPB), ALU.mult).then_inc(row_done, 1)
                        dve.wait_ge(row_done, b + 1)
                        v.tensor_tensor(o, h, bc(bias(b), 1, TPB), ALU.add)

            @block.gpsimd
            def _(pool):
                g = nc.gpsimd
                for b in range(B):
                    s = slice(b * TPB, (b + 1) * TPB)
                    pool.wait_ge(mv_done, (b + 1) * TPB)
                    g.tensor_scalar(ve[:, s], mv[:, s, 1], LN_EPS, None, ALU.add).then_inc(rs_done, 1)
                    pool.wait_ge(rs_done, 2 * b + 1)
                    g.tensor_tensor(rstd[:, s], ve[:, s], K.neghalf[:, s], ALU.pow).then_inc(rs_done, 1)

            if to_T:
                @block.tensor
                def _(pe):
                    for c in range(NCH):
                        pe.wait_ge(hat_done, (c + 1) * CPT)
                        for t in range(CPT):
                            m = nc.tensor.transpose(hp[c][:, t, :], hat[:, c * CPT + t, :], K.ident[:])
                        m.then_inc(turned, 1)

                @block.scalar
                def _(act):
                    scale, bias = to_T
                    for c in range(NCH):
                        act.wait_ge(turned, c + 1)
                        b = c * CPT // TPB
                        nc.scalar.activation(K.hT[:, c * CH:(c + 1) * CH], hp[c][:].rearrange("p t d -> p (t d)"),
                                             ACT.Identity, bias=bias(b), scale=scale(b))


def rms_stage(nc, K, A, st, hq, hk):
    with ExitStack() as s2:
        wn = K.sb("w_nat", [P, 2, PAIRS, D], ctx=s2)
        gram = K.sb("gram", [P, 2, D], ctx=s2)
        z = K.sb("z", [P, 2, CH], ctx=s2)
        inv_d = K.sb("inv_d", [P, P], ctx=s2)
        ms = K.sb("mean_square", [P, 2, CH], ctx=s2)
        rr = K.sb("rrms", [P, 2, CH], ctx=s2)
        root = K.sb("root", [P, 2, CH], ctx=s2)
        gp = K.ps("gram_ps", [P, 2, D], s2)
        up = [K.ps(f"u_ps{i}", [P, CH], s2) for i in range(2)]
        sp_ = [K.ps(f"ssum_ps{i}", [P, CH], s2) for i in range(2)]
        (w_in, cst, g_mm, g_out, u_mm, z_done, s_mm, ms_done, root_done, r_done, scaled) = K.sems(s2, 
            "rms", "w_in", "const", "gram_mm", "gram_out", "u_mm", "z", "sum_mm", "ms", "root", "r", "scaled")
        units = [(c, i) for c in range(NCH) for i in range(2)]
        with nc.Block() as block:
            @block.sync
            def _(sp):
                for i, w in enumerate(("L0_attn_wq", "L0_attn_wk")):
                    sp.dma_start(wn[:, i], A[w].rearrange("(c p) d -> p c d", p=P)).then_inc(w_in, 16)

            @block.tensor
            def _(pe):
                pe.wait_ge(w_in, 32)
                for i in range(2):
                    for c in range(PAIRS):
                        m = nc.tensor.matmul(gp[:, i, :], wn[:, i, c, :], wn[:, i, c, :],
                                             start=(c == 0), stop=(c == PAIRS - 1))
                m.then_inc(g_mm, 1)
                pe.wait_ge(g_out, 1)
                pe.wait_ge(cst, 1)
                for n in range(len(units) + 1):
                    if n < len(units):
                        c, i = units[n]
                        if n >= 2:
                            pe.wait_ge(z_done, n - 1)
                        nc.tensor.matmul(up[n % 2][:], gram[:, i, :], K.hT[:, c * CH:(c + 1) * CH],
                                         start=True, stop=True).then_inc(u_mm, 1)
                    if n >= 1:
                        pe.wait_ge(z_done, n)
                        if n >= 3:
                            pe.wait_ge(ms_done, n - 2)
                        nc.tensor.matmul(sp_[(n - 1) % 2][:], inv_d[:], z[:, (n - 1) % 2, :],
                                         start=True, stop=True).then_inc(s_mm, 1)

            @block.scalar
            def _(act):
                act.wait_ge(g_mm, 1)
                nc.scalar.copy(gram[:], gp[:]).then_inc(g_out, 1)
                for n in range(len(units)):
                    act.wait_ge(ms_done, n + 1)
                    if n >= 2:
                        act.wait_ge(r_done, n - 1)
                    nc.scalar.activation(root[:, n % 2, :], ms[:, n % 2, :], ACT.Sqrt).then_inc(root_done, 1)

            @block.vector
            def _(dve):
                v = nc.vector
                v.memset(inv_d[:], 1.0 / (H0 * HD0)).then_inc(cst, 1)
                for n in range(len(units) + 2):
                    if n < len(units):
                        c, i = units[n]
                        dve.wait_ge(u_mm, n + 1)
                        if n >= 2:
                            dve.wait_ge(s_mm, n - 1)
                        v.tensor_tensor(z[:, n % 2, :], up[n % 2][:], K.hT[:, c * CH:(c + 1) * CH],
                                        ALU.mult).then_inc(z_done, 1)
                    if 1 <= n <= len(units):
                        dve.wait_ge(s_mm, n)
                        if n >= 3:
                            dve.wait_ge(root_done, n - 2)
                        v.tensor_scalar(ms[:, (n - 1) % 2, :], sp_[(n - 1) % 2][:], 0.0, RMS_EPS,
                                        ALU.max, ALU.add).then_inc(ms_done, 1)
                    if n >= 2:
                        k = n - 2
                        dve.wait_ge(root_done, k + 1)
                        if k >= 2:
                            dve.wait_ge(scaled, k - 1)
                        v.reciprocal(rr[:, k % 2, :], root[:, k % 2, :]).then_inc(r_done, 1)

            @block.gpsimd
            def _(pool):
                g = nc.gpsimd
                for n, (c, i) in enumerate(units):
                    pool.wait_ge(r_done, n + 1)
                    g.tensor_tensor((hq, hk)[i][:, c * CH:(c + 1) * CH], K.hT[:, c * CH:(c + 1) * CH],
                                    rr[:, n % 2, :], ALU.mult).then_inc(scaled, 1)


def window_attention_stage(nc, K, A):
    with ExitStack() as st:
        hq = K.sb("hq", [P, B * T], ctx=st)
        hk = K.sb("hk", [P, B * T], ctx=st)
        rms_stage(nc, K, A, st, hq, hk)
        wq = K.sb("wqT", [P, PAIRS, P], ctx=st)
        wk = K.sb("wkT", [P, PAIRS, P], ctx=st)
        wv = K.sb("wvT", [P, PAIRS, P], ctx=st)
        wo = K.sb("woT", [P, PAIRS, D], ctx=st)
        nbias = K.sb("nbias", [P, PAIRS, 2, P], ctx=st)
        qn = K.sb("qn", [P, 2, PAIRS], ctx=st)
        qs = K.sb("qscale", [P, PAIRS], ctx=st)
        hb = K.nat[:, 0:TPB, :].rearrange("p t d -> p (t d)")
        qbd = K.sb("q_bd", [P, 2, NBLK, P], ctx=st)
        kk = K.sb("k_pad", [P, 2, BLK + T], ctx=st)
        vv = K.sb("v_tiles", [P, 2, TPB, P], ctx=st)
        vs = K.sb("v_shift", [P, 2, TPB, P], ctx=st)
        sb_ = K.sb("s_biased", [P, 4, 4, P], ctx=st)
        mn = K.sb("s_min", [P, 4, 4], ctx=st)
        pr = K.sb("probs", [P, 4, 4, P], ctx=st)
        sm = K.sb("p_sum", [P, 4, 4], ctx=st)
        ri = K.sb("p_rsum", [P, 4, 4], ctx=st)
        pt = K.sb("probsT", [P, 2, 4, P], ctx=st)
        oT = K.sb("oT", [P, 2, T], ctx=st)
        tmp = K.nat[:, TPB:2 * TPB, :]
        pj = [K.ps(f"proj_ps{i}", [P, CH], st) for i in range(2)]
        sp_ = [K.ps(f"score_ps{i}", [P, 4, P], st) for i in range(2)]
        tp = K.ps("probsT_ps", [P, 4, P], st)
        op = K.ps("o_ps", [P, 4, BLK], st)
        wp = [K.ps(f"wo_ps{i}", [P, CPT, D], st) for i in range(2)]
        (w_in, qs_d, z_d) = K.sems(st, "win0", "w_in", "qscale", "zeros")
        with nc.Block() as block:
            @block.sync
            def _(sp):
                for dst, w in ((wq, "L0_attn_wqT"), (wk, "L0_attn_wkT"), (wv, "L0_attn_wvT")):
                    sp.dma_start(dst[:].rearrange("p c o -> p (c o)"), A[w]).then_inc(w_in, 16)
                sp.dma_start(wo[:], A["L0_attn_woT"].rearrange("(c p) d -> p c d", p=P)).then_inc(w_in, 16)
                sp.dma_start(nbias[:], A["neg_bias"]).then_inc(w_in, 16)
                sp.dma_start(qn[:, 0, :], A["L0_attn_q_norm_c"]).then_inc(w_in, 16)
                sp.dma_start(qn[:, 1, :], A["L0_attn_k_norm_c"]).then_inc(w_in, 16)
                sp.wait_ge(w_in, 7 * 16)

            @block.vector
            def _(dve):
                dve.wait_ge(w_in, 7 * 16)
                nc.vector.scalar_tensor_tensor(out=qs[:], in0=qn[:, 0, :], scalar=-HD0 ** -0.5, in1=qn[:, 1, :],
                                               op0=ALU.mult, op1=ALU.mult)

            @block.gpsimd
            def _(pool):
                nc.gpsimd.memset(qbd[:].rearrange("p a b c -> p (a b c)"), 0.0)
                nc.gpsimd.memset(kk[:, :, 0:BLK], 0.0)
                nc.gpsimd.memset(vs[0:BLK, :, 0, :], 0.0)

        ((h_in, p_mm, a_out, q_out, v_sh0, v_sh1, s_mm, biased, exped, rsum, normed, turned, pt_out, pv_mm, o_out,
          wo_mm, xt), clear) = K.win_sems
        v_sh = (v_sh0, v_sh1)
        GRP = NBLK // 4
        G = PAIRS * GRP
        units = [(h, u) for h in range(PAIRS) for u in range(6)]

        def unit_steps(g):
            h = g // GRP + 1
            if h >= PAIRS or g >= G:
                return []
            return [6 * h + u for u in ((0, 1), (2, 3), (4,), (5,))[g % GRP]]

        with nc.Fori(0, B) as b:
            with nc.Block() as block:
                @block.tensor
                def _(pe):
                    def project(n):
                        h, u = units[n]
                        if n >= 2:
                            hh, uu = units[n - 2]
                            pe.wait_ge(a_out, n - 1)
                            if uu < 2:
                                pe.wait_ge(q_out, 2 * hh + uu + 1)
                        half = u % 2
                        tok = bass.ds(b * T + half * CH, CH)
                        if u < 4:
                            w, src = ((wq, hq), (wk, hk))[u // 2]
                            m = nc.tensor.matmul(pj[n % 2][:], w[:, h, :], src[:, tok], start=True, stop=True)
                        else:
                            for t in range(CPT):
                                m = nc.tensor.matmul(pj[n % 2][:, t * P:(t + 1) * P],
                                                     hb[:, half * CH + t * P:half * CH + (t + 1) * P],
                                                     wv[:, h, :], start=True, stop=True)
                        m.then_inc(p_mm, 1)

                    pe.wait_ge(h_in, 1)
                    for n in range(6):
                        project(n)
                    for g in range(G + 4):
                        h, r = divmod(g, GRP)
                        if g < G:
                            if r == 0:
                                pe.wait_ge(a_out, 6 * h + 4)
                                pe.wait_ge(q_out, 2 * h + 2)
                            if g >= 2:
                                pe.wait_ge(biased, g - 1)
                            for i in range(4):
                                j = 4 * r + i
                                m = nc.tensor.matmul(sp_[g % 2][:, i, :], qbd[:, h % 2, j, :],
                                                     kk[:, h % 2, BLK * j:BLK * j + P], start=True, stop=True)
                            m.then_inc(s_mm, 1)
                        for n in unit_steps(g):
                            project(n)
                        if 2 <= g < G + 2:
                            k = g - 2
                            pe.wait_ge(normed, k + 1)
                            if k >= 1:
                                pe.wait_ge(pt_out, k)
                            for i in range(4):
                                m = nc.tensor.transpose(tp[:, i, :], pr[:, k % 4, i, :], K.ident[:])
                            m.then_inc(turned, 1)
                        if 3 <= g < G + 3:
                            k = g - 3
                            hh, rr = divmod(k, GRP)
                            pe.wait_ge(pt_out, k + 1)
                            if rr == 0:
                                pe.wait_ge(a_out, 6 * hh + 6)
                                pe.wait_ge(v_sh[hh % 2], 32 * (hh // 2 + 1))
                            if k >= 1:
                                pe.wait_ge(o_out, k)
                            for i in range(4):
                                j = 4 * rr + i
                                src = (vs, vv)[j % 2][:, hh % 2, j // 2, :]
                                for a in range(2):
                                    m = nc.tensor.matmul(op[a * BLK:(a + 1) * BLK, i, :], src[:, a * HD0:(a + 1) * HD0],
                                                         pt[:, k % 2, i, a * BLK:(a + 1) * BLK], start=True, stop=True)
                            m.then_inc(pv_mm, 1)
                        if g >= 4 and (g - 4) % GRP == GRP - 1:
                            hh = (g - 4) // GRP
                            pe.wait_ge(o_out, GRP * (hh + 1))
                            for t in range(TPB):
                                m = nc.tensor.matmul(wp[t // CPT][:, t % CPT, :], oT[:, hh % 2, t * P:(t + 1) * P],
                                                     wo[:, hh, :], start=(hh == 0 and t % CPT == 0),
                                                     stop=(hh == PAIRS - 1), skip_group_check=True)
                            m.then_inc(wo_mm, 1)

                @block.scalar
                def _(act):
                    def evacuate(n):
                        h, u = units[n]
                        half = u % 2
                        act.wait_ge(p_mm, n + 1)
                        if u == 0 and h >= 2:
                            act.wait_ge(s_mm, GRP * (h - 1))
                        if u == 4 and h >= 2:
                            act.wait_ge(pv_mm, GRP * (h - 1))
                            act.wait_ge(v_sh[h % 2], 32 * (h // 2))
                        if u < 2:
                            r = nc.scalar.activation(
                                qbd[0:BLK, h % 2, half * 8:half * 8 + 8, 0:BLK],
                                pj[n % 2][0:BLK, :].rearrange("p (j q) -> p j q", q=BLK), ACT.Copy, scale=qs[0:BLK, h:h + 1])
                        elif u < 4:
                            r = nc.scalar.copy(kk[:, h % 2, BLK + half * CH:BLK + (half + 1) * CH], pj[n % 2][:])
                        else:
                            r = nc.scalar.copy(vv[:, h % 2, half * CPT:(half + 1) * CPT, :],
                                               pj[n % 2][:].rearrange("p (t d) -> p t d", d=P))
                        r.then_inc(a_out, 1)

                    nc.scalar.copy(hb, K.hT[:, bass.ds(b * T, T)]).then_inc(h_in, 1)
                    for n in range(6):
                        evacuate(n)
                    for g in range(G + 3):
                        for n in unit_steps(g):
                            evacuate(n)
                        if g < G:
                            act.wait_ge(biased, g + 1)
                            if g >= 4:
                                act.wait_ge(turned, g - 3)
                            for i in range(4):
                                r = nc.scalar.activation(pr[:, g % 4, i, :], sb_[:, g % 4, i, :], ACT.Exp, scale=-1.0,
                                                         bias=mn[:, g % 4, i:i + 1], accum_out=sm[:, g % 4, i:i + 1])
                            r.then_inc(exped, 1)
                        if g >= 3:
                            k = g - 3
                            act.wait_ge(pv_mm, k + 1)
                            if k % GRP == 0 and k >= 2 * GRP:
                                act.wait_ge(wo_mm, k // GRP - 1)
                            nc.scalar.copy(oT[:, k // GRP % 2, (k % GRP) * 256:(k % GRP + 1) * 256],
                                           op[:].rearrange("p i q -> p (i q)")).then_inc(o_out, 1)

                @block.vector
                def _(dve):
                    v = nc.vector

                    def evacuate(n):
                        h, u = units[n]
                        if u >= 2:
                            return
                        dve.wait_ge(p_mm, n + 1)
                        if u == 0 and h >= 2:
                            dve.wait_ge(s_mm, GRP * (h - 1))
                        v.tensor_scalar(qbd[BLK:P, h % 2, u * 8:u * 8 + 8, BLK:P],
                                        pj[n % 2][BLK:P, :].rearrange("p (j q) -> p j q", q=BLK),
                                        qs[BLK:P, h:h + 1], None, ALU.mult).then_inc(q_out, 1)

                    for n in range(6):
                        evacuate(n)
                    for g in range(G + 2):
                        h, r = divmod(g, GRP)
                        for n in unit_steps(g):
                            evacuate(n)
                        if g < G:
                            dve.wait_ge(s_mm, g + 1)
                            if g >= 4:
                                dve.wait_ge(exped, g - 3)
                            for i in range(4):
                                first = 1 if 4 * r + i == 0 else 0
                                q = v.tensor_tensor_reduce(sb_[:, g % 4, i, :], sp_[g % 2][:, i, :],
                                                           nbias[:, h, first, :], 1.0, 3e38, ALU.add, ALU.min,
                                                           mn[:, g % 4, i:i + 1])
                            q.then_inc(biased, 1)
                        if 1 <= g < G + 1:
                            dve.wait_ge(exped, g)
                            v.reciprocal(ri[:, (g - 1) % 4, :], sm[:, (g - 1) % 4, :]).then_inc(rsum, 1)
                        if g >= 2:
                            k = g - 2
                            dve.wait_ge(turned, k + 1)
                            if k >= 2:
                                dve.wait_ge(pv_mm, k - 1)
                            v.tensor_copy(pt[:, k % 2], tp[:]).then_inc(pt_out, 1)
                    dve.wait_ge(wo_mm, PAIRS)
                    for i in range(2):
                        v.tensor_tensor(tmp[:, i * CPT:(i + 1) * CPT, :], wp[i][:],
                                        bc(K.mod_rows[:, 0, bass.ds(b, 1), GA, :].rearrange("p a d -> p (a d)"), 1, CPT),
                                        ALU.mult).then_inc(xt, 1)
                    dve.wait_ge(xt, 2)
                    xs = K.x[:, bass.ds(b * TPB, TPB), :]
                    v.tensor_tensor(xs, xs, tmp, ALU.add)

                @block.gpsimd
                def _(pool):
                    for g in range(G):
                        pool.wait_ge(rsum, g + 1)
                        pb = pr[:, g % 4]
                        nc.gpsimd.tensor_tensor(pb, pb, bc(ri[:, g % 4, :], 2, P), ALU.mult).then_inc(normed, 1)

                @block.sync
                def _(sp):
                    for h in range(PAIRS):
                        sp.wait_ge(a_out, 6 * h + 6)
                        if h >= 2:
                            sp.wait_ge(pv_mm, GRP * (h - 1))
                        sp.dma_start(vs[BLK:P, h % 2], vv[0:BLK, h % 2]).then_inc(v_sh[h % 2], 16)
                        sp.dma_start(vs[0:BLK, h % 2, 1:TPB], vv[BLK:P, h % 2, 0:TPB - 1]).then_inc(v_sh[h % 2], 16)
                    sp.wait_ge(v_sh0, 16 * PAIRS)
                    sp.wait_ge(v_sh1, 16 * PAIRS)
            nc.all_engine_barrier(sems_to_clear=clear)


def routing_stage(nc, K, A, name, wgT, bias, b2, renormalise):
    with ExitStack() as st:
        wg = K.sb(name + "_wg", [P, E], ctx=st)
        bg = K.sb(name + "_bg", [P, E], ctx=st)
        b2s = K.sb(name + "_b2", [E, D], ctx=st)
        lg = K.sb(name + "_logits", [P, NT, E], ctx=st)
        mx = K.sb(name + "_max", [P, NT], ctx=st)
        ex = K.sb(name + "_exp", [P, NT, E], ctx=st)
        sm = K.sb(name + "_sum", [P, NT], ctx=st)
        rs = K.sb(name + "_rsum", [P, NT], ctx=st)
        pb = K.sb(name + "_probs", [P, NT, E], ctx=st)
        gt = K.sb(name + "_above", [P, NT, E * E], ctx=st)
        eq = K.sb(name + "_equal", [P, NT, E * E], ctx=st)
        low = K.sb(name + "_lower", [P, E * E], ctx=st)
        rank = K.sb(name + "_rank", [P, NT, E], ctx=st)
        wT = K.sb(name + "_wT", [E, NT, P], ctx=st)
        lp = K.ps(name + "_lps", [P, NT, E], st)
        tp = [K.ps(f"{name}_tps{i}", [P, CPT, P], st) for i in range(2)]
        bp = [K.ps(f"{name}_bps{i}", [P, CPT, D], st) for i in range(2)]
        (w_in, l_mm, dve, act_s, t_mm, t_out, b_mm, b_out) = K.sems(st, 
            name, "w_in", "logits_mm", "dve", "act", "turned", "wT_out", "b2_mm", "b2_out")
        n_in = 2 + (bias is not None) + (b2 is not None)
        grid = [P, NT, E, E]
        with nc.Block() as block:
            @block.sync
            def _(sp):
                sp.dma_start(wg[:], wgT).then_inc(w_in, 16)
                sp.dma_start(low[:], A["lower"]).then_inc(w_in, 16)
                if bias is not None:
                    sp.dma_start(bg[:], bias.partition_broadcast(P)).then_inc(w_in, 16)
                if b2 is not None:
                    sp.dma_start(b2s[:], b2).then_inc(w_in, 16)

            @block.tensor
            def _(pe):
                pe.wait_ge(w_in, 16 * n_in)
                for t in range(NT):
                    m = nc.tensor.matmul(lp[:, t, :], K.hT[:, t * P:(t + 1) * P], wg[:], start=True, stop=True)
                m.then_inc(l_mm, 1)
                if b2 is not None:
                    pe.wait_ge(dve, DONE)
                    for c in range(NCH):
                        if c >= 2:
                            pe.wait_ge(t_out, c - 1)
                        for t in range(CPT):
                            m = nc.tensor.transpose(tp[c % 2][0:E, t, :], K.w[:, c * CPT + t, :], K.ident[:])
                        m.then_inc(t_mm, 1)
                    for c in range(NCH):
                        pe.wait_ge(t_out, c + 1)
                        if c >= 2:
                            pe.wait_ge(b_out, c - 1)
                        for t in range(CPT):
                            m = nc.tensor.matmul(bp[c % 2][:, t, :], wT[:, c * CPT + t, :], b2s[:], start=True, stop=True)
                        m.then_inc(b_mm, 1)

            @block.scalar
            def _(act):
                act.wait_ge(dve, 2 + (bias is not None))
                nc.scalar.activation(ex[:], lg[:], ACT.Exp).then_inc(act_s, 1)
                if b2 is not None:
                    for c in range(NCH):
                        act.wait_ge(t_mm, c + 1)
                        nc.scalar.copy(wT[:, c * CPT:(c + 1) * CPT, :], tp[c % 2][0:E]).then_inc(t_out, 1)

            @block.vector
            def _(dve_):
                v = nc.vector
                n = [0]

                def step(ins):
                    n[0] += 1
                    ins.then_inc(dve, 1)
                    dve_.wait_ge(dve, n[0])

                dve_.wait_ge(w_in, 16 * n_in)
                dve_.wait_ge(l_mm, 1)
                if bias is not None:
                    step(v.tensor_tensor(lg[:], lp[:], bc(bg[:], 1, NT), ALU.add))
                    src = lg
                else:
                    src = lp
                step(v.tensor_reduce(mx[:], src[:], AX.X, ALU.max))
                step(v.tensor_tensor(lg[:], src[:], bc(mx[:], 2, E), ALU.subtract))
                dve_.wait_ge(act_s, 1)
                step(v.tensor_reduce(sm[:], ex[:], AX.X, ALU.add))
                step(v.reciprocal(rs[:], sm[:]))
                step(v.tensor_tensor(pb[:], ex[:], bc(rs[:], 2, E), ALU.mult))
                over = bc(pb[:], 2, E)
                own = bc(pb[:], 3, E)
                g4 = gt[:].rearrange("p t (a b) -> p t a b", a=E)
                e4 = eq[:].rearrange("p t (a b) -> p t a b", a=E)
                step(v.tensor_tensor(g4, over, own, ALU.is_gt))
                step(v.tensor_tensor(e4, over, own, ALU.is_equal))
                step(v.tensor_tensor(eq[:], eq[:], bc(low[:], 1, NT), ALU.mult))
                step(v.tensor_tensor(gt[:], gt[:], eq[:], ALU.add))
                step(v.tensor_reduce(rank[:], g4, AX.X, ALU.add))
                step(v.scalar_tensor_tensor(out=K.w[:], in0=rank[:], scalar=2.0, in1=pb[:], op0=ALU.is_lt,
                                            op1=ALU.mult))
                if renormalise:
                    step(v.tensor_reduce(sm[:], K.w[:], AX.X, ALU.add))
                    step(v.tensor_scalar(sm[:], sm[:], TOPK_EPS, None, ALU.add))
                    step(v.reciprocal(rs[:], sm[:]))
                    step(v.tensor_tensor(K.w[:], K.w[:], bc(rs[:], 2, E), ALU.mult))
                if b2 is not None:
                    assert n[0] == DONE
                    for c in range(NCH):
                        dve_.wait_ge(b_mm, c + 1)
                        h = K.nat[:, c * CPT:(c + 1) * CPT, :]
                        v.tensor_tensor(h, h, bp[c % 2][:], ALU.add).then_inc(b_out, 1)


DONE = 16


def expert_stage(nc, K, A, name, F, w1, w2, b1, gelu, layer):
    FC = F // P
    with ExitStack() as st:
        w1s = K.sb(name + "_w1", [P, E, F], ctx=st)
        w2s = K.sb(name + "_w2", [P, E, FC, D], ctx=st)
        b1s = K.sb(name + "_b1", [P, E * FC], ctx=st)
        hid = K.sb(name + "_hid", [P, 2, FC, CH], ctx=st)
        acc = K.sb(name + "_acc", [P, TPB, D], ctx=st)
        wb = K.sb(name + "_wb", [P, TPB, E], ctx=st)
        tmp = K.sb(name + "_tmp", [P, TPB, D], ctx=st)
        hp = [K.ps(f"{name}_hps{i}", [P, CH], st) for i in range(4)]
        yp = [K.ps(f"{name}_yps{i}", [P, CPT, D], st) for i in range(2)]
        (w_in,) = K.sems(st, name + "w", "w_in")
        (copied, h_mm, act_d, y_mm, y_add, xt), clear = K.moe_sems
        with nc.Block() as block:
            @block.sync
            def _(sp):
                for e in range(E):
                    sp.dma_start(w1s[:, e, :], w1[e]).then_inc(w_in, 16)
                    sp.dma_start(w2s[:, e], w2[e].rearrange("(c p) d -> p c d", p=P)).then_inc(w_in, 16)
                if b1 is not None:
                    sp.dma_start(b1s[:], b1).then_inc(w_in, 16)
                sp.wait_ge(w_in, 16 * (2 * E + (b1 is not None)))
        S = 2 * E
        with nc.Fori(0, B) as b:
            with nc.Block() as block:
                @block.tensor
                def _(pe):
                    for s in range(S + 1):
                        if s < S:
                            c, e = divmod(s, E)
                            for f in range(FC):
                                n = s * FC + f
                                if n >= 4:
                                    pe.wait_ge(act_d, n - 3)
                                nc.tensor.matmul(hp[n % 4][:], w1s[:, e, f * P:(f + 1) * P],
                                                 K.hT[:, bass.ds(b * T + c * CH, CH)],
                                                 start=True, stop=True).then_inc(h_mm, 1)
                        if s >= 1:
                            k = s - 1
                            pe.wait_ge(act_d, FC * (k + 1))
                            if k >= 2:
                                pe.wait_ge(y_add, CPT * (k - 1))
                            for t in range(CPT):
                                for f in range(FC):
                                    m = nc.tensor.matmul(yp[k % 2][:, t, :], hid[:, k % 2, f, t * P:(t + 1) * P],
                                                         w2s[:, k % E, f, :], start=(f == 0), stop=(f == FC - 1))
                            m.then_inc(y_mm, 1)

                @block.scalar
                def _(act):
                    for s in range(S):
                        if s >= 2:
                            act.wait_ge(y_mm, s - 1)
                        for f in range(FC):
                            n = s * FC + f
                            act.wait_ge(h_mm, n + 1)
                            col = s % E * FC + f
                            nc.scalar.activation(hid[:, s % 2, f, :], hp[n % 4][:], gelu,
                                                 bias=b1s[:, col:col + 1] if b1 is not None else 0.0
                                                 ).then_inc(act_d, 1)

                @block.gpsimd
                def _(pool):
                    nc.gpsimd.tensor_copy(wb[:], K.w[:, bass.ds(b * TPB, TPB), :]).then_inc(copied, 1)
                    nc.gpsimd.tensor_copy(acc[:], K.nat[:, bass.ds(b * TPB, TPB), :]).then_inc(copied, 1)

                @block.vector
                def _(dve):
                    v = nc.vector
                    dve.wait_ge(copied, 2)
                    for s in range(S):
                        c, e = divmod(s, E)
                        dve.wait_ge(y_mm, s + 1)
                        if e:
                            dve.wait_ge(y_add, CPT * s)
                        for t in range(CPT):
                            a = acc[:, c * CPT + t, :]
                            v.scalar_tensor_tensor(out=a, in0=yp[s % 2][:, t, :],
                                                   scalar=wb[:, c * CPT + t, e:e + 1], in1=a, op0=ALU.mult,
                                                   op1=ALU.add).then_inc(y_add, 1)
                    dve.wait_ge(y_add, CPT * S)
                    v.tensor_tensor(tmp[:], acc[:],
                                    bc(K.mod_rows[:, layer, bass.ds(b, 1), GB, :].rearrange("p a d -> p (a d)"), 1, TPB),
                                    ALU.mult).then_inc(xt, 1)
                    dve.wait_ge(xt, 1)
                    xs = K.x[:, bass.ds(b * TPB, TPB), :]
                    v.tensor_tensor(xs, xs, tmp[:], ALU.add)
            nc.all_engine_barrier(sems_to_clear=clear)


def split3(v, eng, done, count, f, parts, r):
    v.tensor_copy(parts[0], f).then_inc(done, 1)
    eng.wait_ge(done, count + 1)
    v.tensor_tensor(r, f, parts[0], ALU.subtract).then_inc(done, 1)
    eng.wait_ge(done, count + 2)
    v.tensor_copy(parts[1], r).then_inc(done, 1)
    eng.wait_ge(done, count + 3)
    v.tensor_tensor(parts[2], r, parts[1], ALU.subtract).then_inc(done, 1)
    return count + 4


def qkv1_stage(nc, K, A, v_nat, parts_dram):
    with ExitStack() as st:
        w = K.sb("w1_qkvT", [P, 3, D], ctx=st)
        bqk = K.sb("b1_qk", [P, 2], ctx=st)
        bqs = K.sb("b1_qk_scaled", [P, 2], ctx=st)
        bv = K.sb("b1_v", [P, D], ctx=st)
        f = K.sb("qk_f", [P, 3, CH], ctx=st)
        r = K.sb("qk_r", [P, 2, CH], ctx=st)
        pa = K.sb("qk_parts", [P, 2, 3, CH], BF16, ctx=st)
        qp = [K.ps(f"qk_ps{i}", [P, CH], st) for i in range(2)]
        vp = [K.ps(f"v1_ps{i}", [P, CPT, D], st) for i in range(2)]
        (w_in, b_s, q_mm, f_out, split, q_stored, k_stored, v_mm, v_out) = K.sems(st, 
            "qkv1", "w_in", "bias", "qk_mm", "qk_out", "split", "q_stored", "k_stored", "v_mm", "v_out")
        stored = (q_stored, k_stored)
        units = [(c, i) for c in range(NCH) for i in range(2)]
        with nc.Block() as block:
            @block.sync
            def _(sp):
                for i, n in enumerate(("L1_attn_WqT", "L1_attn_WkT", "L1_attn_WvT")):
                    sp.dma_start(w[:, i, :], A[n]).then_inc(w_in, 16)
                for i, n in enumerate(("L1_attn_bq", "L1_attn_bk")):
                    sp.dma_start(bqk[:, i:i + 1], A[n].rearrange("(p a) -> p a", a=1)).then_inc(w_in, 16)
                sp.dma_start(bv[:], A["L1_attn_bv"].partition_broadcast(P)).then_inc(w_in, 16)
                for n, (c, i) in enumerate(units):
                    sp.wait_ge(split, 4 * (n + 1))
                    sp.dma_start(parts_dram[i, :, :, c * CH:(c + 1) * CH].rearrange("a p t -> p a t"),
                                 pa[:, n % 2]).then_inc(stored[i], 16)
                    if c * CH >= (B - 1) * T:
                        sp.dma_start(parts_dram[i, :, :, c * CH + T:(c + 1) * CH + T].rearrange("a p t -> p a t"),
                                     pa[:, n % 2]).then_inc(stored[i], 16)
                for q in stored:
                    sp.wait_ge(q, 16 * (NCH + T // CH))

            @block.tensor
            def _(pe):
                pe.wait_ge(w_in, 16 * 6)
                for n, (c, i) in enumerate(units):
                    if n >= 2:
                        pe.wait_ge(f_out, n - 1)
                    nc.tensor.matmul(qp[n % 2][:], w[:, i, :], K.hT[:, c * CH:(c + 1) * CH],
                                     start=True, stop=True).then_inc(q_mm, 1)
                    if i == 1:
                        if c >= 2:
                            pe.wait_ge(v_out, c - 1)
                        for t in range(CPT):
                            m = nc.tensor.matmul(vp[c % 2][:, t, :], K.hT[:, c * CH + t * P:c * CH + (t + 1) * P],
                                                 w[:, 2, :], start=True, stop=True)
                        m.then_inc(v_mm, 1)

            @block.scalar
            def _(act):
                act.wait_ge(b_s, 1)
                for n, (c, i) in enumerate(units):
                    act.wait_ge(q_mm, n + 1)
                    if n >= 3:
                        act.wait_ge(split, 4 * (n - 2))
                    nc.scalar.activation(f[:, n % 3, :], qp[n % 2][:], ACT.Identity, bias=bqs[:, i:i + 1],
                                         scale=HD1 ** -0.5 if i == 0 else 1.0).then_inc(f_out, 1)

            @block.vector
            def _(dve):
                v = nc.vector
                dve.wait_ge(w_in, 16 * 6)
                v.tensor_copy(bqs[:, 1:2], bqk[:, 1:2])
                v.tensor_scalar(bqs[:, 0:1], bqk[:, 0:1], HD1 ** -0.5, None, ALU.mult).then_inc(b_s, 1)
                count = 0
                for n, (c, i) in enumerate(units):
                    dve.wait_ge(f_out, n + 1)
                    if n >= 2:
                        dve.wait_ge(stored[i], 16 * (c + max(0, c - (B - 1) * T // CH)))
                        dve.wait_ge(split, count)
                    count = split3(v, dve, split, count, f[:, n % 3, :], [pa[:, n % 2, j, :] for j in range(3)],
                                   r[:, n % 2, :])
                    if i == 1:
                        dve.wait_ge(v_mm, c + 1)
                        v.tensor_tensor(v_nat[:, c * CPT:(c + 1) * CPT, :], vp[c % 2][:], bc(bv[:], 1, CPT),
                                        ALU.add).then_inc(v_out, 1)


ATT_SEMS = ("loaded0", "loaded1", "loaded2", "loaded3", "m1_mm", "maxed", "m_turned", "m_split", "m_stored", "m_loaded",
            "s2_mm", "exp", "v_aug", "pv_mm", "o_out", "o_turned", "o_done", "o_rsum")


def full_attention_stage(nc, K, A):
    parts = nc.dram_tensor("qk_parts_dram", [2, 3, P, (B + 1) * T], BF16, kind="Internal").ap()
    mdram = nc.dram_tensor("neg_max_dram", [2, 3, 4 * TPB * P], BF16, kind="Internal").ap()
    with ExitStack() as st:
        v_nat = K.sb("v_nat", [P, NT, D], ctx=st)
        qkv1_stage(nc, K, A, v_nat, parts)
        qs = K.sb("q_stack", [P, 4, 4, T], BF16, ctx=st)
        ks = K.sb("k_stack", [P, 4, 4, T], BF16, ctx=st)
        va = K.sb("v_aug", [P, 2, TPB, 4, 32], ctx=st)
        pr = K.sb("probs1", [P, 2, 4, CH], ctx=st)
        osb = K.sb("o_sb", [P, 2, CH], ctx=st)
        mx = K.sb("q_max", [P, 2, 4 * TPB], ctx=st)
        nm = K.sb("neg_max", [4 * TPB, P], ctx=st)
        nr = K.sb("neg_max_rest", [4 * TPB, P], ctx=st)
        mp = K.sb("neg_max_parts", [4 * TPB, 2, 3, P], BF16, ctx=st)
        ro = K.sb("o_rsum", [P, 2, CPT, 4], ctx=st)
        s1 = [K.ps(f"s1_ps{i}", [P, T], st) for i in range(2)]
        s2 = [K.ps(f"s2_ps{i}", [P, CH], st) for i in range(2)]
        op = K.ps("o1_ps", [P, CH], st)
        mi = K.ps("misc_ps", [P, CPT, P], st)
        def load(sp, sem, ring, batch, quad):
            for i, (dst, order) in enumerate(((qs, Q_PART), (ks, K_PART))):
                for slot, part in enumerate(order):
                    src = parts[i, part, quad * 32:(quad + 1) * 32, bass.ds(batch * T, T)]
                    sp.dma_start(dst[slot * HD1:(slot + 1) * HD1, ring], src.rearrange("(h d) t -> d h t", d=HD1)
                                 ).then_inc(sem, 16)
            sp.dma_start(qs[MROW:MROW + 3, ring], ks[KROWS - 3:KROWS, ring]).then_inc(sem, 16)

        LOADS = 16 * (2 * len(Q_PART) + 1)

        def first_pass(pe, sm, n, ring, slot):
            h, qt = divmod(n, TPB)
            k = 4 * TPB * slot + n
            if k >= 2:
                pe.wait_ge(sm["maxed"], k - 1)
            for c in range(2):
                m = nc.tensor.matmul(s1[n % 2][:, c * CH:(c + 1) * CH], qs[0:KROWS, ring, h, qt * P:(qt + 1) * P],
                                     ks[0:KROWS, ring, h, c * CH:(c + 1) * CH], start=True, stop=True)
            m.then_inc(sm["m1_mm"], 1)

        def turn_max(pe, sm, ring, slot, misc_free):
            pe.wait_ge(sm["maxed"], 4 * TPB * (slot + 1))
            misc_free(pe)
            nc.tensor.transpose(mi[0:4 * TPB, 0, :], mx[:, ring % 2, :], K.ident[:]).then_inc(sm["m_turned"], 1)

        def reduce_max(dve, sm, n, ring, slot):
            dve.wait_ge(sm["m1_mm"], 4 * TPB * slot + n + 1)
            nc.vector.tensor_reduce(mx[:, ring % 2, n:n + 1], s1[n % 2][:], AX.X, ALU.max).then_inc(sm["maxed"], 1)

        def split_max(dve, sm, ring, slot):
            dve.wait_ge(sm["m_turned"], slot + 1)
            if slot >= 1:
                dve.wait_ge(sm["m_split"], 5 * slot)
            if slot >= 2:
                dve.wait_ge(sm["m_stored"], 16 * (slot - 1))
            nc.vector.tensor_scalar(nm[:], mi[0:4 * TPB, 0, :], -1.0, None, ALU.mult).then_inc(sm["m_split"], 1)
            dve.wait_ge(sm["m_split"], 5 * slot + 1)
            split3(nc.vector, dve, sm["m_split"], 5 * slot + 1, nm[:], [mp[:, ring % 2, j, :] for j in range(3)], nr[:])

        def move_max(sp, sm, ring, slot):
            sp.wait_ge(sm["m_split"], 5 * (slot + 1))
            if slot >= 1:
                sp.wait_ge(sm["m_loaded"], 16 * slot)
            sp.dma_start(mdram[ring % 2].rearrange("a (c q) -> c a q", q=P), mp[:, ring % 2]).then_inc(sm["m_stored"], 16)
            sp.wait_ge(sm["m_stored"], 16 * (slot + 1))
            sp.wait_ge(sm["maxed"], 4 * TPB * (slot + 1))
            sp.dma_start(qs[MROW:MROW + 3, ring], mdram[ring % 2].rearrange("a (h t) -> a h t", h=4)
                         ).then_inc(sm["m_loaded"], 16)

        (zeros, ones_set) = K.sems(st, "att1z", "zeros", "ones")
        flat = "p a h t -> p (a h t)"
        sm0 = dict(zip(ATT_SEMS, K.sems(st, "att1p", *ATT_SEMS)))
        with nc.Block() as block:
            @block.gpsimd
            def _(pool):
                g = nc.gpsimd
                g.memset(ks[32:64].rearrange(flat), 1.0).then_inc(ones_set, 1)
                pool.wait_ge(ones_set, 1)
                g.memset(va[:].rearrange("p a t h c -> p (a t h c)"), 0.0).then_inc(ones_set, 1)
                pool.wait_ge(ones_set, 2)
                g.memset(va[:, :, :, :, HD1:HD1 + 1].rearrange("p a t h c -> p (a t h) c"), 1.0).then_inc(ones_set, 1)

            @block.sync
            def _(sp):
                sp.wait_ge(zeros, 2)
                sp.wait_ge(ones_set, 1)
                for n in range(2):
                    load(sp, sm0[f"loaded{n}"], n, 0, n)
                for n in range(2):
                    sp.wait_ge(sm0[f"loaded{n}"], LOADS)
                move_max(sp, sm0, 0, 0)
                sp.wait_ge(sm0["m_loaded"], 16)

            @block.tensor
            def _(pe):
                pe.wait_ge(sm0["loaded0"], LOADS)
                for n in range(4 * TPB):
                    first_pass(pe, sm0, n, 0, 0)
                turn_max(pe, sm0, 0, 0, lambda e: None)

            @block.vector
            def _(dve):
                nc.vector.memset(qs[0:KROWS].rearrange(flat).bitcast(F32), 0.0).then_inc(zeros, 1)
                nc.vector.memset(ks[64:KROWS].rearrange(flat).bitcast(F32), 0.0).then_inc(zeros, 1)
                for n in range(4 * TPB):
                    reduce_max(dve, sm0, n, 0, 0)
                split_max(dve, sm0, 0, 0)

        sm_list, clear = K.att_sems
        sm = dict(zip(ATT_SEMS, sm_list))
        STEPS = 2 * TPB
        with nc.Fori(0, B) as b:
            with nc.Block() as block:
                @block.sync
                def _(sp):
                    for s in range(QUADS):
                        if s >= 2:
                            sp.wait_ge(sm["s2_mm"], 4 * STEPS * (s - 1))
                        nq = s + 2
                        load(sp, sm[f"loaded{nq % 4}"], nq % 4, b + nq // 4, nq % 4)
                        move_max(sp, sm, (s + 1) % 4, s)
                    for n in range(QUADS):
                        sp.wait_ge(sm[f"loaded{n}"], LOADS)
                    sp.wait_ge(sm["m_loaded"], 16 * QUADS)

                @block.gpsimd
                def _(pool):
                    for s in range(QUADS):
                        if s >= 2:
                            pool.wait_ge(sm["pv_mm"], STEPS * (s - 1))
                        nc.gpsimd.tensor_copy(
                            va[:, s % 2, :, :, 0:HD1],
                            v_nat[:, bass.ds(b * TPB, TPB), s * 32:(s + 1) * 32].rearrange("p t (h d) -> p t h d", d=HD1)
                        ).then_inc(sm["v_aug"], 1)

                @block.tensor
                def _(pe):
                    def product(s, i):
                        half, kt = divmod(i, TPB)
                        k = STEPS * s + i
                        pe.wait_ge(sm["exp"], 4 * (k + 1))
                        if kt == 0 and k >= TPB:
                            pe.wait_ge(sm["o_out"], k // TPB)
                        for h in range(4):
                            m = nc.tensor.matmul(op[32 * h:32 * h + 32, :], va[:, s % 2, kt, h, :], pr[:, k % 2, h, :],
                                                 start=(kt == 0), stop=(kt == TPB - 1))
                        m.then_inc(sm["pv_mm"], 1)

                    def turn_output(s, half):
                        k = 2 * s + half
                        pe.wait_ge(sm["o_out"], k + 1)
                        misc_free(k // 2, k)
                        for t in range(CPT):
                            m = nc.tensor.transpose(mi[:, t, :], osb[:, k % 2, t * P:(t + 1) * P], K.ident[:])
                        m.then_inc(sm["o_turned"], 1)

                    def misc_free(splits, outs):
                        if splits >= 1:
                            pe.wait_ge(sm["m_split"], 5 * splits)
                        if outs >= 1:
                            pe.wait_ge(sm["o_done"], outs)

                    for s in range(QUADS):
                        ring = (s + 1) % 4
                        if s >= 1:
                            pe.wait_ge(sm[f"loaded{ring}"], LOADS)
                        lead = 6
                        for n in range(lead):
                            first_pass(pe, sm, n, ring, s)
                        done = lead
                        pe.wait_ge(sm["v_aug"], s + 1)
                        for i in range(STEPS):
                            half, kt = divmod(i, TPB)
                            if s >= 1 and i == 0:
                                pe.wait_ge(sm["m_loaded"], 16 * s)
                            for h in range(4):
                                k = (STEPS * s + i) * 4 + h
                                if k >= 2:
                                    pe.wait_ge(sm["exp"], k - 1)
                                nc.tensor.matmul(s2[k % 2][:], ks[0:KROWS, s, h, kt * P:(kt + 1) * P],
                                                 qs[0:KROWS, s, h, half * CH:(half + 1) * CH],
                                                 start=True, stop=True).then_inc(sm["s2_mm"], 1)
                                if h % 2 == 1 and done < min(4 * TPB, lead + 2 * i + h // 2 + 1):
                                    first_pass(pe, sm, done, ring, s)
                                    done += 1
                            if i >= 1:
                                product(s, i - 1)
                            if i == TPB + 2:
                                turn_output(s, 0)
                        while done < 4 * TPB:
                            first_pass(pe, sm, done, ring, s)
                            done += 1
                        turn_max(pe, sm, ring, s, lambda e: misc_free(s, 2 * s + 1))
                        product(s, STEPS - 1)
                        pe.wait_ge(sm["m_split"], 5 * s + 1)
                        pe.wait_ge(sm["o_out"], 2 * s + 2)
                        for t in range(CPT):
                            m = nc.tensor.transpose(mi[:, t, :], osb[:, 1, t * P:(t + 1) * P], K.ident[:])
                        m.then_inc(sm["o_turned"], 1)

                @block.scalar
                def _(act):
                    def output(m):
                        act.wait_ge(sm["pv_mm"], TPB * (m + 1))
                        if m >= 2:
                            act.wait_ge(sm["o_turned"], m - 1)
                        nc.scalar.copy(osb[:, m % 2, :], op[:]).then_inc(sm["o_out"], 1)

                    for s in range(QUADS):
                        for i in range(STEPS):
                            k = STEPS * s + i
                            for h in range(4):
                                act.wait_ge(sm["s2_mm"], 4 * k + h + 1)
                                if h == 0 and k >= 2:
                                    act.wait_ge(sm["pv_mm"], k - 1)
                                nc.scalar.activation(pr[:, k % 2, h, :], s2[(4 * k + h) % 2][:], ACT.Exp
                                                     ).then_inc(sm["exp"], 1)
                            if i == TPB + 1:
                                output(2 * s)
                        output(2 * s + 1)

                @block.vector
                def _(dve):
                    v = nc.vector

                    def divide(m):
                        s, half = divmod(m, 2)
                        dve.wait_ge(sm["o_turned"], m + 1)
                        heads = mi[:].rearrange("p t (h c) -> p t h c", c=32)
                        v.reciprocal(ro[:, m % 2], heads[:, :, :, HD1]).then_inc(sm["o_rsum"], 1)
                        dve.wait_ge(sm["o_rsum"], m + 1)
                        v.tensor_tensor(
                            K.nat[:, bass.ds(b * TPB + half * CPT, CPT), s * 32:(s + 1) * 32]
                            .rearrange("p t (h d) -> p t h d", d=HD1),
                            heads[:, :, :, 0:HD1], bc(ro[:, m % 2], 3, HD1), ALU.mult).then_inc(sm["o_done"], 1)

                    for s in range(QUADS):
                        for n in range(4 * TPB):
                            reduce_max(dve, sm, n, (s + 1) % 4, s)
                            if n == 3 and s >= 1:
                                divide(2 * s - 1)
                            if n == 4 * TPB - 5:
                                divide(2 * s)
                        split_max(dve, sm, (s + 1) % 4, s)
                    divide(2 * QUADS - 1)
            nc.all_engine_barrier(sems_to_clear=clear)


def project_stage(nc, K, name, w_in_ap, bias, residual):
    with ExitStack() as st:
        w = K.sb(name + "_w", [P, D], ctx=st)
        br = K.sb(name + "_b", [P, D], ctx=st)
        aT = K.sb(name + "_aT", [P, NCH, CH], ctx=st)
        tmp = K.sb(name + "_tmp", [P, 2, CPT, D], ctx=st)
        tp = [K.ps(f"{name}_tps{i}", [P, CPT, P], st) for i in range(4)]
        yp = [K.ps(f"{name}_yps{i}", [P, CPT, D], st) for i in range(4)]
        (w_in, turned, t_out, y_mm, y_out, y_b) = K.sems(st, 
            name, "w_in", "turned", "turned_out", "y_mm", "y_out", "y_biased")
        n_in = 1 + (bias is not None)
        with nc.Block() as block:
            @block.sync
            def _(sp):
                sp.dma_start(w[:], w_in_ap).then_inc(w_in, 16)
                if bias is not None:
                    sp.dma_start(br[:], bias.partition_broadcast(P)).then_inc(w_in, 16)
                sp.wait_ge(w_in, 16 * n_in)

            @block.tensor
            def _(pe):
                pe.wait_ge(w_in, 16 * n_in)
                for c in range(NCH + 1):
                    if c < NCH:
                        if c >= 4:
                            pe.wait_ge(t_out, c - 3)
                        for t in range(CPT):
                            m = nc.tensor.transpose(tp[c % 4][:, t, :], K.nat[:, c * CPT + t, :], K.ident[:])
                        m.then_inc(turned, 1)
                    if c >= 1:
                        k = c - 1
                        pe.wait_ge(t_out, k + 1)
                        if k >= 4:
                            pe.wait_ge(y_b, k - 3)
                        for t in range(CPT):
                            m = nc.tensor.matmul(yp[k % 4][:, t, :], aT[:, k, t * P:(t + 1) * P], w[:],
                                                 start=True, stop=True)
                        m.then_inc(y_mm, 1)

            @block.scalar
            def _(act):
                for c in range(NCH):
                    act.wait_ge(turned, c + 1)
                    nc.scalar.copy(aT[:, c, :], tp[c % 4][:].rearrange("p t d -> p (t d)")).then_inc(t_out, 1)

            @block.vector
            def _(dve):
                v = nc.vector
                if bias is not None:
                    dve.wait_ge(w_in, 16 * n_in)
                for c in range(NCH):
                    tiles = slice(c * CPT, (c + 1) * CPT)
                    dve.wait_ge(y_mm, c + 1)
                    if residual is not None:
                        v.tensor_tensor(residual[:, tiles, :], residual[:, tiles, :], yp[c % 4][:], ALU.add
                                        ).then_inc(y_b, 1)
                        continue
                    if c >= 2:
                        dve.wait_ge(y_out, 2 * (c - 1))
                    v.tensor_tensor(tmp[:, c % 2], yp[c % 4][:], bc(br[:], 1, CPT), ALU.add).then_inc(y_b, 1)
                    dve.wait_ge(y_b, c + 1)
                    v.tensor_tensor(tmp[:, c % 2], tmp[:, c % 2], bc(K.mod_rows[:, 1, c * CPT // TPB, GA, :], 1, CPT),
                                    ALU.mult).then_inc(y_out, 1)
                    dve.wait_ge(y_out, 2 * c + 1)
                    v.tensor_tensor(K.x[:, tiles, :], K.x[:, tiles, :], tmp[:, c % 2], ALU.add).then_inc(y_out, 1)


def cross_attention_stage(nc, K, A, res):
    QW, KW = H1 * HD1, KV2 * HD1
    pairs = [(s, t) for s in range(B) for t in range(s + 1)]
    first = [sum(range(s + 1)) for s in range(B)]
    NP = len(pairs)
    M = TPB * KV2
    R = H1 // KV2
    with ExitStack() as st:
        w = K.sb("x_wT", [P, QKV2], ctx=st)
        q = K.sb("x_q", [P, NT, QW], ctx=st)
        k = K.sb("x_k", [P, NT, KW], ctx=st)
        vv = K.sb("x_v", [P, NT, KW], ctx=st)
        pd = K.sb("x_prod", [P, 2, TPB, QW], ctx=st)
        sc = K.sb("x_scores", [P, NP, TPB * H1], ctx=st)
        mx = K.sb("x_max", [P, B, TPB * H1], ctx=st)
        sm = K.sb("x_sum", [P, B, TPB * H1], ctx=st)
        yp = [K.ps(f"x_ps{i}", [P, CH], st) for i in range(4)]
        (w_in, mm, qkv_out, pdone, sdone, smx, exped, nrm, pv, pool_o) = K.sems(st, 
            "cross", "w_in", "qkv_mm", "qkv_out", "product", "score", "softmax", "exp", "norm", "pv", "out")
        with nc.Block() as block:
            @block.sync
            def _(sp):
                sp.dma_start(w[:], A["L1_ffn_qkvT"]).then_inc(w_in, 16)
                sp.wait_ge(w_in, 16)

            @block.tensor
            def _(pe):
                pe.wait_ge(w_in, 16)
                for n in range(NT // 2):
                    if n >= 4:
                        pe.wait_ge(qkv_out, n - 3)
                    for i in range(2):
                        t = 2 * n + i
                        m = nc.tensor.matmul(yp[n % 4][:, i * QKV2:(i + 1) * QKV2], K.hT[:, t * P:(t + 1) * P], w[:],
                                             start=True, stop=True)
                    m.then_inc(mm, 1)

            @block.scalar
            def _(act):
                for n in range(NT // 2):
                    act.wait_ge(mm, n + 1)
                    y = yp[n % 4][:, 0:2 * QKV2].rearrange("p (t c) -> p t c", t=2)
                    t2 = slice(2 * n, 2 * n + 2)
                    nc.scalar.copy(q[:, t2, :], y[:, :, 0:QW])
                    nc.scalar.copy(k[:, t2, :], y[:, :, QW:QW + KW])
                    nc.scalar.copy(vv[:, t2, :], y[:, :, QW + KW:QKV2]).then_inc(qkv_out, 1)
                act.wait_ge(smx, 2 * NP)
                nc.scalar.activation(sc[:], sc[:], ACT.Exp, scale=HD1 ** -0.5).then_inc(exped, 1)

            def grouped(ap):
                return ap.rearrange("p t (g r d) -> p (t g) r d", r=R, d=HD1)

            def shared(ap):
                return bc(ap.rearrange("p t (g d) -> p (t g) d", d=HD1), 2, R)

            def tiles(s):
                return slice(s * TPB, (s + 1) * TPB)

            @block.vector
            def _(dve):
                v = nc.vector
                for n, (s, t) in enumerate(pairs):
                    dve.wait_ge(qkv_out, (max(s, t) + 1) * TPB // 2)
                    if n >= 2:
                        dve.wait_ge(sdone, n - 1)
                    v.tensor_tensor(grouped(pd[:, n % 2]), grouped(q[:, tiles(s), :]), shared(k[:, tiles(t), :]),
                                    ALU.mult).then_inc(pdone, 1)
                    dve.wait_ge(pdone, n + 1)
                    v.tensor_reduce(sc[:, n, :], pd[:, n % 2].rearrange("p t (h d) -> p (t h) d", d=HD1), AX.X,
                                    ALU.add).then_inc(sdone, 1)
                dve.wait_ge(sdone, NP)
                count = 0
                for s in range(B):
                    f = first[s]
                    v.tensor_copy(mx[:, s, :], sc[:, f, :]).then_inc(smx, 1)
                    count += 1
                    for t in range(1, s + 1):
                        dve.wait_ge(smx, count)
                        v.tensor_tensor(mx[:, s, :], mx[:, s, :], sc[:, f + t, :], ALU.max).then_inc(smx, 1)
                        count += 1
                    dve.wait_ge(smx, count)
                    if s == 0:
                        base = count
                for n, (s, t) in enumerate(pairs):
                    v.tensor_tensor(sc[:, n, :], sc[:, n, :], mx[:, s, :], ALU.subtract).then_inc(smx, 1)
                    count += 1
                assert count == 2 * NP
                dve.wait_ge(exped, 1)
                count = 0
                for s in range(B):
                    f = first[s]
                    v.tensor_copy(sm[:, s, :], sc[:, f, :]).then_inc(nrm, 1)
                    count += 1
                    for t in range(1, s + 1):
                        dve.wait_ge(nrm, count)
                        v.tensor_tensor(sm[:, s, :], sm[:, s, :], sc[:, f + t, :], ALU.add).then_inc(nrm, 1)
                        count += 1
                dve.wait_ge(nrm, count)
                v.reciprocal(mx[:], sm[:]).then_inc(nrm, 1)
                count += 1
                dve.wait_ge(nrm, count)
                for n, (s, t) in enumerate(pairs):
                    v.tensor_tensor(sc[:, n, :], sc[:, n, :], mx[:, s, :], ALU.mult).then_inc(nrm, 1)
                    count += 1
                dve.wait_ge(nrm, count)
                done = 0
                for n, (s, t) in enumerate(pairs):
                    weight = bc(sc[:, n, :].rearrange("p (m r) -> p m r", r=R), 3, HD1)
                    dst = K.nat[:, tiles(s), :] if t == 0 else pd[:, n % 2]
                    if t:
                        dve.wait_ge(pv, done)
                    v.tensor_tensor(grouped(dst), shared(vv[:, tiles(t), :]), weight, ALU.mult).then_inc(pv, 1)
                    done += 1
                    if t:
                        dve.wait_ge(pv, done)
                        o = K.nat[:, tiles(s), :]
                        v.tensor_tensor(o, o, pd[:, n % 2], ALU.add).then_inc(pv, 1)
                        done += 1


def output_stage(nc, K, out):
    with ExitStack() as st:
        (stored,) = K.sems(st, "out", "stored")
        with nc.Block() as block:
            @block.sync
            def _(sp):
                sp.dma_start(out.rearrange("b (t p) d -> p (b t) d", p=P), K.x[:]).then_inc(stored, 16)
                sp.wait_ge(stored, 16)


def build(nc, A, out, stages=99):
    with ExitStack() as ctx:
        K = Core(nc, ctx)
        K.win_sems = K.loop_sems(
            "win", "h_in", "proj_mm", "act_out", "q_out", "v_shift_even", "v_shift_odd", "score_mm", "biased", "exp",
            "rsum", "normed", "turned", "probsT_out", "pv_mm", "o_out", "wo_mm", "x_tmp")
        K.moe_sems = K.loop_sems("moe", "copied", "hidden_mm", "gelu", "y_mm", "y_added", "x_tmp")
        K.att_sems = K.loop_sems("att1", *ATT_SEMS)
        K.x = K.sb("x", [P, NT, D])
        K.nat = K.sb("nat", [P, NT, D])
        K.hT = K.sb("hT", [P, B * T])
        K.w = K.sb("expert_w", [P, NT, E])
        K.mod_cols = K.sb("mod_cols", [P, 2, 6, B])
        K.mod_rows = K.sb("mod_rows", [P, 2, B, 6, D])
        K.ident = K.sb("ident", [P, P])
        K.ones = K.sb("ones", [P, P])
        K.neghalf = K.sb("neghalf", [P, NT])

        def cols(layer, scale, shift):
            return (lambda b: K.mod_cols[:, layer, scale, b:b + 1], lambda b: K.mod_cols[:, layer, shift, b:b + 1])

        def rows(layer, scale, shift):
            return (lambda b: K.mod_rows[:, layer, b, scale, :], lambda b: K.mod_rows[:, layer, b, shift, :])

        modulation_stage(nc, K, A)
        if stages >= 1:
            norm_stage(nc, K, "n0a", K.x, to_T=cols(0, CA, SA))
            window_attention_stage(nc, K, A)
        if stages >= 2:
            norm_stage(nc, K, "n0b", K.x, rows=rows(0, CB, SB))
            with ExitStack() as st:
                aff = affine_columns(nc, K, A, "aff0", ("L0_ffn_gamma", "L0_ffn_beta"), st)
                norm_stage(nc, K, "n0c", K.nat, to_T=aff)
            routing_stage(nc, K, A, "rt0", A["L0_ffn_WgT"], A["L0_ffn_bg"], A["L0_ffn_b2"], True)
            expert_stage(nc, K, A, "moe0", F0, A["L0_ffn_W1T"], A["L0_ffn_W2T"], A["L0_ffn_b1c"], ACT.Gelu, 0)
        if stages >= 3:
            norm_stage(nc, K, "n1a", K.x, to_T=cols(1, CA, SA))
            full_attention_stage(nc, K, A)
            project_stage(nc, K, "wo1", A["L1_attn_WoT"], A["L1_attn_bo"], None)
        if stages >= 4:
            with ExitStack() as st:
                res = K.sb("res", [P, NT, D], ctx=st)
                norm_stage(nc, K, "n1b", K.x, rows=rows(1, CB, SB))
                aff1 = affine_columns(nc, K, A, "aff1", ("L1_ffn_ln1_weight", "L1_ffn_ln1_bias"), st)
                aff2 = affine_columns(nc, K, A, "aff2", ("L1_ffn_ln2_weight", "L1_ffn_ln2_bias"), st)
                norm_stage(nc, K, "n1c", K.nat, to_T=aff1)
                copy_stage(nc, K, res, K.nat)
                cross_attention_stage(nc, K, A, res)
                project_stage(nc, K, "pj1", A["L1_ffn_projT"], None, res)
                copy_stage(nc, K, K.nat, res)
                norm_stage(nc, K, "n1d", K.nat, to_T=aff2)
            routing_stage(nc, K, A, "rt1", A["L1_ffn_routerT"], None, None, False)
            expert_stage(nc, K, A, "moe1", F1, A["L1_ffn_moe_w1"], A["L1_ffn_moe_w2"], None, ACT.Gelu_apprx_tanh, 1)
        output_stage(nc, K, out)


def affine_columns(nc, K, A, name, arrays, st):
    c = K.sb(name, [P, 2], ctx=st)
    (c_in,) = K.sems(st, name, "c_in")
    with nc.Block() as block:
        @block.sync
        def _(sp):
            for i, a in enumerate(arrays):
                sp.dma_start(c[:, i:i + 1], A[a].rearrange("(p a) -> p a", a=1)).then_inc(c_in, 16)
            sp.wait_ge(c_in, 32)
    return (lambda b: c[:, 0:1], lambda b: c[:, 1:2])


def copy_stage(nc, K, dst, src):
    with nc.Block() as block:
        @block.vector
        def _(dve):
            nc.vector.tensor_copy(dst[:, 0:NT // 2, :], src[:, 0:NT // 2, :])

        @block.scalar
        def _(act):
            nc.scalar.copy(dst[:, NT // 2:NT, :], src[:, NT // 2:NT, :])


def constants():
    slopes = np.array([2.0 ** (-0.5 * (i + 1)) for i in range(H0)])
    r = np.arange(BLK)[:, None]
    c = np.arange(P)[None, :]
    dist = c - BLK - r
    neg = np.empty((2, BLK, PAIRS, 2, P), np.float32)
    for h in range(H0):
        for v in range(2):
            ok = (dist <= 0) & (dist >= -WIN) & ((c >= BLK) | (v == 0))
            neg[h % 2, :, h // 2, v, :] = np.where(ok, -slopes[h] * dist, 1e30)
    lower = np.broadcast_to((np.arange(E)[None, :] < np.arange(E)[:, None]).astype(np.float32).reshape(1, -1), (P, E * E))
    return {"identity": np.eye(P, dtype=np.float32), "neg_bias": neg.reshape(P, PAIRS, 2, P),
            "lower": np.ascontiguousarray(lower)}


AS_IS = ("L0_attn_x", "L0_attn_wq", "L0_attn_wk", "L0_ffn_gamma", "L0_ffn_beta",
         "L0_ffn_bg", "L0_ffn_b2", "L0_wmod", "L1_attn_bq", "L1_attn_bk", "L1_attn_bv", "L1_attn_bo",
         "L1_ffn_ln1_weight", "L1_ffn_ln1_bias", "L1_ffn_ln2_weight", "L1_ffn_ln2_bias", "L1_ffn_moe_w1",
         "L1_ffn_moe_w2", "L1_wmod")
TURNED = {"L0_attn_wqT": "L0_attn_wq", "L0_attn_wkT": "L0_attn_wk", "L0_attn_wvT": "L0_attn_wv",
          "L0_attn_woT": "L0_attn_wo", "L0_ffn_WgT": "L0_ffn_Wg", "L0_ffn_W1T": "L0_ffn_W1", "L0_ffn_W2T": "L0_ffn_W2",
          "L0_c": "L0_c", "L1_c": "L1_c", "L1_attn_WqT": "L1_attn_Wq", "L1_attn_WkT": "L1_attn_Wk",
          "L1_attn_WvT": "L1_attn_Wv", "L1_attn_WoT": "L1_attn_Wo", "L1_ffn_qkvT": "L1_ffn_qkv_weight",
          "L1_ffn_projT": "L1_ffn_proj_weight", "L1_ffn_routerT": "L1_ffn_router_weight"}


def kernel(**inputs):
    import numpy as _np
    import concourse.bacc as _bacc
    from concourse import mybir as _mybir
    from concourse.bass_utils import run_bass_kernel_spmd as _run

    data = {n: _np.asarray(inputs[n]) for n in AS_IS}
    for n, of in TURNED.items():
        data[n] = _np.swapaxes(_np.asarray(inputs[of]), -1, -2)
    data["L0_ffn_b1c"] = _np.asarray(inputs["L0_ffn_b1"]).reshape(E * F0 // P, P).T
    for n in "qk":
        data[f"L0_attn_{n}_norm_c"] = _np.asarray(inputs[f"L0_attn_{n}_norm_w"]).reshape(PAIRS, P).T
    data.update(constants())
    nc = _bacc.Bacc("TRN2", target_bir_lowering=False, num_devices=1)
    arrays, A = {}, {}
    for n, a in data.items():
        a = _np.ascontiguousarray(a)
        arrays[f"in_{n}"] = a
        A[n] = nc.dram_tensor(f"in_{n}", a.shape, _mybir.dt.from_np(a.dtype), kind="ExternalInput").ap()
    out = nc.dram_tensor("out_x", (B, T, D), F32, kind="ExternalOutput").ap()
    build(nc, A, out)
    r = _run(nc, [arrays], core_ids=[0])
    return r.results[0]["out_x"]
```

```python
from contextlib import ExitStack

import numpy as np

import concourse.bass as bass
from concourse import mybir

F32 = mybir.dt.float32
BF16 = mybir.dt.bfloat16
F32R = mybir.dt.float32r
ALU = mybir.AluOpType
ACT = mybir.ActivationFunctionType
AX = mybir.AxisListType

P = 128
B, T, D = 4, 1024, 128
TPB = T // P
NT = B * TPB
CH = 512
NCH = B * T // CH
CPT = CH // P
LN_EPS = 1e-5
GATE_MIN = 0.25

H0, HD0, WIN = 16, 64, 64
PAIRS = H0 // 2
BLK = 64
NBLK = T // BLK
RMS_EPS = 1e-6
E = 8
F0, F1 = 512, 256
TOPK_EPS = 1e-8
H1, HD1 = 16, 8
QUADS = H1 // 4
KV2 = 4
QKV2 = H1 * HD1 + 2 * KV2 * HD1
Q_PART = (0, 0, 1, 1, 0, 2)
K_PART = (0, 1, 0, 1, 2, 0)
MROW = len(Q_PART) * HD1
KROWS = 96

SA, CA, GA, SB, CB, GB = range(6)


def bc(ap, axis, n):
    a = ap.unsqueeze(axis)
    shape = list(a.shape)
    shape[axis] = n
    return a.broadcast_to(shape)


class Core:

    def __init__(self, nc, ctx):
        self.nc, self.ctx = nc, ctx

    def sb(self, name, shape, dt=F32, ctx=None):
        return (ctx or self.ctx).enter_context(self.nc.sbuf_tensor(name, shape, dt))

    def ps(self, name, shape, ctx):
        return ctx.enter_context(self.nc.psum_tensor(name, shape, F32))

    def sems(self, ctx, prefix, *names):
        s = [self.nc.alloc_semaphore(f"{prefix}_{n}") for n in names]
        ctx.callback(self.clear, s)
        return s

    def clear(self, sems):
        self.nc.clear_and_free_semaphores(sems)
        self.nc.all_engine_barrier()

    def loop_sems(self, prefix, *names):
        s = [self.nc.alloc_semaphore(f"{prefix}_{n}") for n in names]
        numbers = [x.num for x in s]
        assert numbers == list(range(numbers[0], numbers[0] + len(s)))
        return s, range(numbers[0], numbers[0] + len(s))


def modulation_stage(nc, K, A):
    with ExitStack() as st:
        cT = K.sb("cT", [P, 2, B], ctx=st)
        wmod = K.sb("wmod", [P, 2, 6 * D], ctx=st)
        ex = K.sb("silu_exp", [P, 2, B], ctx=st)
        den = K.sb("silu_den", [P, 2, B], ctx=st)
        rec = K.sb("silu_rec", [P, 2, B], ctx=st)
        sil = K.sb("silu", [P, 2, B], ctx=st)
        silb = K.sb("silu_rows", [P, 2, B, P], ctx=st)
        sgn = K.sb("gate_sign", [P, 2, B, 2, D], ctx=st)
        mag = K.sb("gate_size", [P, 2, B, 2, D], ctx=st)
        csgn = K.sb("gate_sign_cols", [P, 2, B], ctx=st)
        cmag = K.sb("gate_size_cols", [P, 2, B], ctx=st)
        colp = K.ps("mod_cols_ps", [P, 2, 6, B], st)
        rowp = [K.ps(f"mod_rows_ps{i}", [P, CH], st) for i in range(4)]
        (x_in, c_in, e_done, dve, cols_mm, rows_mm, rows_out) = K.sems(st, 
            "mod", "x_in", "c_in", "exp", "dve", "cols_mm", "rows_mm", "rows_out")
        half = 3 * D
        with nc.Block() as block:
            @block.sync
            def _(sp):
                for i, (c, w) in enumerate((("L0_c", "L0_wmod"), ("L1_c", "L1_wmod"))):
                    sp.dma_start(cT[:, i, :], A[c]).then_inc(c_in, 16)
                    sp.dma_start(wmod[:, i, :], A[w]).then_inc(c_in, 16)
                sp.dma_start(K.x[:], A["L0_attn_x"].rearrange("b (t p) d -> p (b t) d", p=P)).then_inc(x_in, 16)
                sp.dma_start(K.ident[:], A["identity"]).then_inc(x_in, 16)
                sp.wait_ge(x_in, 32)

            @block.scalar
            def _(act):
                act.wait_ge(c_in, 64)
                nc.scalar.activation(ex[:], cT[:], ACT.Exp, scale=-1.0).then_inc(e_done, 1)
                act.wait_ge(cols_mm, 1)
                nc.scalar.copy(K.mod_cols[:], colp[:]).then_inc(e_done, 1)

            @block.vector
            def _(dve_):
                v = nc.vector
                v.memset(K.neghalf[:], -0.5).then_inc(dve, 1)
                dve_.wait_ge(e_done, 1)
                v.tensor_scalar(den[:], ex[:], 1.0, None, ALU.add).then_inc(dve, 1)
                dve_.wait_ge(dve, 2)
                v.reciprocal(rec[:], den[:]).then_inc(dve, 1)
                dve_.wait_ge(dve, 3)
                v.tensor_tensor(sil[:], cT[:], rec[:], ALU.mult).then_inc(dve, 1)
                dve_.wait_ge(dve, 4)
                v.tensor_copy(silb[:], bc(sil[:], 3, P)).then_inc(dve, 1)
                for n in range(2 * B):
                    dve_.wait_ge(rows_mm, n + 1)
                    for j in range(2):
                        r = v.tensor_copy(K.mod_rows[:, n // B, n % B, 3 * j:3 * j + 3, :],
                                          rowp[2 * (n % 2) + j][:, 0:half].rearrange("p (c d) -> p c d", c=3))
                    r.then_inc(rows_out, 1)
                dve_.wait_ge(rows_out, 2 * B)
                dve_.wait_ge(e_done, 2)
                for c in (CA, CB):
                    v.tensor_scalar(K.mod_cols[:, :, c, :], K.mod_cols[:, :, c, :], 1.0, None, ALU.add)
                    for l in range(2):
                        v.tensor_scalar(K.mod_rows[:, l, :, c, :], K.mod_rows[:, l, :, c, :], 1.0, None, ALU.add)
                g = K.mod_cols[:, :, GB, :]
                v.tensor_scalar(csgn[:], g, 0.0, 2.0, ALU.is_ge, ALU.mult).then_inc(dve, 1)
                v.scalar_tensor_tensor(out=cmag[:], in0=g, scalar=-1.0, in1=g, op0=ALU.mult, op1=ALU.max).then_inc(dve, 1)
                for l in range(2):
                    for i, c in enumerate((GA, GB)):
                        g = K.mod_rows[:, l, :, c, :]
                        v.tensor_scalar(sgn[:, l, :, i, :], g, 0.0, 2.0, ALU.is_ge, ALU.mult).then_inc(dve, 1)
                        v.scalar_tensor_tensor(out=mag[:, l, :, i, :], in0=g, scalar=-1.0, in1=g, op0=ALU.mult,
                                               op1=ALU.max).then_inc(dve, 1)
                dve_.wait_ge(dve, 15)
                v.tensor_scalar(csgn[:], csgn[:], 1.0, None, ALU.subtract).then_inc(dve, 1)
                v.tensor_scalar(sgn[:], sgn[:], 1.0, None, ALU.subtract).then_inc(dve, 1)
                dve_.wait_ge(dve, 17)
                v.scalar_tensor_tensor(out=K.mod_cols[:, :, GB, :], in0=cmag[:], scalar=GATE_MIN, in1=csgn[:],
                                       op0=ALU.max, op1=ALU.mult)
                for l in range(2):
                    for i, c in enumerate((GA, GB)):
                        v.scalar_tensor_tensor(out=K.mod_rows[:, l, :, c, :], in0=mag[:, l, :, i, :],
                                               scalar=GATE_MIN, in1=sgn[:, l, :, i, :], op0=ALU.max, op1=ALU.mult)

            @block.tensor
            def _(pe):
                pe.wait_ge(dve, 5)
                pe.wait_ge(c_in, 64)
                for l in range(2):
                    for c in range(6):
                        m = nc.tensor.matmul(colp[:, l, c, :], wmod[:, l, c * D:(c + 1) * D], sil[:, l, :],
                                             start=True, stop=True)
                m.then_inc(cols_mm, 1)
                for n in range(2 * B):
                    if n >= 2:
                        pe.wait_ge(rows_out, n - 1)
                    for j in range(2):
                        m = nc.tensor.matmul(rowp[2 * (n % 2) + j][:, 0:half], silb[:, n // B, n % B, :],
                                             wmod[:, n // B, j * half:(j + 1) * half], start=True, stop=True)
                    m.then_inc(rows_mm, 1)


def norm_stage(nc, K, name, src, to_T=None, rows=None):
    with ExitStack() as st:
        stats = K.sb(name + "_stats", [P, NT, 6], ctx=st)
        mv = K.sb(name + "_mv", [P, NT, 2], ctx=st)
        ve = K.sb(name + "_ve", [P, NT], ctx=st)
        rstd = K.sb(name + "_rstd", [P, NT], ctx=st)
        hat = K.sb(name + "_hat", [P, NT, D], ctx=st)
        hp = [K.ps(f"{name}_ps{i}", [P, CPT, P], st) for i in range(NCH)] if to_T else None
        (st_done, mv_done, rs_done, hat_done, row_done, turned) = K.sems(st, 
            name, "stats", "meanvar", "rstd", "hat", "rows", "turned")
        with nc.Block() as block:
            @block.vector
            def _(dve):
                v = nc.vector
                for b in range(B):
                    for t in range(b * TPB, (b + 1) * TPB):
                        v.bn_stats(stats[:, t, :], src[:, t, :]).then_inc(st_done, 1)
                    for t in range(b * TPB, (b + 1) * TPB):
                        dve.wait_ge(st_done, t + 1)
                        v.bn_aggr(mv[:, t, :], stats[:, t, :]).then_inc(mv_done, 1)
                for b in range(B):
                    dve.wait_ge(rs_done, 2 * (b + 1))
                    for t in range(b * TPB, (b + 1) * TPB):
                        v.tensor_scalar(hat[:, t, :], src[:, t, :], mv[:, t, 0:1], rstd[:, t:t + 1],
                                        ALU.subtract, ALU.mult).then_inc(hat_done, 1)
                    if rows:
                        scale, bias = rows
                        h, o = hat[:, b * TPB:(b + 1) * TPB, :], K.nat[:, b * TPB:(b + 1) * TPB, :]
                        dve.wait_ge(hat_done, (b + 1) * TPB)
                        v.tensor_tensor(h, h, bc(scale(b), 1, TPB), ALU.mult).then_inc(row_done, 1)
                        dve.wait_ge(row_done, b + 1)
                        v.tensor_tensor(o, h, bc(bias(b), 1, TPB), ALU.add)

            @block.gpsimd
            def _(pool):
                g = nc.gpsimd
                for b in range(B):
                    s = slice(b * TPB, (b + 1) * TPB)
                    pool.wait_ge(mv_done, (b + 1) * TPB)
                    g.tensor_scalar(ve[:, s], mv[:, s, 1], LN_EPS, None, ALU.add).then_inc(rs_done, 1)
                    pool.wait_ge(rs_done, 2 * b + 1)
                    g.tensor_tensor(rstd[:, s], ve[:, s], K.neghalf[:, s], ALU.pow).then_inc(rs_done, 1)

            if to_T:
                @block.tensor
                def _(pe):
                    for c in range(NCH):
                        pe.wait_ge(hat_done, (c + 1) * CPT)
                        for t in range(CPT):
                            m = nc.tensor.transpose(hp[c][:, t, :], hat[:, c * CPT + t, :], K.ident[:])
                        m.then_inc(turned, 1)

                @block.scalar
                def _(act):
                    scale, bias = to_T
                    for c in range(NCH):
                        act.wait_ge(turned, c + 1)
                        b = c * CPT // TPB
                        nc.scalar.activation(K.hT[:, c * CH:(c + 1) * CH], hp[c][:].rearrange("p t d -> p (t d)"),
                                             ACT.Identity, bias=bias(b), scale=scale(b))


def rms_stage(nc, K, A, st, hq, hk):
    with ExitStack() as s2:
        wn = K.sb("w_nat", [P, 2, PAIRS, D], ctx=s2)
        gram = K.sb("gram", [P, 2, D], ctx=s2)
        z = K.sb("z", [P, 2, CH], ctx=s2)
        inv_d = K.sb("inv_d", [P, P], ctx=s2)
        ms = K.sb("mean_square", [P, 2, CH], ctx=s2)
        rr = K.sb("rrms", [P, 2, CH], ctx=s2)
        root = K.sb("root", [P, 2, CH], ctx=s2)
        gp = K.ps("gram_ps", [P, 2, D], s2)
        up = [K.ps(f"u_ps{i}", [P, CH], s2) for i in range(2)]
        sp_ = [K.ps(f"ssum_ps{i}", [P, CH], s2) for i in range(2)]
        (w_in, cst, g_mm, g_out, u_mm, z_done, s_mm, ms_done, root_done, r_done, scaled) = K.sems(s2, 
            "rms", "w_in", "const", "gram_mm", "gram_out", "u_mm", "z", "sum_mm", "ms", "root", "r", "scaled")
        units = [(c, i) for c in range(NCH) for i in range(2)]
        with nc.Block() as block:
            @block.sync
            def _(sp):
                for i, w in enumerate(("L0_attn_wq", "L0_attn_wk")):
                    sp.dma_start(wn[:, i], A[w].rearrange("(c p) d -> p c d", p=P)).then_inc(w_in, 16)

            @block.tensor
            def _(pe):
                pe.wait_ge(w_in, 32)
                for i in range(2):
                    for c in range(PAIRS):
                        m = nc.tensor.matmul(gp[:, i, :], wn[:, i, c, :], wn[:, i, c, :],
                                             start=(c == 0), stop=(c == PAIRS - 1))
                m.then_inc(g_mm, 1)
                pe.wait_ge(g_out, 1)
                pe.wait_ge(cst, 1)
                for n in range(len(units) + 1):
                    if n < len(units):
                        c, i = units[n]
                        if n >= 2:
                            pe.wait_ge(z_done, n - 1)
                        nc.tensor.matmul(up[n % 2][:], gram[:, i, :], K.hT[:, c * CH:(c + 1) * CH],
                                         start=True, stop=True).then_inc(u_mm, 1)
                    if n >= 1:
                        pe.wait_ge(z_done, n)
                        if n >= 3:
                            pe.wait_ge(ms_done, n - 2)
                        nc.tensor.matmul(sp_[(n - 1) % 2][:], inv_d[:], z[:, (n - 1) % 2, :],
                                         start=True, stop=True).then_inc(s_mm, 1)

            @block.scalar
            def _(act):
                act.wait_ge(g_mm, 1)
                nc.scalar.copy(gram[:], gp[:]).then_inc(g_out, 1)
                for n in range(len(units)):
                    act.wait_ge(ms_done, n + 1)
                    if n >= 2:
                        act.wait_ge(r_done, n - 1)
                    nc.scalar.activation(root[:, n % 2, :], ms[:, n % 2, :], ACT.Sqrt).then_inc(root_done, 1)

            @block.vector
            def _(dve):
                v = nc.vector
                v.memset(inv_d[:], 1.0 / (H0 * HD0)).then_inc(cst, 1)
                for n in range(len(units) + 2):
                    if n < len(units):
                        c, i = units[n]
                        dve.wait_ge(u_mm, n + 1)
                        if n >= 2:
                            dve.wait_ge(s_mm, n - 1)
                        v.tensor_tensor(z[:, n % 2, :], up[n % 2][:], K.hT[:, c * CH:(c + 1) * CH],
                                        ALU.mult).then_inc(z_done, 1)
                    if 1 <= n <= len(units):
                        dve.wait_ge(s_mm, n)
                        if n >= 3:
                            dve.wait_ge(root_done, n - 2)
                        v.tensor_scalar(ms[:, (n - 1) % 2, :], sp_[(n - 1) % 2][:], 0.0, RMS_EPS,
                                        ALU.max, ALU.add).then_inc(ms_done, 1)
                    if n >= 2:
                        k = n - 2
                        dve.wait_ge(root_done, k + 1)
                        if k >= 2:
                            dve.wait_ge(scaled, k - 1)
                        v.reciprocal(rr[:, k % 2, :], root[:, k % 2, :]).then_inc(r_done, 1)

            @block.gpsimd
            def _(pool):
                g = nc.gpsimd
                for n, (c, i) in enumerate(units):
                    pool.wait_ge(r_done, n + 1)
                    g.tensor_tensor((hq, hk)[i][:, c * CH:(c + 1) * CH], K.hT[:, c * CH:(c + 1) * CH],
                                    rr[:, n % 2, :], ALU.mult).then_inc(scaled, 1)


def window_attention_stage(nc, K, A):
    with ExitStack() as st:
        hq = K.sb("hq", [P, B * T], ctx=st)
        hk = K.sb("hk", [P, B * T], ctx=st)
        rms_stage(nc, K, A, st, hq, hk)
        wq = K.sb("wqT", [P, PAIRS, P], ctx=st)
        wk = K.sb("wkT", [P, PAIRS, P], ctx=st)
        wv = K.sb("wvT", [P, PAIRS, P], ctx=st)
        wo = K.sb("woT", [P, PAIRS, D], ctx=st)
        nbias = K.sb("nbias", [P, PAIRS, 2, P], ctx=st)
        qn = K.sb("qn", [P, 2, PAIRS], ctx=st)
        qs = K.sb("qscale", [P, PAIRS], ctx=st)
        hb = K.nat[:, 0:TPB, :].rearrange("p t d -> p (t d)")
        qbd = K.sb("q_bd", [P, 2, NBLK, P], ctx=st)
        kk = K.sb("k_pad", [P, 2, BLK + T], ctx=st)
        vv = K.sb("v_tiles", [P, 2, TPB, P], ctx=st)
        vs = K.sb("v_shift", [P, 2, TPB, P], ctx=st)
        sb_ = K.sb("s_biased", [P, 4, 4, P], ctx=st)
        mn = K.sb("s_min", [P, 4, 4], ctx=st)
        pr = K.sb("probs", [P, 4, 4, P], ctx=st)
        sm = K.sb("p_sum", [P, 4, 4], ctx=st)
        ri = K.sb("p_rsum", [P, 4, 4], ctx=st)
        pt = K.sb("probsT", [P, 2, 4, P], ctx=st)
        oT = K.sb("oT", [P, 2, T], ctx=st)
        tmp = K.nat[:, TPB:2 * TPB, :]
        pj = [K.ps(f"proj_ps{i}", [P, CH], st) for i in range(2)]
        sp_ = [K.ps(f"score_ps{i}", [P, 4, P], st) for i in range(2)]
        tp = K.ps("probsT_ps", [P, 4, P], st)
        op = K.ps("o_ps", [P, 4, BLK], st)
        wp = [K.ps(f"wo_ps{i}", [P, CPT, D], st) for i in range(2)]
        (w_in, qs_d, z_d) = K.sems(st, "win0", "w_in", "qscale", "zeros")
        with nc.Block() as block:
            @block.sync
            def _(sp):
                for dst, w in ((wq, "L0_attn_wqT"), (wk, "L0_attn_wkT"), (wv, "L0_attn_wvT")):
                    sp.dma_start(dst[:].rearrange("p c o -> p (c o)"), A[w]).then_inc(w_in, 16)
                sp.dma_start(wo[:], A["L0_attn_woT"].rearrange("(c p) d -> p c d", p=P)).then_inc(w_in, 16)
                sp.dma_start(nbias[:], A["neg_bias"]).then_inc(w_in, 16)
                sp.dma_start(qn[:, 0, :], A["L0_attn_q_norm_c"]).then_inc(w_in, 16)
                sp.dma_start(qn[:, 1, :], A["L0_attn_k_norm_c"]).then_inc(w_in, 16)
                sp.wait_ge(w_in, 7 * 16)

            @block.vector
            def _(dve):
                dve.wait_ge(w_in, 7 * 16)
                nc.vector.scalar_tensor_tensor(out=qs[:], in0=qn[:, 0, :], scalar=-HD0 ** -0.5, in1=qn[:, 1, :],
                                               op0=ALU.mult, op1=ALU.mult)

            @block.gpsimd
            def _(pool):
                nc.gpsimd.memset(qbd[:].rearrange("p a b c -> p (a b c)"), 0.0)
                nc.gpsimd.memset(kk[:, :, 0:BLK], 0.0)
                nc.gpsimd.memset(vs[0:BLK, :, 0, :], 0.0)

        ((h_in, p_mm, a_out, q_out, v_sh0, v_sh1, s_mm, biased, exped, rsum, normed, turned, pt_out, pv_mm, o_out,
          wo_mm, xt), clear) = K.win_sems
        v_sh = (v_sh0, v_sh1)
        GRP = NBLK // 4
        G = PAIRS * GRP
        units = [(h, u) for h in range(PAIRS) for u in range(6)]

        def unit_steps(g):
            h = g // GRP + 1
            if h >= PAIRS or g >= G:
                return []
            return [6 * h + u for u in ((0, 1), (2, 3), (4,), (5,))[g % GRP]]

        with nc.Fori(0, B) as b:
            with nc.Block() as block:
                @block.tensor
                def _(pe):
                    def project(n):
                        h, u = units[n]
                        if n >= 2:
                            hh, uu = units[n - 2]
                            pe.wait_ge(a_out, n - 1)
                            if uu < 2:
                                pe.wait_ge(q_out, 2 * hh + uu + 1)
                        half = u % 2
                        tok = bass.ds(b * T + half * CH, CH)
                        if u < 4:
                            w, src = ((wq, hq), (wk, hk))[u // 2]
                            m = nc.tensor.matmul(pj[n % 2][:], w[:, h, :], src[:, tok], start=True, stop=True)
                        else:
                            for t in range(CPT):
                                m = nc.tensor.matmul(pj[n % 2][:, t * P:(t + 1) * P],
                                                     hb[:, half * CH + t * P:half * CH + (t + 1) * P],
                                                     wv[:, h, :], start=True, stop=True)
                        m.then_inc(p_mm, 1)

                    pe.wait_ge(h_in, 1)
                    for n in range(6):
                        project(n)
                    for g in range(G + 4):
                        h, r = divmod(g, GRP)
                        if g < G:
                            if r == 0:
                                pe.wait_ge(a_out, 6 * h + 4)
                                pe.wait_ge(q_out, 2 * h + 2)
                            if g >= 2:
                                pe.wait_ge(biased, g - 1)
                            for i in range(4):
                                j = 4 * r + i
                                m = nc.tensor.matmul(sp_[g % 2][:, i, :], qbd[:, h % 2, j, :],
                                                     kk[:, h % 2, BLK * j:BLK * j + P], start=True, stop=True)
                            m.then_inc(s_mm, 1)
                        for n in unit_steps(g):
                            project(n)
                        if 2 <= g < G + 2:
                            k = g - 2
                            pe.wait_ge(normed, k + 1)
                            if k >= 1:
                                pe.wait_ge(pt_out, k)
                            for i in range(4):
                                m = nc.tensor.transpose(tp[:, i, :], pr[:, k % 4, i, :], K.ident[:])
                            m.then_inc(turned, 1)
                        if 3 <= g < G + 3:
                            k = g - 3
                            hh, rr = divmod(k, GRP)
                            pe.wait_ge(pt_out, k + 1)
                            if rr == 0:
                                pe.wait_ge(a_out, 6 * hh + 6)
                                pe.wait_ge(v_sh[hh % 2], 32 * (hh // 2 + 1))
                            if k >= 1:
                                pe.wait_ge(o_out, k)
                            for i in range(4):
                                j = 4 * rr + i
                                src = (vs, vv)[j % 2][:, hh % 2, j // 2, :]
                                for a in range(2):
                                    m = nc.tensor.matmul(op[a * BLK:(a + 1) * BLK, i, :], src[:, a * HD0:(a + 1) * HD0],
                                                         pt[:, k % 2, i, a * BLK:(a + 1) * BLK], start=True, stop=True)
                            m.then_inc(pv_mm, 1)
                        if g >= 4 and (g - 4) % GRP == GRP - 1:
                            hh = (g - 4) // GRP
                            pe.wait_ge(o_out, GRP * (hh + 1))
                            for t in range(TPB):
                                m = nc.tensor.matmul(wp[t // CPT][:, t % CPT, :], oT[:, hh % 2, t * P:(t + 1) * P],
                                                     wo[:, hh, :], start=(hh == 0 and t % CPT == 0),
                                                     stop=(hh == PAIRS - 1), skip_group_check=True)
                            m.then_inc(wo_mm, 1)

                @block.scalar
                def _(act):
                    def evacuate(n):
                        h, u = units[n]
                        half = u % 2
                        act.wait_ge(p_mm, n + 1)
                        if u == 0 and h >= 2:
                            act.wait_ge(s_mm, GRP * (h - 1))
                        if u == 4 and h >= 2:
                            act.wait_ge(pv_mm, GRP * (h - 1))
                            act.wait_ge(v_sh[h % 2], 32 * (h // 2))
                        if u < 2:
                            r = nc.scalar.activation(
                                qbd[0:BLK, h % 2, half * 8:half * 8 + 8, 0:BLK],
                                pj[n % 2][0:BLK, :].rearrange("p (j q) -> p j q", q=BLK), ACT.Copy, scale=qs[0:BLK, h:h + 1])
                        elif u < 4:
                            r = nc.scalar.copy(kk[:, h % 2, BLK + half * CH:BLK + (half + 1) * CH], pj[n % 2][:])
                        else:
                            r = nc.scalar.copy(vv[:, h % 2, half * CPT:(half + 1) * CPT, :],
                                               pj[n % 2][:].rearrange("p (t d) -> p t d", d=P))
                        r.then_inc(a_out, 1)

                    nc.scalar.copy(hb, K.hT[:, bass.ds(b * T, T)]).then_inc(h_in, 1)
                    for n in range(6):
                        evacuate(n)
                    for g in range(G + 3):
                        for n in unit_steps(g):
                            evacuate(n)
                        if g < G:
                            act.wait_ge(biased, g + 1)
                            if g >= 4:
                                act.wait_ge(turned, g - 3)
                            for i in range(4):
                                r = nc.scalar.activation(pr[:, g % 4, i, :], sb_[:, g % 4, i, :], ACT.Exp, scale=-1.0,
                                                         bias=mn[:, g % 4, i:i + 1], accum_out=sm[:, g % 4, i:i + 1])
                            r.then_inc(exped, 1)
                        if g >= 3:
                            k = g - 3
                            act.wait_ge(pv_mm, k + 1)
                            if k % GRP == 0 and k >= 2 * GRP:
                                act.wait_ge(wo_mm, k // GRP - 1)
                            nc.scalar.copy(oT[:, k // GRP % 2, (k % GRP) * 256:(k % GRP + 1) * 256],
                                           op[:].rearrange("p i q -> p (i q)")).then_inc(o_out, 1)

                @block.vector
                def _(dve):
                    v = nc.vector

                    def evacuate(n):
                        h, u = units[n]
                        if u >= 2:
                            return
                        dve.wait_ge(p_mm, n + 1)
                        if u == 0 and h >= 2:
                            dve.wait_ge(s_mm, GRP * (h - 1))
                        v.tensor_scalar(qbd[BLK:P, h % 2, u * 8:u * 8 + 8, BLK:P],
                                        pj[n % 2][BLK:P, :].rearrange("p (j q) -> p j q", q=BLK),
                                        qs[BLK:P, h:h + 1], None, ALU.mult).then_inc(q_out, 1)

                    for n in range(6):
                        evacuate(n)
                    for g in range(G + 2):
                        h, r = divmod(g, GRP)
                        for n in unit_steps(g):
                            evacuate(n)
                        if g < G:
                            dve.wait_ge(s_mm, g + 1)
                            if g >= 4:
                                dve.wait_ge(exped, g - 3)
                            for i in range(4):
                                first = 1 if 4 * r + i == 0 else 0
                                q = v.tensor_tensor_reduce(sb_[:, g % 4, i, :], sp_[g % 2][:, i, :],
                                                           nbias[:, h, first, :], 1.0, 3e38, ALU.add, ALU.min,
                                                           mn[:, g % 4, i:i + 1])
                            q.then_inc(biased, 1)
                        if 1 <= g < G + 1:
                            dve.wait_ge(exped, g)
                            v.reciprocal(ri[:, (g - 1) % 4, :], sm[:, (g - 1) % 4, :]).then_inc(rsum, 1)
                        if g >= 2:
                            k = g - 2
                            dve.wait_ge(turned, k + 1)
                            if k >= 2:
                                dve.wait_ge(pv_mm, k - 1)
                            v.tensor_copy(pt[:, k % 2], tp[:]).then_inc(pt_out, 1)
                    dve.wait_ge(wo_mm, PAIRS)
                    for i in range(2):
                        v.tensor_tensor(tmp[:, i * CPT:(i + 1) * CPT, :], wp[i][:],
                                        bc(K.mod_rows[:, 0, bass.ds(b, 1), GA, :].rearrange("p a d -> p (a d)"), 1, CPT),
                                        ALU.mult).then_inc(xt, 1)
                    dve.wait_ge(xt, 2)
                    xs = K.x[:, bass.ds(b * TPB, TPB), :]
                    v.tensor_tensor(xs, xs, tmp, ALU.add)

                @block.gpsimd
                def _(pool):
                    for g in range(G):
                        pool.wait_ge(rsum, g + 1)
                        pb = pr[:, g % 4]
                        nc.gpsimd.tensor_tensor(pb, pb, bc(ri[:, g % 4, :], 2, P), ALU.mult).then_inc(normed, 1)

                @block.sync
                def _(sp):
                    for h in range(PAIRS):
                        sp.wait_ge(a_out, 6 * h + 6)
                        if h >= 2:
                            sp.wait_ge(pv_mm, GRP * (h - 1))
                        sp.dma_start(vs[BLK:P, h % 2], vv[0:BLK, h % 2]).then_inc(v_sh[h % 2], 16)
                        sp.dma_start(vs[0:BLK, h % 2, 1:TPB], vv[BLK:P, h % 2, 0:TPB - 1]).then_inc(v_sh[h % 2], 16)
                    sp.wait_ge(v_sh0, 16 * PAIRS)
                    sp.wait_ge(v_sh1, 16 * PAIRS)
            nc.all_engine_barrier(sems_to_clear=clear)


def routing_stage(nc, K, A, name, wgT, bias, b2, renormalise, M):
    with ExitStack() as st:
        wg = K.sb(name + "_wg", [P, E], ctx=st)
        bg = K.sb(name + "_bg", [P, E], ctx=st)
        b2s = K.sb(name + "_b2", [E, D], ctx=st)
        lg = K.sb(name + "_logits", [P, NT, E], ctx=st)
        mx = K.sb(name + "_max", [P, NT], ctx=st)
        ex = K.sb(name + "_exp", [P, NT, E], ctx=st)
        sm = K.sb(name + "_sum", [P, NT], ctx=st)
        rs = K.sb(name + "_rsum", [P, NT], ctx=st)
        pb = K.sb(name + "_probs", [P, NT, E], ctx=st)
        gt = K.sb(name + "_above", [P, NT, E * E], ctx=st)
        eq = K.sb(name + "_equal", [P, NT, E * E], ctx=st)
        low = K.sb(name + "_lower", [P, E * E], ctx=st)
        rank = K.sb(name + "_rank", [P, NT, E], ctx=st)
        wT = K.sb(name + "_wT", [E, NT, P], ctx=st)
        w3 = K.sb(name + "_w3", [P, NT, 3, E], ctx=st)
        wp = K.sb(name + "_wp", [P, NT, E], BF16, ctx=st)
        wr = K.sb(name + "_wr", [P, NT, E], ctx=st)
        raw = K.sb(name + "_raw", [P, RAW, M.F], ctx=st)
        sraw = K.sb(name + "_sraw", [KROWS, E * P], ctx=st)
        lp = K.ps(name + "_lps", [P, NT, E], st)
        tp = [K.ps(f"{name}_tps{i}", [P, CPT, P], st) for i in range(2)]
        bp = [K.ps(f"{name}_bps{i}", [P, CPT, D], st) for i in range(2)]
        (w_in, l_mm, dve, act_s, t_mm, t_out, b_mm, b_out) = K.sems(st, 
            name, "w_in", "logits_mm", "dve", "act", "turned", "wT_out", "b2_mm", "b2_out")
        (s_in, hi_out, lo_out, zeroed, *m_in) = K.sems(
            st, name + "m", "sel_in", "hi_out", "lo_out", "zeroed", *(f"matrix_in{i}" for i in range(RAW)))
        matrices = [(w, part, e) for w, part in ((M.w1, M.w1_in), (M.w2, M.w2_in)) for e in range(E)]
        n_in = 2 + (bias is not None) + (b2 is not None)
        n_chain = 11 + (bias is not None) + 4 * renormalise
        b_turns = NCH * (b2 is not None)
        with nc.Block() as block:
            @block.sync
            def _(sp):
                sp.dma_start(wg[:], wgT).then_inc(w_in, 16)
                sp.dma_start(low[:], A["lower"]).then_inc(w_in, 16)
                if bias is not None:
                    sp.dma_start(bg[:], bias.partition_broadcast(P)).then_inc(w_in, 16)
                if b2 is not None:
                    sp.dma_start(b2s[:], b2).then_inc(w_in, 16)
                sp.dma_start(sraw[:], A["select"]).then_inc(s_in, 16)
                if M.b1_in is not None:
                    sp.dma_start(M.b1[:], M.b1_in).then_inc(s_in, 16)
                for i, (w, part, e) in enumerate(matrices):
                    if i >= RAW:
                        sp.wait_ge(lo_out, i - RAW + 1)
                    src = part[e] if part is M.w1_in else part[e].rearrange("(c p) d -> p c d", p=P)
                    dst = raw[:, i % RAW, :]
                    if part is M.w2_in:
                        dst = dst.rearrange("p (c d) -> p c d", d=D)
                    sp.dma_start(dst, src).then_inc(m_in[i % RAW], 16)
                sp.wait_ge(s_in, 16 * (1 + (M.b1_in is not None)))

            @block.gpsimd
            def _(pool):
                nc.gpsimd.memset(M.wT3[:], 0.0).then_inc(zeroed, 1)
                for i, (w, part, e) in enumerate(matrices):
                    pool.wait_ge(hi_out, i + 1)
                    cs = slice(e * M.F, (e + 1) * M.F)
                    nc.gpsimd.tensor_tensor(w[1][:, cs], raw[:, i % RAW, :], w[0][:, cs].bitcast(F32),
                                            ALU.subtract).then_inc(lo_out, 1)

            @block.tensor
            def _(pe):
                pe.wait_ge(w_in, 16 * n_in)
                for t in range(NT):
                    m = nc.tensor.matmul(lp[:, t, :], K.hT[:, t * P:(t + 1) * P], wg[:], start=True, stop=True)
                m.then_inc(l_mm, 1)
                if b2 is not None:
                    pe.wait_ge(dve, n_chain)
                    for c in range(NCH):
                        if c >= 2:
                            pe.wait_ge(t_out, c - 1)
                        for t in range(CPT):
                            m = nc.tensor.transpose(tp[c % 2][0:E, t, :], K.w[:, c * CPT + t, :], K.ident[:])
                        m.then_inc(t_mm, 1)
                    for c in range(NCH):
                        pe.wait_ge(t_out, c + 1)
                        if c >= 2:
                            pe.wait_ge(b_out, c - 1)
                        for t in range(CPT):
                            m = nc.tensor.matmul(bp[c % 2][:, t, :], wT[:, c * CPT + t, :], b2s[:], start=True, stop=True)
                        m.then_inc(b_mm, 1)
                pe.wait_ge(dve, n_chain + 6)
                for c in range(NCH):
                    u = c + b_turns
                    if u >= 2:
                        pe.wait_ge(t_out, u - 1)
                    for t in range(CPT):
                        m = nc.tensor.transpose(tp[u % 2][0:3 * E, t, :],
                                                w3[:, c * CPT + t].rearrange("p a e -> p (a e)"), K.ident[:])
                    m.then_inc(t_mm, 1)

            @block.scalar
            def _(act):
                act.wait_ge(dve, 2 + (bias is not None))
                nc.scalar.activation(ex[:], lg[:], ACT.Exp).then_inc(act_s, 1)
                for i, (w, part, e) in enumerate(matrices):
                    act.wait_ge(m_in[i % RAW], 16 * (i // RAW + 1))
                    nc.scalar.copy(w[0][:, e * M.F:(e + 1) * M.F], raw[:, i % RAW, :]).then_inc(hi_out, 1)
                if b2 is not None:
                    for c in range(NCH):
                        act.wait_ge(t_mm, c + 1)
                        nc.scalar.copy(wT[:, c * CPT:(c + 1) * CPT, :], tp[c % 2][0:E]).then_inc(t_out, 1)
                act.wait_ge(zeroed, 1)
                for c in range(NCH):
                    u = c + b_turns
                    act.wait_ge(t_mm, u + 1)
                    nc.scalar.copy(M.wT3[0:3 * E, c * CH:(c + 1) * CH],
                                   tp[u % 2][0:3 * E].rearrange("e t q -> e (t q)")).then_inc(t_out, 1)
                act.wait_ge(s_in, 16 * (1 + (M.b1_in is not None)))
                nc.scalar.copy(M.sel[:], sraw[:])

            @block.vector
            def _(dve_):
                v = nc.vector
                n = [0]

                def step(ins):
                    n[0] += 1
                    ins.then_inc(dve, 1)
                    dve_.wait_ge(dve, n[0])

                dve_.wait_ge(w_in, 16 * n_in)
                dve_.wait_ge(l_mm, 1)
                if bias is not None:
                    step(v.tensor_tensor(lg[:], lp[:], bc(bg[:], 1, NT), ALU.add))
                    src = lg
                else:
                    src = lp
                step(v.tensor_reduce(mx[:], src[:], AX.X, ALU.max))
                step(v.tensor_tensor(lg[:], src[:], bc(mx[:], 2, E), ALU.subtract))
                dve_.wait_ge(act_s, 1)
                step(v.tensor_reduce(sm[:], ex[:], AX.X, ALU.add))
                step(v.reciprocal(rs[:], sm[:]))
                step(v.tensor_tensor(pb[:], ex[:], bc(rs[:], 2, E), ALU.mult))
                over = bc(pb[:], 2, E)
                own = bc(pb[:], 3, E)
                g4 = gt[:].rearrange("p t (a b) -> p t a b", a=E)
                e4 = eq[:].rearrange("p t (a b) -> p t a b", a=E)
                step(v.tensor_tensor(g4, over, own, ALU.is_gt))
                step(v.tensor_tensor(e4, over, own, ALU.is_equal))
                step(v.tensor_tensor(eq[:], eq[:], bc(low[:], 1, NT), ALU.mult))
                step(v.tensor_tensor(gt[:], gt[:], eq[:], ALU.add))
                step(v.tensor_reduce(rank[:], g4, AX.X, ALU.add))
                step(v.scalar_tensor_tensor(out=K.w[:], in0=rank[:], scalar=2.0, in1=pb[:], op0=ALU.is_lt,
                                            op1=ALU.mult))
                if renormalise:
                    step(v.tensor_reduce(sm[:], K.w[:], AX.X, ALU.add))
                    step(v.tensor_scalar(sm[:], sm[:], TOPK_EPS, None, ALU.add))
                    step(v.reciprocal(rs[:], sm[:]))
                    step(v.tensor_tensor(K.w[:], K.w[:], bc(rs[:], 2, E), ALU.mult))
                assert n[0] == n_chain
                step(v.tensor_copy(wp[:], K.w[:]))
                step(v.tensor_copy(w3[:, :, 0, :], wp[:]))
                step(v.tensor_tensor(wr[:], K.w[:], wp[:], ALU.subtract))
                step(v.tensor_copy(wp[:], wr[:]))
                step(v.tensor_copy(w3[:, :, 1, :], wp[:]))
                step(v.tensor_tensor(w3[:, :, 2, :], wr[:], wp[:], ALU.subtract))
                if b2 is not None:
                    for c in range(NCH):
                        dve_.wait_ge(b_mm, c + 1)
                        h = K.nat[:, c * CPT:(c + 1) * CPT, :]
                        v.tensor_tensor(h, h, bp[c % 2][:], ALU.add).then_inc(b_out, 1)


RAW = 4


class Experts:

    def __init__(self, K, A, name, F, w1, w2, b1, st):
        self.F, self.w1_in, self.w2_in, self.b1_in = F, w1, w2, b1
        self.w1 = [K.sb(f"{name}_w1{part}", [P, E * F], F32R, ctx=st) for part in ("hi", "lo")]
        self.w2 = [K.sb(f"{name}_w2{part}", [P, E * F], F32R, ctx=st) for part in ("hi", "lo")]
        self.b1 = K.sb(name + "_b1", [P, E * F // P], ctx=st)
        self.wT3 = K.sb(name + "_wT3", [KROWS, B * T], BF16, ctx=st)
        self.sel = K.sb(name + "_sel", [KROWS, E * P], BF16, ctx=st)


def expert_stage(nc, K, A, name, M, gelu, layer):
    F = M.F
    FC = F // P
    with ExitStack() as st:
        hs = [K.sb(f"{name}_h{part}", [P, 2, CH], F32R, ctx=st) for part in ("hi", "lo")]
        hf = K.sb(name + "_hid", [P, 3, CH], ctx=st)
        hid = [K.sb(f"{name}_hid_{part}", [P, 2, FC, CH], F32R, ctx=st) for part in ("hi", "lo")]
        wbs = K.sb(name + "_wb", [P, 2, CH], ctx=st)
        ym = K.sb(name + "_ym", [P, 2, CH], ctx=st)
        hp = [K.ps(f"{name}_hps{i}", [P, CH], st) for i in range(4)]
        yp = [K.ps(f"{name}_yps{i}", [P, CH], st) for i in range(2)]
        wp = K.ps(f"{name}_wps", [P, CH], st)
        (h_hi, h_lo, h_mm, g_out, hid_hi, hid_lo, w_mm, w_out, y_mm, y_out, y_sum, x_out), clear = K.moe_sems
        S = 2 * E
        SPLITS = (E // 2, E + E // 2)

        def sums(k):
            return k + 1 - (k // E + 1)

        (hi0, lo0) = K.sems(st, name + "h", "h_hi", "h_lo")
        with nc.Block() as block:
            @block.scalar
            def _(act):
                nc.scalar.copy(hs[0][:, 0, :], K.hT[:, 0:CH]).then_inc(hi0, 1)

            @block.vector
            def _(dve):
                nc.vector.memset(K.hT[:, B * T:], 0.0)
                dve.wait_ge(hi0, 1)
                nc.vector.tensor_tensor(hs[1][:, 0, :], K.hT[:, 0:CH], hs[0][:, 0, :].bitcast(F32), ALU.subtract
                                        ).then_inc(lo0, 1)

        with nc.Fori(0, B) as b:
            def tokens(c):
                return K.hT[:, bass.ds(b * T + c * CH, CH)]

            def acc(c):
                return K.nat[:, bass.ds(b * TPB + c * CPT, CPT), :].rearrange("p t d -> p (t d)")

            with nc.Block() as block:
                @block.tensor
                def _(pe):
                    def passes(out, w, cols, x, first, last):
                        nc.tensor.matmul(out, w[0][:, cols], x[0], start=first, stop=False)
                        nc.tensor.matmul(out, w[0][:, cols], x[1], start=False, stop=False)
                        return nc.tensor.matmul(out, w[1][:, cols], x[0], start=False, stop=last)

                    for s in range(S + 1):
                        if s < S:
                            c, e = divmod(s, E)
                            if s == E:
                                pe.wait_ge(h_lo, 1)
                            for f in range(FC):
                                n = s * FC + f
                                if n >= 4:
                                    pe.wait_ge(g_out, n - 3)
                                passes(hp[n % 4][:], M.w1, slice((e * FC + f) * P, (e * FC + f + 1) * P),
                                       [x[:, c, :] for x in hs], True, True).then_inc(h_mm, 1)
                            if s >= 1:
                                pe.wait_ge(w_out, s)
                            nc.tensor.matmul(wp[:], M.sel[:, e * P:(e + 1) * P],
                                             M.wT3[:, bass.ds(b * T + c * CH, CH)], start=True, stop=True
                                             ).then_inc(w_mm, 1)
                        if s >= 1:
                            k = s - 1
                            e = k % E
                            pe.wait_ge(hid_lo, FC * (k + 1))
                            if k >= 2:
                                pe.wait_ge(y_out, k - 1)
                            for f in range(FC):
                                m = passes(yp[k % 2][:], M.w2, slice((e * FC + f) * D, (e * FC + f + 1) * D),
                                           [x[:, k % 2, f, :] for x in hid], f == 0, f == FC - 1)
                            m.then_inc(y_mm, 1)

                @block.scalar
                def _(act):
                    for s in range(S):
                        for f in range(FC):
                            n = s * FC + f
                            act.wait_ge(h_mm, n + 1)
                            if n >= 3:
                                act.wait_ge(hid_lo, n - 2)
                            col = s % E * FC + f
                            nc.scalar.activation(hf[:, n % 3, :], hp[n % 4][:], gelu,
                                                 bias=M.b1[:, col:col + 1] if M.b1_in is not None else 0.0
                                                 ).then_inc(g_out, 1)
                        act.wait_ge(w_mm, s + 1)
                        if s >= 2:
                            act.wait_ge(y_out, s - 1)
                        nc.scalar.copy(wbs[:, s % 2, :], wp[:]).then_inc(w_out, 1)
                        for i, split in enumerate(SPLITS):
                            if s == split:
                                nc.scalar.copy(hs[0][:, 1 - i, :], tokens(1 + i)).then_inc(h_hi, 1)

                @block.gpsimd
                def _(pool):
                    for k in range(S):
                        c, e = divmod(k, E)
                        if e:
                            pool.wait_ge(y_out, k + 1)
                            if e >= 2:
                                pool.wait_ge(y_sum, sums(k - 1))
                            nc.gpsimd.tensor_tensor(acc(c), acc(c), ym[:, k % 2, :], ALU.add).then_inc(y_sum, 1)

                @block.vector
                def _(dve):
                    v = nc.vector

                    def weigh(k):
                        c, e = divmod(k, E)
                        dve.wait_ge(y_mm, k + 1)
                        dve.wait_ge(w_out, k + 1)
                        if k >= 2 and sums(k - 2):
                            dve.wait_ge(y_sum, sums(k - 2))
                        v.tensor_tensor(acc(c) if e == 0 else ym[:, k % 2, :], yp[k % 2][:], wbs[:, k % 2, :],
                                        ALU.mult).then_inc(y_out, 1)

                    ts = bass.ds(b * TPB, TPB)
                    gate = K.mod_rows[:, layer, bass.ds(b, 1), GB, :].rearrange("p a d -> p (a d)")
                    gated = ym[:].rearrange("p a (t d) -> p (a t) d", d=D)
                    v.tensor_tensor(gated, K.nat[:, ts, :], bc(gate, 1, TPB), ALU.mult).then_inc(x_out, 1)
                    dve.wait_ge(x_out, 1)
                    v.tensor_tensor(K.x[:, ts, :], K.x[:, ts, :], gated, ALU.add).then_inc(x_out, 1)
                    dve.wait_ge(x_out, 2)
                    for s in range(S):
                        for f in range(FC):
                            n = s * FC + f
                            dve.wait_ge(g_out, n + 1)
                            if f == 0 and s >= 2:
                                dve.wait_ge(y_mm, s - 1)
                            v.tensor_copy(hid[0][:, s % 2, f, :], hf[:, n % 3, :]).then_inc(hid_hi, 1)
                            dve.wait_ge(hid_hi, n + 1)
                            v.tensor_tensor(hid[1][:, s % 2, f, :], hf[:, n % 3, :],
                                            hid[0][:, s % 2, f, :].bitcast(F32), ALU.subtract).then_inc(hid_lo, 1)
                        if s >= 1:
                            weigh(s - 1)
                        for i, split in enumerate(SPLITS):
                            if s == split:
                                dve.wait_ge(h_hi, i + 1)
                                v.tensor_tensor(hs[1][:, 1 - i, :], tokens(1 + i), hs[0][:, 1 - i, :].bitcast(F32),
                                                ALU.subtract).then_inc(h_lo, 1)
                    weigh(S - 1)
            nc.all_engine_barrier(sems_to_clear=clear)

        (gated, turned, added) = K.sems(st, name + "x", "gated", "turned", "added")
        with nc.Block() as block:
            @block.scalar
            def _(act):
                for c in range(NCH):
                    if c >= 2:
                        act.wait_ge(turned, c - 1)
                    nc.scalar.activation(ym[:, c % 2, :], K.nat[:, c * CPT:(c + 1) * CPT, :].rearrange("p t d -> p (t d)"),
                                         ACT.Identity, scale=K.mod_cols[:, layer, GB, c * CH // T:c * CH // T + 1]
                                         ).then_inc(gated, 1)

            @block.tensor
            def _(pe):
                for c in range(NCH):
                    pe.wait_ge(gated, c + 1)
                    if c >= 2:
                        pe.wait_ge(added, c - 1)
                    for t in range(CPT):
                        m = nc.tensor.transpose(yp[c % 2][:, t * P:(t + 1) * P], ym[:, c % 2, t * P:(t + 1) * P], K.ident[:])
                    m.then_inc(turned, 1)

            @block.vector
            def _(dve):
                for c in range(NCH):
                    dve.wait_ge(turned, c + 1)
                    h = K.x[:, c * CPT:(c + 1) * CPT, :]
                    nc.vector.tensor_tensor(h, h, yp[c % 2][:].rearrange("p (t d) -> p t d", d=D), ALU.add
                                            ).then_inc(added, 1)


def split3(v, eng, done, count, f, parts, r):
    v.tensor_copy(parts[0], f).then_inc(done, 1)
    eng.wait_ge(done, count + 1)
    v.tensor_tensor(r, f, parts[0], ALU.subtract).then_inc(done, 1)
    eng.wait_ge(done, count + 2)
    v.tensor_copy(parts[1], r).then_inc(done, 1)
    eng.wait_ge(done, count + 3)
    v.tensor_tensor(parts[2], r, parts[1], ALU.subtract).then_inc(done, 1)
    return count + 4


def qkv1_stage(nc, K, A, v_nat, parts_dram):
    with ExitStack() as st:
        w = K.sb("w1_qkvT", [P, 3, D], ctx=st)
        bqk = K.sb("b1_qk", [P, 2], ctx=st)
        bqs = K.sb("b1_qk_scaled", [P, 2], ctx=st)
        bv = K.sb("b1_v", [P, D], ctx=st)
        f = K.sb("qk_f", [P, 3, CH], ctx=st)
        r = K.sb("qk_r", [P, 2, CH], ctx=st)
        pa = K.sb("qk_parts", [P, 2, 3, CH], BF16, ctx=st)
        qp = [K.ps(f"qk_ps{i}", [P, CH], st) for i in range(2)]
        vp = [K.ps(f"v1_ps{i}", [P, CPT, D], st) for i in range(2)]
        (w_in, b_s, q_mm, f_out, split, q_stored, k_stored, v_mm, v_out) = K.sems(st, 
            "qkv1", "w_in", "bias", "qk_mm", "qk_out", "split", "q_stored", "k_stored", "v_mm", "v_out")
        stored = (q_stored, k_stored)
        units = [(c, i) for c in range(NCH) for i in range(2)]
        with nc.Block() as block:
            @block.sync
            def _(sp):
                for i, n in enumerate(("L1_attn_WqT", "L1_attn_WkT", "L1_attn_WvT")):
                    sp.dma_start(w[:, i, :], A[n]).then_inc(w_in, 16)
                for i, n in enumerate(("L1_attn_bq", "L1_attn_bk")):
                    sp.dma_start(bqk[:, i:i + 1], A[n].rearrange("(p a) -> p a", a=1)).then_inc(w_in, 16)
                sp.dma_start(bv[:], A["L1_attn_bv"].partition_broadcast(P)).then_inc(w_in, 16)
                for n, (c, i) in enumerate(units):
                    sp.wait_ge(split, 4 * (n + 1))
                    sp.dma_start(parts_dram[i, :, :, c * CH:(c + 1) * CH].rearrange("a p t -> p a t"),
                                 pa[:, n % 2]).then_inc(stored[i], 16)
                    if c * CH >= (B - 1) * T:
                        sp.dma_start(parts_dram[i, :, :, c * CH + T:(c + 1) * CH + T].rearrange("a p t -> p a t"),
                                     pa[:, n % 2]).then_inc(stored[i], 16)
                for q in stored:
                    sp.wait_ge(q, 16 * (NCH + T // CH))

            @block.tensor
            def _(pe):
                pe.wait_ge(w_in, 16 * 6)
                for n, (c, i) in enumerate(units):
                    if n >= 2:
                        pe.wait_ge(f_out, n - 1)
                    nc.tensor.matmul(qp[n % 2][:], w[:, i, :], K.hT[:, c * CH:(c + 1) * CH],
                                     start=True, stop=True).then_inc(q_mm, 1)
                    if i == 1:
                        if c >= 2:
                            pe.wait_ge(v_out, c - 1)
                        for t in range(CPT):
                            m = nc.tensor.matmul(vp[c % 2][:, t, :], K.hT[:, c * CH + t * P:c * CH + (t + 1) * P],
                                                 w[:, 2, :], start=True, stop=True)
                        m.then_inc(v_mm, 1)

            @block.scalar
            def _(act):
                act.wait_ge(b_s, 1)
                for n, (c, i) in enumerate(units):
                    act.wait_ge(q_mm, n + 1)
                    if n >= 3:
                        act.wait_ge(split, 4 * (n - 2))
                    nc.scalar.activation(f[:, n % 3, :], qp[n % 2][:], ACT.Identity, bias=bqs[:, i:i + 1],
                                         scale=HD1 ** -0.5 if i == 0 else 1.0).then_inc(f_out, 1)

            @block.vector
            def _(dve):
                v = nc.vector
                dve.wait_ge(w_in, 16 * 6)
                v.tensor_copy(bqs[:, 1:2], bqk[:, 1:2])
                v.tensor_scalar(bqs[:, 0:1], bqk[:, 0:1], HD1 ** -0.5, None, ALU.mult).then_inc(b_s, 1)
                count = 0
                for n, (c, i) in enumerate(units):
                    dve.wait_ge(f_out, n + 1)
                    if n >= 2:
                        dve.wait_ge(stored[i], 16 * (c + max(0, c - (B - 1) * T // CH)))
                        dve.wait_ge(split, count)
                    count = split3(v, dve, split, count, f[:, n % 3, :], [pa[:, n % 2, j, :] for j in range(3)],
                                   r[:, n % 2, :])
                    if i == 1:
                        dve.wait_ge(v_mm, c + 1)
                        v.tensor_tensor(v_nat[:, c * CPT:(c + 1) * CPT, :], vp[c % 2][:], bc(bv[:], 1, CPT),
                                        ALU.add).then_inc(v_out, 1)


ATT_SEMS = ("loaded0", "loaded1", "loaded2", "loaded3", "m1_mm", "maxed", "m_turned", "m_neg", "m_split", "m_stored", "m_loaded",
            "s2_mm", "exp", "v_aug", "pv_mm", "o_out", "o_turned", "o_done", "o_rsum")


def full_attention_stage(nc, K, A):
    parts = nc.dram_tensor("qk_parts_dram", [2, 3, P, (B + 1) * T], BF16, kind="Internal").ap()
    mdram = nc.dram_tensor("neg_max_dram", [2, 3, 4 * TPB * P], BF16, kind="Internal").ap()
    with ExitStack() as st:
        v_nat = K.sb("v_nat", [P, NT, D], ctx=st)
        qkv1_stage(nc, K, A, v_nat, parts)
        qs = K.sb("q_stack", [P, 4, 4, T], BF16, ctx=st)
        ks = K.sb("k_stack", [P, 4, 4, T], BF16, ctx=st)
        va = K.sb("v_aug", [P, 2, TPB, 4, 32], ctx=st)
        pr = K.sb("probs1", [P, 2, 4, CH], ctx=st)
        osb = K.sb("o_sb", [P, 2, CH], ctx=st)
        mx = K.sb("q_max", [P, 2, 4 * TPB], ctx=st)
        nm = K.sb("neg_max", [4 * TPB, P], ctx=st)
        nr = K.sb("neg_max_rest", [4 * TPB, P], ctx=st)
        mp = K.sb("neg_max_parts", [4 * TPB, 2, 3, P], BF16, ctx=st)
        ro = K.sb("o_rsum", [P, 2, CPT, 4], ctx=st)
        s1 = [K.ps(f"s1_ps{i}", [P, T], st) for i in range(2)]
        s2 = [K.ps(f"s2_ps{i}", [P, CH], st) for i in range(2)]
        op = K.ps("o1_ps", [P, CH], st)
        mi = K.ps("misc_ps", [P, CPT, P], st)
        def load(sp, sem, ring, batch, quad):
            for i, (dst, order) in enumerate(((qs, Q_PART), (ks, K_PART))):
                for slot, part in enumerate(order):
                    src = parts[i, part, quad * 32:(quad + 1) * 32, bass.ds(batch * T, T)]
                    sp.dma_start(dst[slot * HD1:(slot + 1) * HD1, ring], src.rearrange("(h d) t -> d h t", d=HD1)
                                 ).then_inc(sem, 16)
            sp.dma_start(qs[MROW:MROW + 3, ring], ks[KROWS - 3:KROWS, ring]).then_inc(sem, 16)

        LOADS = 16 * (2 * len(Q_PART) + 1)

        UNITS = 4 * TPB
        LEAD = 8

        def first_pass(pe, sm, k, ring, n):
            h, qt = divmod(n, TPB)
            if k >= 2:
                pe.wait_ge(sm["maxed"], k - 1)
            for c in range(2):
                m = nc.tensor.matmul(s1[k % 2][:, c * CH:(c + 1) * CH], qs[0:KROWS, ring, h, qt * P:(qt + 1) * P],
                                     ks[0:KROWS, ring, h, c * CH:(c + 1) * CH], start=True, stop=True)
            m.then_inc(sm["m1_mm"], 1)

        def reduce_max(dve, sm, k, ring, n):
            dve.wait_ge(sm["m1_mm"], k + 1)
            nc.vector.tensor_reduce(mx[:, ring % 2, n:n + 1], s1[k % 2][:], AX.X, ALU.max).then_inc(sm["maxed"], 1)

        def turn_max(pe, sm, ring, units):
            pe.wait_ge(sm["maxed"], units)
            nc.tensor.transpose(mi[0:UNITS, 0, :], mx[:, ring % 2, :], K.ident[:]).then_inc(sm["m_turned"], 1)

        def negate_max(dve, sm, slot):
            dve.wait_ge(sm["m_turned"], slot + 1)
            if slot >= 1:
                dve.wait_ge(sm["m_split"], 4 * slot)
            nc.vector.tensor_scalar(nm[:], mi[0:UNITS, 0, :], -1.0, None, ALU.mult).then_inc(sm["m_neg"], 1)

        def split_max(pool, sm, ring, slot):
            pool.wait_ge(sm["m_neg"], slot + 1)
            if slot >= 2:
                pool.wait_ge(sm["m_stored"], 16 * (slot - 1))
            split3(nc.gpsimd, pool, sm["m_split"], 4 * slot, nm[:], [mp[:, ring % 2, j, :] for j in range(3)], nr[:])

        def move_max(sp, sm, ring, slot, units):
            sp.wait_ge(sm["m_split"], 4 * (slot + 1))
            if slot >= 1:
                sp.wait_ge(sm["m_loaded"], 16 * slot)
            sp.dma_start(mdram[ring % 2].rearrange("a (c q) -> c a q", q=P), mp[:, ring % 2]).then_inc(sm["m_stored"], 16)
            sp.wait_ge(sm["m_stored"], 16 * (slot + 1))
            sp.wait_ge(sm["maxed"], units)
            sp.dma_start(qs[MROW:MROW + 3, ring], mdram[ring % 2].rearrange("a (h t) -> a h t", h=4)
                         ).then_inc(sm["m_loaded"], 16)

        (zeros, ones_set) = K.sems(st, "att1z", "zeros", "ones")
        flat = "p a h t -> p (a h t)"
        sm0 = dict(zip(ATT_SEMS, K.sems(st, "att1p", *ATT_SEMS)))
        ahead = [(0, n) for n in range(UNITS)] + [(1, n) for n in range(LEAD)]
        with nc.Block() as block:
            @block.gpsimd
            def _(pool):
                g = nc.gpsimd
                g.memset(ks[32:64].rearrange(flat), 1.0).then_inc(ones_set, 1)
                pool.wait_ge(ones_set, 1)
                g.memset(va[:].rearrange("p a t h c -> p (a t h c)"), 0.0).then_inc(ones_set, 1)
                pool.wait_ge(ones_set, 2)
                g.memset(va[:, :, :, :, HD1:HD1 + 1].rearrange("p a t h c -> p (a t h) c"), 1.0).then_inc(ones_set, 1)
                split_max(pool, sm0, 0, 0)

            @block.sync
            def _(sp):
                sp.wait_ge(zeros, 2)
                sp.wait_ge(ones_set, 1)
                for n in range(2):
                    load(sp, sm0[f"loaded{n}"], n, 0, n)
                for n in range(2):
                    sp.wait_ge(sm0[f"loaded{n}"], LOADS)
                move_max(sp, sm0, 0, 0, UNITS)
                sp.wait_ge(sm0["m_loaded"], 16)

            @block.tensor
            def _(pe):
                for k, (ring, n) in enumerate(ahead):
                    if n == 0:
                        pe.wait_ge(sm0[f"loaded{ring}"], LOADS)
                    first_pass(pe, sm0, k, ring, n)
                    if k == UNITS + 1:
                        turn_max(pe, sm0, 0, UNITS)

            @block.vector
            def _(dve):
                nc.vector.memset(qs[0:KROWS].rearrange(flat).bitcast(F32), 0.0).then_inc(zeros, 1)
                nc.vector.memset(ks[64:KROWS].rearrange(flat).bitcast(F32), 0.0).then_inc(zeros, 1)
                for k, (ring, n) in enumerate(ahead):
                    reduce_max(dve, sm0, k, ring, n)
                    if k == UNITS:
                        negate_max(dve, sm0, 0)

        sm_list, clear = K.att_sems
        sm = dict(zip(ATT_SEMS, sm_list))
        STEPS = 2 * TPB
        REST = UNITS - LEAD

        def unit(s, u):
            return ((s + 1) % 4, u + LEAD) if u < REST else ((s + 2) % 4, u - REST)

        TURN_MAX = REST // 2
        TURN_OUT = 2
        with nc.Fori(0, B) as b:
            with nc.Block() as block:
                @block.sync
                def _(sp):
                    for s in range(QUADS):
                        if s >= 2:
                            sp.wait_ge(sm["s2_mm"], 4 * STEPS * (s - 1))
                        nq = s + 2
                        load(sp, sm[f"loaded{nq % 4}"], nq % 4, b + nq // 4, nq % 4)
                        move_max(sp, sm, (s + 1) % 4, s, UNITS * s + REST)
                    for n in range(QUADS):
                        sp.wait_ge(sm[f"loaded{n}"], LOADS)
                    sp.wait_ge(sm["m_loaded"], 16 * QUADS)

                @block.gpsimd
                def _(pool):
                    for s in range(QUADS):
                        if s >= 1:
                            split_max(pool, sm, s % 4, s - 1)
                        if s >= 2:
                            pool.wait_ge(sm["pv_mm"], STEPS * (s - 1))
                        nc.gpsimd.tensor_copy(
                            va[:, s % 2, :, :, 0:HD1],
                            v_nat[:, bass.ds(b * TPB, TPB), s * 32:(s + 1) * 32].rearrange("p t (h d) -> p t h d", d=HD1)
                        ).then_inc(sm["v_aug"], 1)
                    split_max(pool, sm, QUADS % 4, QUADS - 1)

                @block.tensor
                def _(pe):
                    def scores(k, h):
                        s, i = divmod(k, STEPS)
                        half, kt = divmod(i, TPB)
                        if i == 0 and s >= 1 and h == 0:
                            pe.wait_ge(sm["m_loaded"], 16 * s)
                        n = 4 * k + h
                        if n >= 2:
                            pe.wait_ge(sm["exp"], n - 1)
                        nc.tensor.matmul(s2[n % 2][:], ks[0:KROWS, s, h, kt * P:(kt + 1) * P],
                                         qs[0:KROWS, s, h, half * CH:(half + 1) * CH],
                                         start=True, stop=True).then_inc(sm["s2_mm"], 1)

                    def product(k):
                        s, i = divmod(k, STEPS)
                        kt = i % TPB
                        if i == 0:
                            pe.wait_ge(sm["v_aug"], s + 1)
                        pe.wait_ge(sm["exp"], 4 * (k + 1))
                        if kt == 0 and k >= TPB:
                            pe.wait_ge(sm["o_out"], k // TPB)
                        for h in range(4):
                            m = nc.tensor.matmul(op[32 * h:32 * h + 32, :], va[:, s % 2, kt, h, :], pr[:, k % 2, h, :],
                                                 start=(kt == 0), stop=(kt == TPB - 1))
                        m.then_inc(sm["pv_mm"], 1)

                    def turn_output(m, splits):
                        pe.wait_ge(sm["o_out"], m + 1)
                        if splits >= 1:
                            pe.wait_ge(sm["m_neg"], splits)
                        if m >= 1:
                            pe.wait_ge(sm["o_done"], m)
                        for t in range(CPT):
                            x = nc.tensor.transpose(mi[:, t, :], osb[:, m % 2, t * P:(t + 1) * P], K.ident[:])
                        x.then_inc(sm["o_turned"], 1)

                    for k in range(STEPS * QUADS):
                        s, i = divmod(k, STEPS)
                        scores(k, 0)
                        scores(k, 1)
                        if k >= 1:
                            product(k - 1)
                        scores(k, 2)
                        scores(k, 3)
                        if i == TURN_MAX:
                            pe.wait_ge(sm[f"loaded{(s + 2) % 4}"], LOADS)
                        first_pass(pe, sm, 2 * k, *unit(s, 2 * i))
                        if i == TURN_MAX:
                            pe.wait_ge(sm["o_done"], 2 * s + 1)
                            turn_max(pe, sm, (s + 1) % 4, UNITS * s + REST)
                        first_pass(pe, sm, 2 * k + 1, *unit(s, 2 * i + 1))
                        if i % TPB == TURN_OUT and k >= TPB:
                            turn_output(k // TPB - 1, s)
                    product(STEPS * QUADS - 1)
                    turn_output(2 * QUADS - 1, QUADS)

                @block.scalar
                def _(act):
                    def output(m):
                        act.wait_ge(sm["pv_mm"], TPB * (m + 1))
                        if m >= 2:
                            act.wait_ge(sm["o_turned"], m - 1)
                        nc.scalar.copy(osb[:, m % 2, :], op[:]).then_inc(sm["o_out"], 1)

                    for k in range(STEPS * QUADS):
                        for h in range(4):
                            act.wait_ge(sm["s2_mm"], 4 * k + h + 1)
                            if h == 0 and k >= 2:
                                act.wait_ge(sm["pv_mm"], k - 1)
                            nc.scalar.activation(pr[:, k % 2, h, :], s2[(4 * k + h) % 2][:], ACT.Exp
                                                 ).then_inc(sm["exp"], 1)
                            if h == 1 and k % TPB == 0 and k >= TPB:
                                output(k // TPB - 1)
                    output(2 * QUADS - 1)

                @block.vector
                def _(dve):
                    v = nc.vector

                    def divide(m):
                        s, half = divmod(m, 2)
                        dve.wait_ge(sm["o_turned"], m + 1)
                        heads = mi[:].rearrange("p t (h c) -> p t h c", c=32)
                        v.reciprocal(ro[:, m % 2], heads[:, :, :, HD1]).then_inc(sm["o_rsum"], 1)
                        dve.wait_ge(sm["o_rsum"], m + 1)
                        v.tensor_tensor(
                            K.nat[:, bass.ds(b * TPB + half * CPT, CPT), s * 32:(s + 1) * 32]
                            .rearrange("p t (h d) -> p t h d", d=HD1),
                            heads[:, :, :, 0:HD1], bc(ro[:, m % 2], 3, HD1), ALU.mult).then_inc(sm["o_done"], 1)

                    for s in range(QUADS):
                        for u in range(UNITS):
                            ring, n = unit(s, u)
                            if n == 0 and s >= 1:
                                dve.wait_ge(sm["m_turned"], s)
                            reduce_max(dve, sm, UNITS * s + u, ring, n)
                            if u == 2 * TURN_MAX:
                                negate_max(dve, sm, s)
                            i, odd = divmod(u, 2)
                            if i % TPB == TURN_OUT + 1 and odd == 0 and 2 * s + i // TPB >= 1:
                                divide(2 * s + i // TPB - 1)
                    divide(2 * QUADS - 1)
            nc.all_engine_barrier(sems_to_clear=clear)


def project_stage(nc, K, name, w_in_ap, bias, residual):
    with ExitStack() as st:
        w = K.sb(name + "_w", [P, D], ctx=st)
        br = K.sb(name + "_b", [P, D], ctx=st)
        aT = K.sb(name + "_aT", [P, NCH, CH], ctx=st)
        tmp = K.sb(name + "_tmp", [P, 2, CPT, D], ctx=st)
        tp = [K.ps(f"{name}_tps{i}", [P, CPT, P], st) for i in range(4)]
        yp = [K.ps(f"{name}_yps{i}", [P, CPT, D], st) for i in range(4)]
        (w_in, turned, t_out, y_mm, y_out, y_b) = K.sems(st, 
            name, "w_in", "turned", "turned_out", "y_mm", "y_out", "y_biased")
        n_in = 1 + (bias is not None)
        with nc.Block() as block:
            @block.sync
            def _(sp):
                sp.dma_start(w[:], w_in_ap).then_inc(w_in, 16)
                if bias is not None:
                    sp.dma_start(br[:], bias.partition_broadcast(P)).then_inc(w_in, 16)
                sp.wait_ge(w_in, 16 * n_in)

            @block.tensor
            def _(pe):
                pe.wait_ge(w_in, 16 * n_in)
                for c in range(NCH + 1):
                    if c < NCH:
                        if c >= 4:
                            pe.wait_ge(t_out, c - 3)
                        for t in range(CPT):
                            m = nc.tensor.transpose(tp[c % 4][:, t, :], K.nat[:, c * CPT + t, :], K.ident[:])
                        m.then_inc(turned, 1)
                    if c >= 1:
                        k = c - 1
                        pe.wait_ge(t_out, k + 1)
                        if k >= 4:
                            pe.wait_ge(y_b, k - 3)
                        for t in range(CPT):
                            m = nc.tensor.matmul(yp[k % 4][:, t, :], aT[:, k, t * P:(t + 1) * P], w[:],
                                                 start=True, stop=True)
                        m.then_inc(y_mm, 1)

            @block.scalar
            def _(act):
                for c in range(NCH):
                    act.wait_ge(turned, c + 1)
                    nc.scalar.copy(aT[:, c, :], tp[c % 4][:].rearrange("p t d -> p (t d)")).then_inc(t_out, 1)

            @block.vector
            def _(dve):
                v = nc.vector
                if bias is not None:
                    dve.wait_ge(w_in, 16 * n_in)
                for c in range(NCH):
                    tiles = slice(c * CPT, (c + 1) * CPT)
                    dve.wait_ge(y_mm, c + 1)
                    if residual is not None:
                        v.tensor_tensor(residual[:, tiles, :], residual[:, tiles, :], yp[c % 4][:], ALU.add
                                        ).then_inc(y_b, 1)
                        continue
                    if c >= 2:
                        dve.wait_ge(y_out, 2 * (c - 1))
                    v.tensor_tensor(tmp[:, c % 2], yp[c % 4][:], bc(br[:], 1, CPT), ALU.add).then_inc(y_b, 1)
                    dve.wait_ge(y_b, c + 1)
                    v.tensor_tensor(tmp[:, c % 2], tmp[:, c % 2], bc(K.mod_rows[:, 1, c * CPT // TPB, GA, :], 1, CPT),
                                    ALU.mult).then_inc(y_out, 1)
                    dve.wait_ge(y_out, 2 * c + 1)
                    v.tensor_tensor(K.x[:, tiles, :], K.x[:, tiles, :], tmp[:, c % 2], ALU.add).then_inc(y_out, 1)


def cross_attention_stage(nc, K, A, res):
    QW, KW = H1 * HD1, KV2 * HD1
    pairs = [(s, t) for s in range(B) for t in range(s + 1)]
    first = [sum(range(s + 1)) for s in range(B)]
    NP = len(pairs)
    M = TPB * KV2
    R = H1 // KV2
    with ExitStack() as st:
        w = K.sb("x_wT", [P, QKV2], ctx=st)
        q = K.sb("x_q", [P, NT, QW], ctx=st)
        k = K.sb("x_k", [P, NT, KW], ctx=st)
        vv = K.sb("x_v", [P, NT, KW], ctx=st)
        pd = K.sb("x_prod", [P, 2, TPB, QW], ctx=st)
        sc = K.sb("x_scores", [P, NP, TPB * H1], ctx=st)
        mx = K.sb("x_max", [P, B, TPB * H1], ctx=st)
        sm = K.sb("x_sum", [P, B, TPB * H1], ctx=st)
        yp = [K.ps(f"x_ps{i}", [P, CH], st) for i in range(4)]
        (w_in, mm, qkv_out, pdone, sdone, smx, exped, nrm, pv, pool_o) = K.sems(st, 
            "cross", "w_in", "qkv_mm", "qkv_out", "product", "score", "softmax", "exp", "norm", "pv", "out")
        with nc.Block() as block:
            @block.sync
            def _(sp):
                sp.dma_start(w[:], A["L1_ffn_qkvT"]).then_inc(w_in, 16)
                sp.wait_ge(w_in, 16)

            @block.tensor
            def _(pe):
                pe.wait_ge(w_in, 16)
                for n in range(NT // 2):
                    if n >= 4:
                        pe.wait_ge(qkv_out, n - 3)
                    for i in range(2):
                        t = 2 * n + i
                        m = nc.tensor.matmul(yp[n % 4][:, i * QKV2:(i + 1) * QKV2], K.hT[:, t * P:(t + 1) * P], w[:],
                                             start=True, stop=True)
                    m.then_inc(mm, 1)

            @block.scalar
            def _(act):
                for n in range(NT // 2):
                    act.wait_ge(mm, n + 1)
                    y = yp[n % 4][:, 0:2 * QKV2].rearrange("p (t c) -> p t c", t=2)
                    t2 = slice(2 * n, 2 * n + 2)
                    nc.scalar.copy(q[:, t2, :], y[:, :, 0:QW])
                    nc.scalar.copy(k[:, t2, :], y[:, :, QW:QW + KW])
                    nc.scalar.copy(vv[:, t2, :], y[:, :, QW + KW:QKV2]).then_inc(qkv_out, 1)
                act.wait_ge(smx, 2 * NP)
                nc.scalar.activation(sc[:], sc[:], ACT.Exp, scale=HD1 ** -0.5).then_inc(exped, 1)

            def grouped(ap):
                return ap.rearrange("p t (g r d) -> p (t g) r d", r=R, d=HD1)

            def shared(ap):
                return bc(ap.rearrange("p t (g d) -> p (t g) d", d=HD1), 2, R)

            def tiles(s):
                return slice(s * TPB, (s + 1) * TPB)

            @block.vector
            def _(dve):
                v = nc.vector
                for n, (s, t) in enumerate(pairs):
                    dve.wait_ge(qkv_out, (max(s, t) + 1) * TPB // 2)
                    if n >= 2:
                        dve.wait_ge(sdone, n - 1)
                    v.tensor_tensor(grouped(pd[:, n % 2]), grouped(q[:, tiles(s), :]), shared(k[:, tiles(t), :]),
                                    ALU.mult).then_inc(pdone, 1)
                    dve.wait_ge(pdone, n + 1)
                    v.tensor_reduce(sc[:, n, :], pd[:, n % 2].rearrange("p t (h d) -> p (t h) d", d=HD1), AX.X,
                                    ALU.add).then_inc(sdone, 1)
                dve.wait_ge(sdone, NP)
                count = 0
                for s in range(B):
                    f = first[s]
                    v.tensor_copy(mx[:, s, :], sc[:, f, :]).then_inc(smx, 1)
                    count += 1
                    for t in range(1, s + 1):
                        dve.wait_ge(smx, count)
                        v.tensor_tensor(mx[:, s, :], mx[:, s, :], sc[:, f + t, :], ALU.max).then_inc(smx, 1)
                        count += 1
                    dve.wait_ge(smx, count)
                    if s == 0:
                        base = count
                for n, (s, t) in enumerate(pairs):
                    v.tensor_tensor(sc[:, n, :], sc[:, n, :], mx[:, s, :], ALU.subtract).then_inc(smx, 1)
                    count += 1
                assert count == 2 * NP
                dve.wait_ge(exped, 1)
                count = 0
                for s in range(B):
                    f = first[s]
                    v.tensor_copy(sm[:, s, :], sc[:, f, :]).then_inc(nrm, 1)
                    count += 1
                    for t in range(1, s + 1):
                        dve.wait_ge(nrm, count)
                        v.tensor_tensor(sm[:, s, :], sm[:, s, :], sc[:, f + t, :], ALU.add).then_inc(nrm, 1)
                        count += 1
                dve.wait_ge(nrm, count)
                v.reciprocal(mx[:], sm[:]).then_inc(nrm, 1)
                count += 1
                dve.wait_ge(nrm, count)
                for n, (s, t) in enumerate(pairs):
                    v.tensor_tensor(sc[:, n, :], sc[:, n, :], mx[:, s, :], ALU.mult).then_inc(nrm, 1)
                    count += 1
                dve.wait_ge(nrm, count)
                done = 0
                for n, (s, t) in enumerate(pairs):
                    weight = bc(sc[:, n, :].rearrange("p (m r) -> p m r", r=R), 3, HD1)
                    dst = K.nat[:, tiles(s), :] if t == 0 else pd[:, n % 2]
                    if t:
                        dve.wait_ge(pv, done)
                    v.tensor_tensor(grouped(dst), shared(vv[:, tiles(t), :]), weight, ALU.mult).then_inc(pv, 1)
                    done += 1
                    if t:
                        dve.wait_ge(pv, done)
                        o = K.nat[:, tiles(s), :]
                        v.tensor_tensor(o, o, pd[:, n % 2], ALU.add).then_inc(pv, 1)
                        done += 1


def output_stage(nc, K, out):
    with ExitStack() as st:
        (stored,) = K.sems(st, "out", "stored")
        with nc.Block() as block:
            @block.sync
            def _(sp):
                sp.dma_start(out.rearrange("b (t p) d -> p (b t) d", p=P), K.x[:]).then_inc(stored, 16)
                sp.wait_ge(stored, 16)


def build(nc, A, out, stages=99):
    with ExitStack() as ctx:
        K = Core(nc, ctx)
        K.win_sems = K.loop_sems(
            "win", "h_in", "proj_mm", "act_out", "q_out", "v_shift_even", "v_shift_odd", "score_mm", "biased", "exp",
            "rsum", "normed", "turned", "probsT_out", "pv_mm", "o_out", "wo_mm", "x_tmp")
        K.moe_sems = K.loop_sems("moe", "h_hi", "h_lo", "hidden_mm", "gelu", "hidden_hi", "hidden_lo", "weights_mm", "weights_out",
                                  "y_mm", "y_weighed", "y_summed", "x_out")
        K.att_sems = K.loop_sems("att1", *ATT_SEMS)
        K.x = K.sb("x", [P, NT, D])
        K.nat = K.sb("nat", [P, NT, D])
        K.hT = K.sb("hT", [P, B * T + CH])
        K.w = K.sb("expert_w", [P, NT, E])
        K.mod_cols = K.sb("mod_cols", [P, 2, 6, B])
        K.mod_rows = K.sb("mod_rows", [P, 2, B, 6, D])
        K.ident = K.sb("ident", [P, P])
        K.neghalf = K.sb("neghalf", [P, NT])

        def cols(layer, scale, shift):
            return (lambda b: K.mod_cols[:, layer, scale, b:b + 1], lambda b: K.mod_cols[:, layer, shift, b:b + 1])

        def rows(layer, scale, shift):
            return (lambda b: K.mod_rows[:, layer, b, scale, :], lambda b: K.mod_rows[:, layer, b, shift, :])

        modulation_stage(nc, K, A)
        if stages >= 1:
            norm_stage(nc, K, "n0a", K.x, to_T=cols(0, CA, SA))
            window_attention_stage(nc, K, A)
        if stages >= 2:
            norm_stage(nc, K, "n0b", K.x, rows=rows(0, CB, SB))
            with ExitStack() as st:
                aff = affine_columns(nc, K, A, "aff0", ("L0_ffn_gamma", "L0_ffn_beta"), st)
                norm_stage(nc, K, "n0c", K.nat, to_T=aff)
            with ExitStack() as st:
                M = Experts(K, A, "moe0", F0, A["L0_ffn_W1T"], A["L0_ffn_W2T"], A["L0_ffn_b1c"], st)
                routing_stage(nc, K, A, "rt0", A["L0_ffn_WgT"], A["L0_ffn_bg"], A["L0_ffn_b2"], True, M)
                expert_stage(nc, K, A, "moe0", M, ACT.Gelu, 0)
        if stages >= 3:
            norm_stage(nc, K, "n1a", K.x, to_T=cols(1, CA, SA))
            full_attention_stage(nc, K, A)
            project_stage(nc, K, "wo1", A["L1_attn_WoT"], A["L1_attn_bo"], None)
        if stages >= 4:
            with ExitStack() as st:
                res = K.sb("res", [P, NT, D], ctx=st)
                norm_stage(nc, K, "n1b", K.x, rows=rows(1, CB, SB))
                aff1 = affine_columns(nc, K, A, "aff1", ("L1_ffn_ln1_weight", "L1_ffn_ln1_bias"), st)
                aff2 = affine_columns(nc, K, A, "aff2", ("L1_ffn_ln2_weight", "L1_ffn_ln2_bias"), st)
                norm_stage(nc, K, "n1c", K.nat, to_T=aff1)
                copy_stage(nc, K, res, K.nat)
                cross_attention_stage(nc, K, A, res)
                project_stage(nc, K, "pj1", A["L1_ffn_projT"], None, res)
                copy_stage(nc, K, K.nat, res)
                norm_stage(nc, K, "n1d", K.nat, to_T=aff2)
            with ExitStack() as st:
                M = Experts(K, A, "moe1", F1, A["L1_ffn_moe_w1"], A["L1_ffn_moe_w2"], None, st)
                routing_stage(nc, K, A, "rt1", A["L1_ffn_routerT"], None, None, False, M)
                expert_stage(nc, K, A, "moe1", M, ACT.Gelu_apprx_tanh, 1)
        output_stage(nc, K, out)


def affine_columns(nc, K, A, name, arrays, st):
    c = K.sb(name, [P, 2], ctx=st)
    (c_in,) = K.sems(st, name, "c_in")
    with nc.Block() as block:
        @block.sync
        def _(sp):
            for i, a in enumerate(arrays):
                sp.dma_start(c[:, i:i + 1], A[a].rearrange("(p a) -> p a", a=1)).then_inc(c_in, 16)
            sp.wait_ge(c_in, 32)
    return (lambda b: c[:, 0:1], lambda b: c[:, 1:2])


def copy_stage(nc, K, dst, src):
    with nc.Block() as block:
        @block.vector
        def _(dve):
            nc.vector.tensor_copy(dst[:, 0:NT // 2, :], src[:, 0:NT // 2, :])

        @block.scalar
        def _(act):
            nc.scalar.copy(dst[:, NT // 2:NT, :], src[:, NT // 2:NT, :])


def constants():
    slopes = np.array([2.0 ** (-0.5 * (i + 1)) for i in range(H0)])
    r = np.arange(BLK)[:, None]
    c = np.arange(P)[None, :]
    dist = c - BLK - r
    neg = np.empty((2, BLK, PAIRS, 2, P), np.float32)
    for h in range(H0):
        for v in range(2):
            ok = (dist <= 0) & (dist >= -WIN) & ((c >= BLK) | (v == 0))
            neg[h % 2, :, h // 2, v, :] = np.where(ok, -slopes[h] * dist, 1e30)
    lower = np.broadcast_to((np.arange(E)[None, :] < np.arange(E)[:, None]).astype(np.float32).reshape(1, -1), (P, E * E))
    select = np.zeros((KROWS, E, P), np.float32)
    for row in range(3 * E):
        select[row, row % E, :] = 1.0
    return {"identity": np.eye(P, dtype=np.float32), "neg_bias": neg.reshape(P, PAIRS, 2, P),
            "lower": np.ascontiguousarray(lower), "select": select.reshape(KROWS, E * P)}


AS_IS = ("L0_attn_x", "L0_attn_wq", "L0_attn_wk", "L0_ffn_gamma", "L0_ffn_beta",
         "L0_ffn_bg", "L0_ffn_b2", "L0_wmod", "L1_attn_bq", "L1_attn_bk", "L1_attn_bv", "L1_attn_bo",
         "L1_ffn_ln1_weight", "L1_ffn_ln1_bias", "L1_ffn_ln2_weight", "L1_ffn_ln2_bias", "L1_ffn_moe_w1",
         "L1_ffn_moe_w2", "L1_wmod")
TURNED = {"L0_attn_wqT": "L0_attn_wq", "L0_attn_wkT": "L0_attn_wk", "L0_attn_wvT": "L0_attn_wv",
          "L0_attn_woT": "L0_attn_wo", "L0_ffn_WgT": "L0_ffn_Wg", "L0_ffn_W1T": "L0_ffn_W1", "L0_ffn_W2T": "L0_ffn_W2",
          "L0_c": "L0_c", "L1_c": "L1_c", "L1_attn_WqT": "L1_attn_Wq", "L1_attn_WkT": "L1_attn_Wk",
          "L1_attn_WvT": "L1_attn_Wv", "L1_attn_WoT": "L1_attn_Wo", "L1_ffn_qkvT": "L1_ffn_qkv_weight",
          "L1_ffn_projT": "L1_ffn_proj_weight", "L1_ffn_routerT": "L1_ffn_router_weight"}


def kernel(**inputs):
    import numpy as _np
    import concourse.bacc as _bacc
    from concourse import mybir as _mybir
    from concourse.bass_utils import run_bass_kernel_spmd as _run

    data = {n: _np.asarray(inputs[n]) for n in AS_IS}
    for n, of in TURNED.items():
        data[n] = _np.swapaxes(_np.asarray(inputs[of]), -1, -2)
    data["L0_ffn_b1c"] = _np.asarray(inputs["L0_ffn_b1"]).reshape(E * F0 // P, P).T
    for n in "qk":
        data[f"L0_attn_{n}_norm_c"] = _np.asarray(inputs[f"L0_attn_{n}_norm_w"]).reshape(PAIRS, P).T
    data.update(constants())
    nc = _bacc.Bacc("TRN2", target_bir_lowering=False, num_devices=1)
    arrays, A = {}, {}
    for n, a in data.items():
        a = _np.ascontiguousarray(a)
        arrays[f"in_{n}"] = a
        A[n] = nc.dram_tensor(f"in_{n}", a.shape, _mybir.dt.from_np(a.dtype), kind="ExternalInput").ap()
    out = nc.dram_tensor("out_x", (B, T, D), F32, kind="ExternalOutput").ap()
    build(nc, A, out)
    r = _run(nc, [arrays], core_ids=[0])
    return r.results[0]["out_x"]
```

```python
from contextlib import ExitStack

import numpy as np

import concourse.bass as bass
from concourse import mybir

F32 = mybir.dt.float32
BF16 = mybir.dt.bfloat16
F32R = mybir.dt.float32r
ALU = mybir.AluOpType
ACT = mybir.ActivationFunctionType
AX = mybir.AxisListType

P = 128
B, T, D = 4, 1024, 128
TPB = T // P
NT = B * TPB
CH = 512
NCH = B * T // CH
CPT = CH // P
LN_EPS = 1e-5
GATE_MIN = 0.25

H0, HD0, WIN = 16, 64, 64
PAIRS = H0 // 2
BLK = 64
NBLK = T // BLK
RMS_EPS = 1e-6
E = 8
F0, F1 = 512, 256
TOPK_EPS = 1e-8
H1, HD1 = 16, 8
QUADS = H1 // 4
KV2 = 4
QKV2 = H1 * HD1 + 2 * KV2 * HD1
Q_PART = (0, 0, 1, 1, 0, 2)
K_PART = (0, 1, 0, 1, 2, 0)
MROW = len(Q_PART) * HD1
KROWS = 96

SA, CA, GA, SB, CB, GB = range(6)


def bc(ap, axis, n):
    a = ap.unsqueeze(axis)
    shape = list(a.shape)
    shape[axis] = n
    return a.broadcast_to(shape)


class Core:

    def __init__(self, nc, ctx):
        self.nc, self.ctx = nc, ctx

    def sb(self, name, shape, dt=F32, ctx=None):
        return (ctx or self.ctx).enter_context(self.nc.sbuf_tensor(name, shape, dt))

    def ps(self, name, shape, ctx):
        return ctx.enter_context(self.nc.psum_tensor(name, shape, F32))

    def sems(self, ctx, prefix, *names):
        s = [self.nc.alloc_semaphore(f"{prefix}_{n}") for n in names]
        ctx.callback(self.clear, s)
        return s

    def clear(self, sems):
        self.nc.clear_and_free_semaphores(sems)
        self.nc.all_engine_barrier()

    def loop_sems(self, prefix, *names):
        s = [self.nc.alloc_semaphore(f"{prefix}_{n}") for n in names]
        numbers = [x.num for x in s]
        assert numbers == list(range(numbers[0], numbers[0] + len(s)))
        return s, range(numbers[0], numbers[0] + len(s))


class Norm:

    def __init__(self, nc, K, name, src, hat, st):
        self.nc, self.K, self.src, self.hat = nc, K, src, hat
        self.stats = K.sb(name + "_stats", [P, NT, 6], ctx=st)
        self.mv = K.sb(name + "_mv", [P, NT, 2], ctx=st)
        self.ve = K.sb(name + "_ve", [P, NT], ctx=st)
        self.rstd = K.sb(name + "_rstd", [P, NT], ctx=st)
        self.shift = K.sb(name + "_shift", [P, NT], ctx=st)
        (self.st_done, self.mv_done, self.rs_done, self.hat_even, self.hat_odd, self.turned, self.turn_read) = K.sems(
            st, name, "stats", "meanvar", "rstd", "hat_even", "hat_odd", "turned", "turn_read")

    def statistics(self, dve, b):
        v = self.nc.vector
        for t in range(b * TPB, (b + 1) * TPB):
            v.bn_stats(self.stats[:, t, :], self.src[:, t, :]).then_inc(self.st_done, 1)
        for t in range(b * TPB, (b + 1) * TPB):
            dve.wait_ge(self.st_done, t + 1)
            v.bn_aggr(self.mv[:, t, :], self.stats[:, t, :]).then_inc(self.mv_done, 1)

    def deviation(self, pool, b):
        g, s = self.nc.gpsimd, slice(b * TPB, (b + 1) * TPB)
        pool.wait_ge(self.mv_done, (b + 1) * TPB)
        g.tensor_scalar(self.ve[:, s], self.mv[:, s, 1], LN_EPS, None, ALU.add).then_inc(self.rs_done, 1)
        pool.wait_ge(self.rs_done, 4 * b + 1)
        g.tensor_tensor(self.rstd[:, s], self.ve[:, s], self.K.neghalf[:, s], ALU.pow).then_inc(self.rs_done, 1)
        pool.wait_ge(self.rs_done, 4 * b + 2)
        g.tensor_tensor(self.shift[:, s], self.mv[:, s, 0], self.rstd[:, s], ALU.mult).then_inc(self.rs_done, 1)
        pool.wait_ge(self.rs_done, 4 * b + 3)
        g.tensor_scalar(self.shift[:, s], self.shift[:, s], -1.0, None, ALU.mult).then_inc(self.rs_done, 1)

    def normalised_even(self, act, b):
        act.wait_ge(self.rs_done, 4 * (b + 1))
        for t in range(b * TPB, (b + 1) * TPB, 2):
            self.nc.scalar.activation(self.hat[:, t, :], self.src[:, t, :], ACT.Identity, scale=self.rstd[:, t:t + 1],
                                      bias=self.shift[:, t:t + 1]).then_inc(self.hat_even, 1)

    def normalised_odd(self, dve, b):
        dve.wait_ge(self.rs_done, 4 * (b + 1))
        for t in range(b * TPB + 1, (b + 1) * TPB, 2):
            self.nc.vector.tensor_scalar(self.hat[:, t, :], self.src[:, t, :], self.rstd[:, t:t + 1],
                                         self.shift[:, t:t + 1], ALU.mult, ALU.add).then_inc(self.hat_odd, 1)

    def wait_normalised(self, eng, tiles):
        eng.wait_ge(self.hat_even, tiles // 2)
        eng.wait_ge(self.hat_odd, tiles // 2)

    def turn(self, pe, banks, b):
        for c in range(2 * b, 2 * b + 2):
            self.wait_normalised(pe, (c + 1) * CPT)
            if c >= len(banks):
                pe.wait_ge(self.turn_read, c - len(banks) + 1)
            for t in range(CPT):
                m = self.nc.tensor.transpose(banks[c % len(banks)][:, t, :], self.hat[:, c * CPT + t, :],
                                             self.K.ident[:])
            m.then_inc(self.turned, 1)

    def affine(self, act, banks, b, scale, bias):
        for c in range(2 * b, 2 * b + 2):
            act.wait_ge(self.turned, c + 1)
            self.nc.scalar.activation(self.K.hT[:, c * CH:(c + 1) * CH],
                                      banks[c % len(banks)][:].rearrange("p t d -> p (t d)"),
                                      ACT.Identity, bias=bias, scale=scale).then_inc(self.turn_read, 1)


def double_norm_stage(nc, K, A, name, layer, scale, shift, arrays, M=None, before=None):
    with ExitStack() as st:
        hat = K.sb(name + "_hat", [P, NT, D], ctx=st)
        hat2 = K.sb(name + "_hat2", [P, NT, D], ctx=st)
        aff = K.sb(name + "_affine", [P, 2], ctx=st)
        if before:
            before.buffers(st)
        N1 = Norm(nc, K, name + "a", K.x, hat, st)
        N2 = Norm(nc, K, name + "b", K.nat, hat2, st)
        banks = [K.ps(f"{name}_ps{i}", [P, CPT, P], st) for i in range(4)]
        (aff_in, scaled, shifted) = K.sems(st, name, "affine_in", "scaled", "shifted")
        with nc.Block() as block:
            @block.sync
            def _(sp):
                for i, a in enumerate(arrays):
                    sp.dma_start(aff[:, i:i + 1], A[a].rearrange("(p a) -> p a", a=1)).then_inc(aff_in, 16)
                sp.wait_ge(aff_in, 32)
                if M:
                    M.load_router(sp, A)

            @block.vector
            def _(dve):
                for b in range(B):
                    if before:
                        before.add(dve, b)
                        before.wait_added(dve, b)
                    N1.statistics(dve, b)
                for b in range(B + 3):
                    if b < B:
                        N1.normalised_odd(dve, b)
                        N1.wait_normalised(dve, (b + 1) * TPB)
                        h = hat[:, b * TPB:(b + 1) * TPB, :]
                        nc.vector.tensor_tensor(h, h, bc(K.mod_rows[:, layer, b, scale, :], 1, TPB), ALU.mult
                                                ).then_inc(scaled, 1)
                    if 2 <= b < B + 2:
                        dve.wait_ge(shifted, b - 1)
                        N2.statistics(dve, b - 2)
                    if b >= 3:
                        N2.normalised_odd(dve, b - 3)

            @block.gpsimd
            def _(pool):
                for b in range(B):
                    N1.deviation(pool, b)
                for b in range(B + 1):
                    if b < B:
                        pool.wait_ge(scaled, b + 1)
                        nc.gpsimd.tensor_tensor(K.nat[:, b * TPB:(b + 1) * TPB, :], hat[:, b * TPB:(b + 1) * TPB, :],
                                                bc(K.mod_rows[:, layer, b, shift, :], 1, TPB), ALU.add
                                                ).then_inc(shifted, 1)
                    if b >= 1:
                        N2.deviation(pool, b - 1)

            @block.tensor
            def _(pe):
                if before:
                    before.products(pe)
                for b in range(B):
                    N2.turn(pe, banks, b)
                    if M and b >= 1:
                        M.logits(nc, K, pe, N2, b - 1)
                if M:
                    M.logits(nc, K, pe, N2, B - 1)

            @block.scalar
            def _(act):
                act.wait_ge(aff_in, 32)
                if before:
                    before.turned_out(act)
                for b in range(B):
                    N1.normalised_even(act, b)
                for b in range(B + 1):
                    if b < B:
                        N2.normalised_even(act, b)
                    if b >= 1:
                        N2.affine(act, banks, b - 1, aff[:, 0:1], aff[:, 1:2])


def last_norm_stage(nc, K, A, name, arrays, M):
    with ExitStack() as st:
        hat = K.sb(name + "_hat", [P, NT, D], ctx=st)
        aff = K.sb(name + "_affine", [P, 2], ctx=st)
        N = Norm(nc, K, name, K.nat, hat, st)
        banks = [K.ps(f"{name}_ps{i}", [P, CPT, P], st) for i in range(4)]
        (aff_in,) = K.sems(st, name + "w", "affine_in")
        with nc.Block() as block:
            @block.sync
            def _(sp):
                for i, a in enumerate(arrays):
                    sp.dma_start(aff[:, i:i + 1], A[a].rearrange("(p a) -> p a", a=1)).then_inc(aff_in, 16)
                sp.wait_ge(aff_in, 32)
                M.load_router(sp, A)

            @block.vector
            def _(dve):
                for b in range(B):
                    N.statistics(dve, b)
                for b in range(B):
                    N.normalised_odd(dve, b)

            @block.gpsimd
            def _(pool):
                for b in range(B):
                    N.deviation(pool, b)

            @block.tensor
            def _(pe):
                for b in range(B):
                    N.turn(pe, banks, b)
                    if b >= 1:
                        M.logits(nc, K, pe, N, b - 1)
                M.logits(nc, K, pe, N, B - 1)

            @block.scalar
            def _(act):
                act.wait_ge(aff_in, 32)
                for b in range(B + 1):
                    if b < B:
                        N.normalised_even(act, b)
                    if b >= 1:
                        N.affine(act, banks, b - 1, aff[:, 0:1], aff[:, 1:2])


def start_stage(nc, K, A, gram):
    with ExitStack() as st:
        cT = K.sb("cT", [P, 2, B], ctx=st)
        wmod = K.sb("wmod", [P, 2, 6 * D], ctx=st)
        ex = K.sb("silu_exp", [P, 2, B], ctx=st)
        den = K.sb("silu_den", [P, 2, B], ctx=st)
        rec = K.sb("silu_rec", [P, 2, B], ctx=st)
        sil = K.sb("silu", [P, 2, B], ctx=st)
        silb = K.sb("silu_rows", [P, 2, B, P], ctx=st)
        csgn = K.sb("gate_sign_cols", [P, 2, B], ctx=st)
        cmag = K.sb("gate_size_cols", [P, 2, B], ctx=st)
        hat = K.sb("n0a_hat", [P, NT, D], ctx=st)
        N = Norm(nc, K, "n0a", K.x, hat, st)
        wn = K.sb("w_nat", [P, 2, PAIRS, D], ctx=st)
        colp = K.ps("mod_cols_ps", [P, 2, 6, B], st)
        gp = K.ps("gram_ps", [P, 2, D], st)
        rowp = [K.ps(f"mod_rows_ps{i}", [P, CH], st) for i in range(2)]
        banks = [K.ps(f"n0a_ps{i}", [P, CPT, P], st) for i in range(4)]
        (c_in, wn_in, e_done, chain, cols_mm, cols_out, scales, const_set, rows_mm, rows_out0, rows_out1, g_mm,
         *x_in) = K.sems(
            st, "start", "c_in", "wn_in", "exp", "silu", "cols_mm", "cols_out", "scales", "const", "rows_mm",
            "rows_out0", "rows_out1", "gram_mm", *(f"x_in{b}" for b in range(B)), "ident_in")
        rows_out = (rows_out0, rows_out1)
        half = 3 * D

        def rows_product(pe, n):
            if n >= 2:
                m = n - 1
                pe.wait_ge(rows_out[m > 2 * B], m if m <= 2 * B else m - 2 * B)
            l, b, j = n // (2 * B), n // 2 % B, n % 2
            nc.tensor.matmul(rowp[n % 2][:, 0:half], silb[:, l, b, :], wmod[:, l, j * half:(j + 1) * half],
                             start=True, stop=True).then_inc(rows_mm, 1)

        def rows_copy(eng, copy, n):
            eng.wait_ge(rows_mm, n + 1)
            l, b, j = n // (2 * B), n // 2 % B, n % 2
            copy(K.mod_rows[:, l, b, 3 * j:3 * j + 3, :],
                 rowp[n % 2][:, 0:half].rearrange("p (c d) -> p c d", c=3)).then_inc(rows_out[l], 1)

        with nc.Block() as block:
            @block.sync
            def _(sp):
                for i, (c, w) in enumerate((("L0_c", "L0_wmod"), ("L1_c", "L1_wmod"))):
                    sp.dma_start(cT[:, i, :], A[c]).then_inc(c_in, 16)
                    sp.dma_start(wmod[:, i, :], A[w]).then_inc(c_in, 16)
                for b in range(B):
                    src = A["L0_attn_x"][b].rearrange("(t p) d -> p t d", p=P)
                    sp.dma_start(K.x[:, b * TPB:(b + 1) * TPB, :], src).then_inc(x_in[b], 16)
                sp.dma_start(K.ident[:], A["identity"]).then_inc(x_in[B], 16)
                for i, w in enumerate(("L0_attn_wq", "L0_attn_wk")):
                    sp.dma_start(wn[:, i], A[w].rearrange("(c p) d -> p c d", p=P)).then_inc(wn_in, 16)

            @block.tensor
            def _(pe):
                pe.wait_ge(chain, 3)
                pe.wait_ge(c_in, 64)
                for l in range(2):
                    for c in range(6):
                        m = nc.tensor.matmul(colp[:, l, c, :], wmod[:, l, c * D:(c + 1) * D], sil[:, l, :],
                                             start=True, stop=True)
                m.then_inc(cols_mm, 1)
                pe.wait_ge(chain, 4)
                for n in range(2 * B):
                    rows_product(pe, n)
                pe.wait_ge(x_in[B], 16)
                for b in range(B):
                    N.turn(pe, banks, b)
                pe.wait_ge(wn_in, 32)
                for i in range(2):
                    for c in range(PAIRS):
                        m = nc.tensor.matmul(gp[:, i, :], wn[:, i, c, :], wn[:, i, c, :],
                                             start=(c == 0), stop=(c == PAIRS - 1))
                m.then_inc(g_mm, 1)
                for n in range(2 * B, 4 * B):
                    rows_product(pe, n)

            @block.scalar
            def _(act):
                act.wait_ge(c_in, 64)
                nc.scalar.activation(ex[:], cT[:], ACT.Exp, scale=-1.0).then_inc(e_done, 1)
                act.wait_ge(cols_mm, 1)
                nc.scalar.copy(K.mod_cols[:], colp[:]).then_inc(cols_out, 1)
                for n in range(2 * B):
                    rows_copy(act, nc.scalar.copy, n)
                act.wait_ge(scales, 1)
                for b in range(B + 1):
                    if b < B:
                        N.normalised_even(act, b)
                    if b >= 1:
                        N.affine(act, banks, b - 1, K.mod_cols[:, 0, CA, b - 1:b], K.mod_cols[:, 0, SA, b - 1:b])
                act.wait_ge(g_mm, 1)
                nc.scalar.copy(gram[:], gp[:])

            @block.gpsimd
            def _(pool):
                nc.gpsimd.memset(K.neghalf[:], -0.5).then_inc(const_set, 1)
                pool.wait_ge(const_set, 1)
                for b in range(B):
                    N.deviation(pool, b)

            @block.vector
            def _(dve):
                v = nc.vector
                dve.wait_ge(e_done, 1)
                v.tensor_scalar(den[:], ex[:], 1.0, None, ALU.add).then_inc(chain, 1)
                dve.wait_ge(chain, 1)
                v.reciprocal(rec[:], den[:]).then_inc(chain, 1)
                dve.wait_ge(chain, 2)
                v.tensor_tensor(sil[:], cT[:], rec[:], ALU.mult).then_inc(chain, 1)
                dve.wait_ge(chain, 3)
                v.tensor_copy(silb[:], bc(sil[:], 3, P)).then_inc(chain, 1)
                dve.wait_ge(x_in[0], 16)
                N.statistics(dve, 0)
                dve.wait_ge(cols_out, 1)
                cols = K.mod_cols[:].rearrange("p l (h c) b -> p l h c b", h=2)
                v.tensor_scalar(cols[:, :, :, CA, :], cols[:, :, :, CA, :], 1.0, None, ALU.add).then_inc(chain, 1)
                g = K.mod_cols[:, :, GB, :]
                v.tensor_scalar(csgn[:], g, 0.0, 2.0, ALU.is_ge, ALU.mult).then_inc(chain, 1)
                v.scalar_tensor_tensor(out=cmag[:], in0=g, scalar=-1.0, in1=g, op0=ALU.mult, op1=ALU.max
                                       ).then_inc(chain, 1)
                dve.wait_ge(chain, 7)
                v.tensor_scalar(csgn[:], csgn[:], 1.0, None, ALU.subtract).then_inc(chain, 1)
                dve.wait_ge(chain, 8)
                v.scalar_tensor_tensor(out=g, in0=cmag[:], scalar=GATE_MIN, in1=csgn[:], op0=ALU.max, op1=ALU.mult
                                       ).then_inc(scales, 1)
                for b in range(1, B):
                    dve.wait_ge(x_in[b], 16)
                    N.statistics(dve, b)
                for b in range(B):
                    N.normalised_odd(dve, b)
                for n in range(2 * B, 4 * B):
                    rows_copy(dve, v.tensor_copy, n)


def gate_rows_step(nc, K, dve, n, sgn, mag, done):
    v = nc.vector
    g = K.mod_rows[:, n // 8, :, (GA, GB)[n // 4 % 2], :]
    if n >= 1:
        dve.wait_ge(done, n)
    if n % 4 == 0:
        r = v.tensor_scalar(sgn[:], g, 0.0, 2.0, ALU.is_ge, ALU.mult)
    elif n % 4 == 1:
        r = v.tensor_scalar(sgn[:], sgn[:], 1.0, None, ALU.subtract)
    elif n % 4 == 2:
        r = v.scalar_tensor_tensor(out=mag[:], in0=g, scalar=-1.0, in1=g, op0=ALU.mult, op1=ALU.max)
    else:
        r = v.scalar_tensor_tensor(out=g, in0=mag[:], scalar=GATE_MIN, in1=sgn[:], op0=ALU.max, op1=ALU.mult)
    r.then_inc(done, 1)


def rms_stage(nc, K, gram, hq, hk, load_weights, fill, scale_q):
    with ExitStack() as s2:
        units = [(c, i) for c in range(NCH) for i in range(2)]
        U = len(units)
        z = K.sb("z", [P, 2, CH], ctx=s2)
        mean = K.sb("mean_columns", [P, U, U], ctx=s2)
        spread = K.sb("spread", [U, U, P], F32R, ctx=s2)
        ms = K.sb("mean_square", [U, CH], ctx=s2)
        root = K.sb("root", [U, CH], ctx=s2)
        rr = K.sb("rrms", [U, CH], ctx=s2)
        rp = [K.sb(f"rrms_{part}", [U, CH], F32R, ctx=s2) for part in ("hi", "lo")]
        up = [K.ps(f"u_ps{i}", [P, CH], s2) for i in range(2)]
        sq = K.ps("mean_square_ps", [P, CH], s2)
        bp = [K.ps(f"rrms_ps{i}", [P, CH], s2) for i in range(4)]
        sgn = K.sb("gate_sign", [P, B, D], ctx=s2)
        mag = K.sb("gate_size", [P, B, D], ctx=s2)
        (gated, scaled_rows, cst, u_mm, z_done, s_mm, dve_s, root_done, b_mm, scaled) = K.sems(
            s2, "rms", "gated", "scaled_rows", "const", "u_mm", "z", "sum_mm", "dve", "root", "spread_mm",
            "scaled")
        with nc.Block() as block:
            @block.sync
            def _(sp):
                load_weights(sp)

            @block.gpsimd
            def _(pool):
                g = nc.gpsimd
                fill(pool)
                for n in range(4):
                    r = K.mod_rows[:, n // 2, :, (CA, CB)[n % 2], :]
                    g.tensor_scalar(r, r, 1.0, None, ALU.add).then_inc(scaled_rows, 1)
                    pool.wait_ge(scaled_rows, n + 1)

            @block.tensor
            def _(pe):
                for n in range(U + 1):
                    if n < U:
                        c, i = units[n]
                        if n >= 2:
                            pe.wait_ge(z_done, n - 1)
                        nc.tensor.matmul(up[n % 2][:], gram[:, i, :], K.hT[:, c * CH:(c + 1) * CH],
                                         start=True, stop=True).then_inc(u_mm, 1)
                    if n == 1:
                        pe.wait_ge(cst, 3)
                    if n >= 1:
                        pe.wait_ge(z_done, n)
                        nc.tensor.matmul(sq[0:U, :], mean[:, n - 1, :], z[:, (n - 1) % 2, :],
                                         start=(n == 1), stop=(n == U)).then_inc(s_mm, 1)
                pe.wait_ge(dve_s, 4)
                for n in range(U):
                    if n >= 4:
                        pe.wait_ge(scaled, n - 3)
                    nc.tensor.matmul(bp[n % 4][:], spread[:, n, :], rp[0][:], start=True, stop=False)
                    nc.tensor.matmul(bp[n % 4][:], spread[:, n, :], rp[1][:], start=False, stop=True
                                     ).then_inc(b_mm, 1)

            @block.scalar
            def _(act):
                act.wait_ge(dve_s, 1)
                nc.scalar.activation(root[:], ms[:], ACT.Sqrt).then_inc(root_done, 1)

            @block.vector
            def _(dve):
                v = nc.vector
                flat = mean[:].rearrange("p a b -> p (a b)")
                v.memset(flat, 0.0).then_inc(cst, 1)
                dve.wait_ge(cst, 1)
                v.memset(flat[:, ::U + 1], 1.0 / (H0 * HD0)).then_inc(cst, 1)
                v.tensor_copy(spread[:], bc(K.ident[0:U, 0:U], 2, P)).then_inc(cst, 1)
                for n, (c, i) in enumerate(units):
                    dve.wait_ge(u_mm, n + 1)
                    if n >= 2:
                        dve.wait_ge(s_mm, n - 1)
                    v.tensor_tensor(z[:, n % 2, :], up[n % 2][:], K.hT[:, c * CH:(c + 1) * CH],
                                    ALU.mult).then_inc(z_done, 1)
                    gate_rows_step(nc, K, dve, n, sgn, mag, gated)
                dve.wait_ge(s_mm, U)
                v.tensor_scalar(ms[:], sq[0:U, :], 0.0, RMS_EPS, ALU.max, ALU.add).then_inc(dve_s, 1)
                dve.wait_ge(root_done, 1)
                v.reciprocal(rr[:], root[:]).then_inc(dve_s, 1)
                dve.wait_ge(dve_s, 2)
                v.tensor_copy(rp[0][:], rr[:]).then_inc(dve_s, 1)
                dve.wait_ge(dve_s, 3)
                v.tensor_tensor(rp[1][:], rr[:], rp[0][:].bitcast(F32), ALU.subtract).then_inc(dve_s, 1)
                for n, (c, i) in enumerate(units):
                    dve.wait_ge(b_mm, n + 1)
                    v.tensor_tensor((hq, hk)[i][:, c * CH:(c + 1) * CH], K.hT[:, c * CH:(c + 1) * CH], bp[n % 4][:],
                                    ALU.mult).then_inc(scaled, 1)
                scale_q(dve)


def window_attention_stage(nc, K, A, gram):
    with ExitStack() as st:
        hq = K.sb("hq", [P, B * T], ctx=st)
        hk = K.sb("hk", [P, B * T], ctx=st)
        wq = K.sb("wqT", [P, PAIRS, P], ctx=st)
        wk = K.sb("wkT", [P, PAIRS, P], ctx=st)
        wv = K.sb("wvT", [P, PAIRS, P], ctx=st)
        wo = K.sb("woT", [P, PAIRS, D], ctx=st)
        nbias = K.sb("nbias", [P, PAIRS, 2, P], ctx=st)
        qn = K.sb("qn", [P, 2, PAIRS], ctx=st)
        qs = K.sb("qscale", [P, PAIRS], ctx=st)
        hb = K.nat[:, 0:TPB, :].rearrange("p t d -> p (t d)")
        qbd = K.sb("q_bd", [P, 2, NBLK, P], ctx=st)
        kk = K.sb("k_pad", [P, 2, BLK + T], ctx=st)
        vs = K.sb("v_shift", [P, 2, TPB, P], ctx=st)
        (w_in, filled) = K.sems(st, "win0", "w_in", "filled")

        def load_weights(sp):
            for dst, w in ((wq, "L0_attn_wqT"), (wk, "L0_attn_wkT"), (wv, "L0_attn_wvT")):
                sp.dma_start(dst[:].rearrange("p c o -> p (c o)"), A[w]).then_inc(w_in, 16)
            sp.dma_start(wo[:], A["L0_attn_woT"].rearrange("(c p) d -> p c d", p=P)).then_inc(w_in, 16)
            sp.dma_start(nbias[:], A["neg_bias"]).then_inc(w_in, 16)
            sp.dma_start(qn[:, 0, :], A["L0_attn_q_norm_c"]).then_inc(w_in, 16)
            sp.dma_start(qn[:, 1, :], A["L0_attn_k_norm_c"]).then_inc(w_in, 16)
            sp.wait_ge(w_in, 7 * 16)

        def fill(pool):
            for n, dst in enumerate((qbd[:].rearrange("p a b c -> p (a b c)"), kk[:, :, 0:BLK], vs[0:BLK, :, 0, :])):
                nc.gpsimd.memset(dst, 0.0).then_inc(filled, 1)
                pool.wait_ge(filled, n + 1)

        def scale_q(dve):
            dve.wait_ge(w_in, 7 * 16)
            nc.vector.scalar_tensor_tensor(out=qs[:], in0=qn[:, 0, :], scalar=-HD0 ** -0.5, in1=qn[:, 1, :],
                                           op0=ALU.mult, op1=ALU.mult)

        rms_stage(nc, K, gram, hq, hk, load_weights, fill, scale_q)
        vv = K.sb("v_tiles", [P, 2, TPB, P], ctx=st)
        sb_ = K.sb("s_biased", [P, 4, 4, P], ctx=st)
        mn = K.sb("s_min", [P, 4, 4], ctx=st)
        pr = K.sb("probs", [P, 4, 4, P], ctx=st)
        sm = K.sb("p_sum", [P, 4, 4], ctx=st)
        ri = K.sb("p_rsum", [P, 4, 4], ctx=st)
        pt = K.sb("probsT", [P, 2, 4, P], ctx=st)
        oT = K.sb("oT", [P, 2, T], ctx=st)
        wog = K.sb("woT_gated", [P, PAIRS, D], ctx=st)
        pj = [K.ps(f"proj_ps{i}", [P, CH], st) for i in range(2)]
        sp_ = [K.ps(f"score_ps{i}", [P, 4, P], st) for i in range(2)]
        tp = K.ps("probsT_ps", [P, 4, P], st)
        op = K.ps("o_ps", [P, 4, BLK], st)
        wp = [K.ps(f"wo_ps{i}", [P, CPT, D], st) for i in range(2)]
        ((h_in, p_mm, a_out, q_out, v_sh0, v_sh1, s_mm, biased, exped, rsum, normed, turned, pt_out, pv_mm, o_out,
          wo_mm, wo_gated), clear) = K.win_sems
        v_sh = (v_sh0, v_sh1)
        GRP = NBLK // 4
        G = PAIRS * GRP
        units = [(h, u) for h in range(PAIRS) for u in range(6)]

        def unit_steps(g):
            h = g // GRP + 1
            if h >= PAIRS or g >= G:
                return []
            return [6 * h + u for u in ((0, 1), (2, 3), (4,), (5,))[g % GRP]]

        with nc.Fori(0, B) as b:
            with nc.Block() as block:
                @block.tensor
                def _(pe):
                    def project(n):
                        h, u = units[n]
                        if n >= 2:
                            hh, uu = units[n - 2]
                            pe.wait_ge(a_out, n - 1)
                            if uu < 2:
                                pe.wait_ge(q_out, 2 * hh + uu + 1)
                        half = u % 2
                        tok = bass.ds(b * T + half * CH, CH)
                        if u < 4:
                            w, src = ((wq, hq), (wk, hk))[u // 2]
                            m = nc.tensor.matmul(pj[n % 2][:], w[:, h, :], src[:, tok], start=True, stop=True)
                        else:
                            for t in range(CPT):
                                m = nc.tensor.matmul(pj[n % 2][:, t * P:(t + 1) * P],
                                                     hb[:, half * CH + t * P:half * CH + (t + 1) * P],
                                                     wv[:, h, :], start=True, stop=True)
                        m.then_inc(p_mm, 1)

                    for n in range(6):
                        if units[n] == (0, 4):
                            pe.wait_ge(h_in, 1)
                        project(n)
                    for g in range(G + 4):
                        h, r = divmod(g, GRP)
                        if g < G:
                            if r == 0:
                                pe.wait_ge(a_out, 6 * h + 4)
                                pe.wait_ge(q_out, 2 * h + 2)
                            if g >= 2:
                                pe.wait_ge(biased, g - 1)
                            for i in range(4):
                                j = 4 * r + i
                                m = nc.tensor.matmul(sp_[g % 2][:, i, :], qbd[:, h % 2, j, :],
                                                     kk[:, h % 2, BLK * j:BLK * j + P], start=True, stop=True)
                            m.then_inc(s_mm, 1)
                        for n in unit_steps(g):
                            project(n)
                        if 2 <= g < G + 2:
                            k = g - 2
                            pe.wait_ge(normed, k + 1)
                            if k >= 1:
                                pe.wait_ge(pt_out, k)
                            for i in range(4):
                                m = nc.tensor.transpose(tp[:, i, :], pr[:, k % 4, i, :], K.ident[:])
                            m.then_inc(turned, 1)
                        if 3 <= g < G + 3:
                            k = g - 3
                            hh, rr = divmod(k, GRP)
                            pe.wait_ge(pt_out, k + 1)
                            if rr == 0:
                                pe.wait_ge(a_out, 6 * hh + 6)
                                pe.wait_ge(v_sh[hh % 2], 32 * (hh // 2 + 1))
                            if k >= 1:
                                pe.wait_ge(o_out, k)
                            for i in range(4):
                                j = 4 * rr + i
                                src = (vs, vv)[j % 2][:, hh % 2, j // 2, :]
                                for a in range(2):
                                    m = nc.tensor.matmul(op[a * BLK:(a + 1) * BLK, i, :], src[:, a * HD0:(a + 1) * HD0],
                                                         pt[:, k % 2, i, a * BLK:(a + 1) * BLK], start=True, stop=True)
                            m.then_inc(pv_mm, 1)
                        if g >= 4 and (g - 4) % GRP == GRP - 1:
                            hh = (g - 4) // GRP
                            pe.wait_ge(o_out, GRP * (hh + 1))
                            pe.wait_ge(wo_gated, 1)
                            for t in range(TPB):
                                m = nc.tensor.matmul(wp[t // CPT][:, t % CPT, :], oT[:, hh % 2, t * P:(t + 1) * P],
                                                     wog[:, hh, :], start=(hh == 0 and t % CPT == 0),
                                                     stop=(hh == PAIRS - 1), skip_group_check=True)
                            m.then_inc(wo_mm, 1)

                @block.scalar
                def _(act):
                    def evacuate(n):
                        h, u = units[n]
                        half = u % 2
                        act.wait_ge(p_mm, n + 1)
                        if u == 0 and h >= 2:
                            act.wait_ge(s_mm, GRP * (h - 1))
                        if u == 4 and h >= 2:
                            act.wait_ge(pv_mm, GRP * (h - 1))
                            act.wait_ge(v_sh[h % 2], 32 * (h // 2))
                        if u < 2:
                            r = nc.scalar.activation(
                                qbd[0:BLK, h % 2, half * 8:half * 8 + 8, 0:BLK],
                                pj[n % 2][0:BLK, :].rearrange("p (j q) -> p j q", q=BLK), ACT.Copy, scale=qs[0:BLK, h:h + 1])
                        elif u < 4:
                            r = nc.scalar.copy(kk[:, h % 2, BLK + half * CH:BLK + (half + 1) * CH], pj[n % 2][:])
                        else:
                            r = nc.scalar.copy(vv[:, h % 2, half * CPT:(half + 1) * CPT, :],
                                               pj[n % 2][:].rearrange("p (t d) -> p t d", d=P))
                        r.then_inc(a_out, 1)

                    for n in range(6):
                        if n == 1:
                            nc.scalar.copy(hb, K.hT[:, bass.ds(b * T, T)]).then_inc(h_in, 1)
                        evacuate(n)
                    for g in range(G + 3):
                        for n in unit_steps(g):
                            evacuate(n)
                        if g < G:
                            act.wait_ge(biased, g + 1)
                            if g >= 4:
                                act.wait_ge(turned, g - 3)
                            for i in range(4):
                                r = nc.scalar.activation(pr[:, g % 4, i, :], sb_[:, g % 4, i, :], ACT.Exp, scale=-1.0,
                                                         bias=mn[:, g % 4, i:i + 1], accum_out=sm[:, g % 4, i:i + 1])
                            r.then_inc(exped, 1)
                        if g >= 3:
                            k = g - 3
                            act.wait_ge(pv_mm, k + 1)
                            if k % GRP == 0 and k >= 2 * GRP:
                                act.wait_ge(wo_mm, k // GRP - 1)
                            nc.scalar.copy(oT[:, k // GRP % 2, (k % GRP) * 256:(k % GRP + 1) * 256],
                                           op[:].rearrange("p i q -> p (i q)")).then_inc(o_out, 1)

                @block.vector
                def _(dve):
                    v = nc.vector

                    def evacuate(n):
                        h, u = units[n]
                        if u >= 2:
                            return
                        dve.wait_ge(p_mm, n + 1)
                        if u == 0 and h >= 2:
                            dve.wait_ge(s_mm, GRP * (h - 1))
                        v.tensor_scalar(qbd[BLK:P, h % 2, u * 8:u * 8 + 8, BLK:P],
                                        pj[n % 2][BLK:P, :].rearrange("p (j q) -> p j q", q=BLK),
                                        qs[BLK:P, h:h + 1], None, ALU.mult).then_inc(q_out, 1)

                    for n in range(6):
                        evacuate(n)
                    for g in range(G + 2):
                        h, r = divmod(g, GRP)
                        for n in unit_steps(g):
                            evacuate(n)
                        if g < G:
                            dve.wait_ge(s_mm, g + 1)
                            if g >= 4:
                                dve.wait_ge(exped, g - 3)
                            for i in range(4):
                                first = 1 if 4 * r + i == 0 else 0
                                q = v.tensor_tensor_reduce(sb_[:, g % 4, i, :], sp_[g % 2][:, i, :],
                                                           nbias[:, h, first, :], 1.0, 3e38, ALU.add, ALU.min,
                                                           mn[:, g % 4, i:i + 1])
                            q.then_inc(biased, 1)
                        if 1 <= g < G + 1:
                            dve.wait_ge(exped, g)
                            v.reciprocal(ri[:, (g - 1) % 4, :], sm[:, (g - 1) % 4, :]).then_inc(rsum, 1)
                        if g >= 2:
                            k = g - 2
                            dve.wait_ge(turned, k + 1)
                            if k >= 2:
                                dve.wait_ge(pv_mm, k - 1)
                            v.tensor_copy(pt[:, k % 2], tp[:]).then_inc(pt_out, 1)
                    dve.wait_ge(wo_mm, PAIRS)
                    for i in range(2):
                        xs = K.x[:, bass.ds(b * TPB + i * CPT, CPT), :]
                        v.tensor_tensor(xs, xs, wp[i][:], ALU.add)

                @block.gpsimd
                def _(pool):
                    gate = K.mod_rows[:, 0, bass.ds(b, 1), GA, :].rearrange("p a d -> p (a d)")
                    nc.gpsimd.tensor_tensor(wog[:], wo[:], bc(gate, 1, PAIRS), ALU.mult).then_inc(wo_gated, 1)
                    for g in range(G):
                        pool.wait_ge(rsum, g + 1)
                        pb = pr[:, g % 4]
                        nc.gpsimd.tensor_tensor(pb, pb, bc(ri[:, g % 4, :], 2, P), ALU.mult).then_inc(normed, 1)

                @block.sync
                def _(sp):
                    for h in range(PAIRS):
                        sp.wait_ge(a_out, 6 * h + 6)
                        if h >= 2:
                            sp.wait_ge(pv_mm, GRP * (h - 1))
                        sp.dma_start(vs[BLK:P, h % 2], vv[0:BLK, h % 2]).then_inc(v_sh[h % 2], 16)
                        sp.dma_start(vs[0:BLK, h % 2, 1:TPB], vv[BLK:P, h % 2, 0:TPB - 1]).then_inc(v_sh[h % 2], 16)
                    sp.wait_ge(v_sh0, 16 * PAIRS)
                    sp.wait_ge(v_sh1, 16 * PAIRS)
            nc.all_engine_barrier(sems_to_clear=clear)


def routing_stage(nc, K, A, name, b2, renormalise, M):
    with ExitStack() as st:
        b2f = K.sb(name + "_b2", [KROWS, D], ctx=st)
        b2r = K.sb(name + "_b2_rest", [KROWS, D], ctx=st)
        b2p = K.sb(name + "_b2_parts", [KROWS, 3, D], BF16, ctx=st)
        lg = K.sb(name + "_logits", [P, NT, E], ctx=st)
        mx = K.sb(name + "_max", [P, NT], ctx=st)
        ex = K.sb(name + "_exp", [P, NT, E], ctx=st)
        sm = K.sb(name + "_sum", [P, NT], ctx=st)
        rs = K.sb(name + "_rsum", [P, NT], ctx=st)
        pb = K.sb(name + "_probs", [P, NT, E], ctx=st)
        gt = K.sb(name + "_above", [P, NT, E * E], ctx=st)
        eq = K.sb(name + "_equal", [P, NT, E * E], ctx=st)
        rank = K.sb(name + "_rank", [P, NT, E], ctx=st)
        w3 = K.sb(name + "_w3", [P, NT, 3, E], ctx=st)
        wp = K.sb(name + "_wp", [P, NT, E], BF16, ctx=st)
        wr = K.sb(name + "_wr", [P, NT, E], ctx=st)
        raw = K.sb(name + "_raw", [P, RAW, M.F], ctx=st)
        sraw = K.sb(name + "_sraw", [KROWS, E * P], ctx=st)
        bias, bg, low, lp = M.bias_in, M.bg, M.low, M.lp
        tp = [K.ps(f"{name}_tps{i}", [P, CPT, P], st) for i in range(2)]
        bp = [K.ps(f"{name}_bps{i}", [P, CPT, D], st) for i in range(2)]
        (dve, act_s, t_mm, t_out, b_mm, b_out, b2_in, b2_split) = K.sems(
            st, name, "dve", "act", "turned", "wT_out", "b2_mm", "b2_out", "b2_in",
            "b2_split")
        (s_in, hi_out, lo_out, zeroed, *m_in) = K.sems(
            st, name + "m", "sel_in", "hi_out", "lo_out", "zeroed", *(f"matrix_in{i}" for i in range(RAW)))
        matrices = [(w, part, e) for w, part in ((M.w1, M.w1_in), (M.w2, M.w2_in)) for e in range(E)]
        n_chain = 11 + (bias is not None) + 4 * renormalise

        def low_part(eng, e_, i):
            w, _, e = matrices[i]
            eng.wait_ge(hi_out, i + 1)
            cs = slice(e * M.F, (e + 1) * M.F)
            return e_.tensor_tensor(w[1][:, cs], raw[:, i % RAW, :], w[0][:, cs].bitcast(F32), ALU.subtract)

        with nc.Block() as block:
            @block.sync
            def _(sp):
                if b2 is not None:
                    sp.wait_ge(zeroed, 1)
                    for i in range(3):
                        sp.dma_start(b2f[i * E:(i + 1) * E, :], b2).then_inc(b2_in, 16)
                sp.dma_start(sraw[:], A["select"]).then_inc(s_in, 16)
                if M.b1_in is not None:
                    sp.dma_start(M.b1[:], M.b1_in).then_inc(s_in, 16)
                for i, (w, part, e) in enumerate(matrices):
                    if i >= RAW:
                        sp.wait_ge(lo_out, i - RAW + 1)
                    src = part[e] if part is M.w1_in else part[e].rearrange("(c p) d -> p c d", p=P)
                    dst = raw[:, i % RAW, :]
                    if part is M.w2_in:
                        dst = dst.rearrange("p (c d) -> p c d", d=D)
                    sp.dma_start(dst, src).then_inc(m_in[i % RAW], 16)
                sp.wait_ge(s_in, 16 * (1 + (M.b1_in is not None)))

            @block.gpsimd
            def _(pool):
                nc.gpsimd.memset(b2f[:], 0.0).then_inc(zeroed, 1)
                nc.gpsimd.memset(M.wT3[:], 0.0).then_inc(zeroed, 1)
                if b2 is not None:
                    pool.wait_ge(b2_in, 48)
                    split3(nc.gpsimd, pool, b2_split, 0, b2f[:], [b2p[:, j, :] for j in range(3)], b2r[:])
                for i in range(len(matrices) - RAW):
                    low_part(pool, nc.gpsimd, i).then_inc(lo_out, 1)

            @block.tensor
            def _(pe):
                pe.wait_ge(dve, n_chain + 6)
                for c in range(NCH):
                    if c >= 2:
                        pe.wait_ge(t_out, c - 1)
                    for t in range(CPT):
                        m = nc.tensor.transpose(tp[c % 2][0:3 * E, t, :],
                                                w3[:, c * CPT + t].rearrange("p a e -> p (a e)"), K.ident[:])
                    m.then_inc(t_mm, 1)
                if b2 is not None:
                    pe.wait_ge(b2_split, 4)
                    for c in range(NCH):
                        pe.wait_ge(t_out, c + 1)
                        if c >= 2:
                            pe.wait_ge(b_out, c - 1)
                        for t in range(CPT):
                            k = c * CPT + t
                            for j in range(3):
                                m = nc.tensor.matmul(bp[c % 2][:, t, :], M.wT3[:, k * P:(k + 1) * P], b2p[:, j, :],
                                                     start=(j == 0), stop=(j == 2))
                        m.then_inc(b_mm, 1)

            @block.scalar
            def _(act):
                act.wait_ge(dve, 2 + (bias is not None))
                nc.scalar.activation(ex[:], lg[:], ACT.Exp).then_inc(act_s, 1)
                for i, (w, part, e) in enumerate(matrices):
                    act.wait_ge(m_in[i % RAW], 16 * (i // RAW + 1))
                    nc.scalar.copy(w[0][:, e * M.F:(e + 1) * M.F], raw[:, i % RAW, :]).then_inc(hi_out, 1)
                act.wait_ge(zeroed, 2)
                for c in range(NCH):
                    act.wait_ge(t_mm, c + 1)
                    nc.scalar.copy(M.wT3[0:3 * E, c * CH:(c + 1) * CH],
                                   tp[c % 2][0:3 * E].rearrange("e t q -> e (t q)")).then_inc(t_out, 1)
                act.wait_ge(s_in, 16 * (1 + (M.b1_in is not None)))
                nc.scalar.copy(M.sel[:], sraw[:])

            @block.vector
            def _(dve_):
                v = nc.vector
                n = [0]

                def step(ins):
                    n[0] += 1
                    ins.then_inc(dve, 1)
                    dve_.wait_ge(dve, n[0])

                if bias is not None:
                    step(v.tensor_tensor(lg[:], lp[:], bc(bg[:], 1, NT), ALU.add))
                    src = lg
                else:
                    src = lp
                step(v.tensor_reduce(mx[:], src[:], AX.X, ALU.max))
                step(v.tensor_tensor(lg[:], src[:], bc(mx[:], 2, E), ALU.subtract))
                dve_.wait_ge(act_s, 1)
                step(v.tensor_reduce(sm[:], ex[:], AX.X, ALU.add))
                step(v.reciprocal(rs[:], sm[:]))
                step(v.tensor_tensor(pb[:], ex[:], bc(rs[:], 2, E), ALU.mult))
                over = bc(pb[:], 2, E)
                own = bc(pb[:], 3, E)
                g4 = gt[:].rearrange("p t (a b) -> p t a b", a=E)
                e4 = eq[:].rearrange("p t (a b) -> p t a b", a=E)
                step(v.tensor_tensor(g4, over, own, ALU.is_gt))
                step(v.tensor_tensor(e4, over, own, ALU.is_equal))
                step(v.tensor_tensor(eq[:], eq[:], bc(low[:], 1, NT), ALU.mult))
                step(v.tensor_tensor(gt[:], gt[:], eq[:], ALU.add))
                step(v.tensor_reduce(rank[:], g4, AX.X, ALU.add))
                step(v.scalar_tensor_tensor(out=K.w[:], in0=rank[:], scalar=2.0, in1=pb[:], op0=ALU.is_lt,
                                            op1=ALU.mult))
                if renormalise:
                    step(v.tensor_reduce(sm[:], K.w[:], AX.X, ALU.add))
                    step(v.tensor_scalar(sm[:], sm[:], TOPK_EPS, None, ALU.add))
                    step(v.reciprocal(rs[:], sm[:]))
                    step(v.tensor_tensor(K.w[:], K.w[:], bc(rs[:], 2, E), ALU.mult))
                assert n[0] == n_chain
                step(v.tensor_copy(wp[:], K.w[:]))
                step(v.tensor_copy(w3[:, :, 0, :], wp[:]))
                step(v.tensor_tensor(wr[:], K.w[:], wp[:], ALU.subtract))
                step(v.tensor_copy(wp[:], wr[:]))
                step(v.tensor_copy(w3[:, :, 1, :], wp[:]))
                step(v.tensor_tensor(w3[:, :, 2, :], wr[:], wp[:], ALU.subtract))
                for i in range(len(matrices) - RAW, len(matrices)):
                    low_part(dve_, v, i)
                if b2 is not None:
                    for c in range(NCH):
                        dve_.wait_ge(b_mm, c + 1)
                        h = K.nat[:, c * CPT:(c + 1) * CPT, :]
                        v.tensor_tensor(h, h, bp[c % 2][:], ALU.add).then_inc(b_out, 1)


RAW = 4


class Experts:

    def __init__(self, K, name, F, w1, w2, b1, router, bias, st):
        self.F, self.w1_in, self.w2_in, self.b1_in, self.router_in, self.bias_in = F, w1, w2, b1, router, bias
        self.w1 = [K.sb(f"{name}_w1{part}", [P, E * F], F32R, ctx=st) for part in ("hi", "lo")]
        self.w2 = [K.sb(f"{name}_w2{part}", [P, E * F], F32R, ctx=st) for part in ("hi", "lo")]
        self.b1 = K.sb(name + "_b1", [P, E * F // P], ctx=st)
        self.wT3 = K.sb(name + "_wT3", [KROWS, B * T], BF16, ctx=st)
        self.sel = K.sb(name + "_sel", [KROWS, E * P], BF16, ctx=st)
        self.wg = K.sb(name + "_wg", [P, E], ctx=st)
        self.bg = K.sb(name + "_bg", [P, E], ctx=st)
        self.low = K.sb(name + "_lower", [P, E * E], ctx=st)
        self.lp = K.ps(name + "_logits_ps", [P, NT, E], st)
        (self.router_loaded,) = K.sems(st, name, "router_in")

    def load_router(self, sp, A):
        n_in = 2 + (self.bias_in is not None)
        sp.dma_start(self.wg[:], self.router_in).then_inc(self.router_loaded, 16)
        sp.dma_start(self.low[:], A["lower"]).then_inc(self.router_loaded, 16)
        if self.bias_in is not None:
            sp.dma_start(self.bg[:], self.bias_in.partition_broadcast(P)).then_inc(self.router_loaded, 16)
        sp.wait_ge(self.router_loaded, 16 * n_in)

    def logits(self, nc, K, pe, N, b):
        pe.wait_ge(N.turn_read, 2 * b + 2)
        pe.wait_ge(self.router_loaded, 16 * (2 + (self.bias_in is not None)))
        for t in range(b * TPB, (b + 1) * TPB):
            nc.tensor.matmul(self.lp[:, t, :], K.hT[:, t * P:(t + 1) * P], self.wg[:], start=True, stop=True)


def expert_stage(nc, K, name, M, gelu, layer, out=None):
    F = M.F
    FC = F // P
    with ExitStack() as st:
        hs = [K.sb(f"{name}_h{part}", [P, 2, CH], F32R, ctx=st) for part in ("hi", "lo")]
        hf = K.sb(name + "_hid", [P, 3, CH], ctx=st)
        hid = [K.sb(f"{name}_hid_{part}", [P, 2, FC, CH], F32R, ctx=st) for part in ("hi", "lo")]
        wbs = K.sb(name + "_wb", [P, 2, CH], ctx=st)
        ym = K.sb(name + "_ym", [P, 2, CH], ctx=st)
        hp = [K.ps(f"{name}_hps{i}", [P, CH], st) for i in range(4)]
        yp = [K.ps(f"{name}_yps{i}", [P, CH], st) for i in range(2)]
        wp = K.ps(f"{name}_wps", [P, CH], st)
        (h_hi, h_lo, h_mm, g_out, hid_hi, hid_lo, w_mm, w_out, y_mm, y_out, y_sum, x_out), clear = K.moe_sems
        S = 2 * E
        SPLITS = (E // 2, E + E // 2)

        def sums(k):
            return k + 1 - (k // E + 1)

        (hi0, lo0) = K.sems(st, name + "h", "h_hi", "h_lo")
        with nc.Block() as block:
            @block.scalar
            def _(act):
                nc.scalar.copy(hs[0][:, 0, :], K.hT[:, 0:CH]).then_inc(hi0, 1)

            @block.vector
            def _(dve):
                nc.vector.memset(K.hT[:, B * T:], 0.0)
                dve.wait_ge(hi0, 1)
                nc.vector.tensor_tensor(hs[1][:, 0, :], K.hT[:, 0:CH], hs[0][:, 0, :].bitcast(F32), ALU.subtract
                                        ).then_inc(lo0, 1)

        with nc.Fori(0, B) as b:
            def tokens(c):
                return K.hT[:, bass.ds(b * T + c * CH, CH)]

            def acc(c):
                return K.nat[:, bass.ds(b * TPB + c * CPT, CPT), :].rearrange("p t d -> p (t d)")

            with nc.Block() as block:
                @block.tensor
                def _(pe):
                    def passes(out, w, cols, x, first, last):
                        nc.tensor.matmul(out, w[0][:, cols], x[0], start=first, stop=False)
                        nc.tensor.matmul(out, w[0][:, cols], x[1], start=False, stop=False)
                        return nc.tensor.matmul(out, w[1][:, cols], x[0], start=False, stop=last)

                    for s in range(S + 1):
                        if s < S:
                            c, e = divmod(s, E)
                            if s == E:
                                pe.wait_ge(h_lo, 1)
                            for f in range(FC):
                                n = s * FC + f
                                if n >= 4:
                                    pe.wait_ge(g_out, n - 3)
                                passes(hp[n % 4][:], M.w1, slice((e * FC + f) * P, (e * FC + f + 1) * P),
                                       [x[:, c, :] for x in hs], True, True).then_inc(h_mm, 1)
                            if s >= 1:
                                pe.wait_ge(w_out, s)
                            nc.tensor.matmul(wp[:], M.sel[:, e * P:(e + 1) * P],
                                             M.wT3[:, bass.ds(b * T + c * CH, CH)], start=True, stop=True
                                             ).then_inc(w_mm, 1)
                        if s >= 1:
                            k = s - 1
                            e = k % E
                            pe.wait_ge(hid_lo, FC * (k + 1))
                            if k >= 2:
                                pe.wait_ge(y_out, k - 1)
                            for f in range(FC):
                                m = passes(yp[k % 2][:], M.w2, slice((e * FC + f) * D, (e * FC + f + 1) * D),
                                           [x[:, k % 2, f, :] for x in hid], f == 0, f == FC - 1)
                            m.then_inc(y_mm, 1)

                @block.scalar
                def _(act):
                    for s in range(S):
                        for f in range(FC):
                            n = s * FC + f
                            act.wait_ge(h_mm, n + 1)
                            if n >= 3:
                                act.wait_ge(hid_lo, n - 2)
                            col = s % E * FC + f
                            nc.scalar.activation(hf[:, n % 3, :], hp[n % 4][:], gelu,
                                                 bias=M.b1[:, col:col + 1] if M.b1_in is not None else 0.0
                                                 ).then_inc(g_out, 1)
                        act.wait_ge(w_mm, s + 1)
                        if s >= 2:
                            act.wait_ge(y_out, s - 1)
                        nc.scalar.copy(wbs[:, s % 2, :], wp[:]).then_inc(w_out, 1)
                        for i, split in enumerate(SPLITS):
                            if s == split:
                                nc.scalar.copy(hs[0][:, 1 - i, :], tokens(1 + i)).then_inc(h_hi, 1)

                @block.gpsimd
                def _(pool):
                    for k in range(S):
                        c, e = divmod(k, E)
                        if e:
                            pool.wait_ge(y_out, k + 1)
                            if e >= 2:
                                pool.wait_ge(y_sum, sums(k - 1))
                            nc.gpsimd.tensor_tensor(acc(c), acc(c), ym[:, k % 2, :], ALU.add).then_inc(y_sum, 1)

                @block.vector
                def _(dve):
                    v = nc.vector

                    def weigh(k):
                        c, e = divmod(k, E)
                        dve.wait_ge(y_mm, k + 1)
                        dve.wait_ge(w_out, k + 1)
                        if k >= 2 and sums(k - 2):
                            dve.wait_ge(y_sum, sums(k - 2))
                        v.tensor_tensor(acc(c) if e == 0 else ym[:, k % 2, :], yp[k % 2][:], wbs[:, k % 2, :],
                                        ALU.mult).then_inc(y_out, 1)

                    ts = bass.ds(b * TPB, TPB)
                    gate = K.mod_rows[:, layer, bass.ds(b, 1), GB, :].rearrange("p a d -> p (a d)")
                    gated = ym[:].rearrange("p a (t d) -> p (a t) d", d=D)
                    v.tensor_tensor(gated, K.nat[:, ts, :], bc(gate, 1, TPB), ALU.mult).then_inc(x_out, 1)
                    dve.wait_ge(x_out, 1)
                    v.tensor_tensor(K.x[:, ts, :], K.x[:, ts, :], gated, ALU.add).then_inc(x_out, 1)
                    dve.wait_ge(x_out, 2)
                    for s in range(S):
                        for f in range(FC):
                            n = s * FC + f
                            dve.wait_ge(g_out, n + 1)
                            if f == 0 and s >= 2:
                                dve.wait_ge(y_mm, s - 1)
                            v.tensor_copy(hid[0][:, s % 2, f, :], hf[:, n % 3, :]).then_inc(hid_hi, 1)
                            dve.wait_ge(hid_hi, n + 1)
                            v.tensor_tensor(hid[1][:, s % 2, f, :], hf[:, n % 3, :],
                                            hid[0][:, s % 2, f, :].bitcast(F32), ALU.subtract).then_inc(hid_lo, 1)
                        if s >= 1:
                            weigh(s - 1)
                        for i, split in enumerate(SPLITS):
                            if s == split:
                                dve.wait_ge(h_hi, i + 1)
                                v.tensor_tensor(hs[1][:, 1 - i, :], tokens(1 + i), hs[0][:, 1 - i, :].bitcast(F32),
                                                ALU.subtract).then_inc(h_lo, 1)
                    weigh(S - 1)
            nc.all_engine_barrier(sems_to_clear=clear)

        (gated, turned, added) = K.sems(st, name + "x", "gated", "turned", "added")
        (stored,) = K.sems(st, name + "o", "stored")
        with nc.Block() as block:
            if out is not None:
                @block.sync
                def _(sp):
                    for c in range(NCH):
                        sp.wait_ge(added, c + 1)
                        b, t = divmod(c * CPT, TPB)
                        sp.dma_start(out[b].rearrange("(t p) d -> p t d", p=P)[:, t:t + CPT, :],
                                     K.x[:, c * CPT:(c + 1) * CPT, :]).then_inc(stored, 16)
                    sp.wait_ge(stored, 16 * NCH)

            @block.scalar
            def _(act):
                for c in range(NCH):
                    if c >= 2:
                        act.wait_ge(turned, c - 1)
                    sums_t = K.nat[:, c * CPT:(c + 1) * CPT, :].rearrange("p t d -> p (t d)")
                    nc.scalar.activation(ym[:, c % 2, :], sums_t, ACT.Identity,
                                         scale=K.mod_cols[:, layer, GB, c * CH // T:c * CH // T + 1]
                                         ).then_inc(gated, 1)

            @block.tensor
            def _(pe):
                for c in range(NCH):
                    pe.wait_ge(gated, c + 1)
                    if c >= 2:
                        pe.wait_ge(added, c - 1)
                    for t in range(CPT):
                        cols = slice(t * P, (t + 1) * P)
                        m = nc.tensor.transpose(yp[c % 2][:, cols], ym[:, c % 2, cols], K.ident[:])
                    m.then_inc(turned, 1)

            @block.vector
            def _(dve):
                for c in range(NCH):
                    dve.wait_ge(turned, c + 1)
                    h = K.x[:, c * CPT:(c + 1) * CPT, :]
                    nc.vector.tensor_tensor(h, h, yp[c % 2][:].rearrange("p (t d) -> p t d", d=D), ALU.add
                                            ).then_inc(added, 1)


def split3(v, eng, done, count, f, parts, r):
    v.tensor_copy(parts[0], f).then_inc(done, 1)
    eng.wait_ge(done, count + 1)
    v.tensor_tensor(r, f, parts[0], ALU.subtract).then_inc(done, 1)
    eng.wait_ge(done, count + 2)
    v.tensor_copy(parts[1], r).then_inc(done, 1)
    eng.wait_ge(done, count + 3)
    v.tensor_tensor(parts[2], r, parts[1], ALU.subtract).then_inc(done, 1)
    return count + 4


def qkv1_stage(nc, K, A, v_nat, parts_dram, set_up, first_load):
    with ExitStack() as st:
        w = K.sb("w1_qkvT", [P, 3, D], ctx=st)
        bqk = K.sb("b1_qk", [P, 2], ctx=st)
        bqs = K.sb("b1_qk_scaled", [P, 2], ctx=st)
        bv = K.sb("b1_v", [P, D], ctx=st)
        f = K.sb("qk_f", [P, 3, CH], ctx=st)
        r = K.sb("qk_r", [P, 2, CH], ctx=st)
        pa = K.sb("qk_parts", [P, 2, 3, CH], BF16, ctx=st)
        qp = [K.ps(f"qk_ps{i}", [P, CH], st) for i in range(2)]
        vp = [K.ps(f"v1_ps{i}", [P, CPT, D], st) for i in range(2)]
        (w_in, b_s, q_mm, f_out, split, q_stored, k_stored, v_mm, v_out) = K.sems(
            st, "qkv1", "w_in", "bias", "qk_mm", "qk_out", "split", "q_stored", "k_stored", "v_mm", "v_out")
        stored = (q_stored, k_stored)
        units = [(c, i) for c in range(NCH) for i in range(2)]
        N = Norm(nc, K, "n1a", K.x, K.nat, st)
        banks = [K.ps(f"n1a_ps{i}", [P, CPT, P], st) for i in range(4)]
        with nc.Block() as block:
            @block.gpsimd
            def _(pool):
                for b in range(B):
                    N.deviation(pool, b)
                set_up(pool, 0)
                set_up(pool, 1)

            @block.sync
            def _(sp):
                for i, n in enumerate(("L1_attn_WqT", "L1_attn_WkT", "L1_attn_WvT")):
                    sp.dma_start(w[:, i, :], A[n]).then_inc(w_in, 16)
                for i, n in enumerate(("L1_attn_bq", "L1_attn_bk")):
                    sp.dma_start(bqk[:, i:i + 1], A[n].rearrange("(p a) -> p a", a=1)).then_inc(w_in, 16)
                sp.dma_start(bv[:], A["L1_attn_bv"].partition_broadcast(P)).then_inc(w_in, 16)
                for n, (c, i) in enumerate(units):
                    sp.wait_ge(split, 4 * (n + 1))
                    sp.dma_start(parts_dram[i, :, :, c * CH:(c + 1) * CH].rearrange("a p t -> p a t"),
                                 pa[:, n % 2]).then_inc(stored[i], 16)
                    if c * CH >= (B - 1) * T:
                        sp.dma_start(parts_dram[i, :, :, c * CH + T:(c + 1) * CH + T].rearrange("a p t -> p a t"),
                                     pa[:, n % 2]).then_inc(stored[i], 16)
                for q in stored:
                    sp.wait_ge(q, 16 * (NCH + T // CH))

            @block.tensor
            def _(pe):
                pe.wait_ge(w_in, 16 * 6)
                N.turn(pe, banks, 0)
                for n, (c, i) in enumerate(units):
                    b, first = divmod(2 * c + i, 2 * T // CH)
                    if first == 0 and b + 1 < B:
                        N.turn(pe, banks, b + 1)
                    pe.wait_ge(N.turn_read, c + 1)
                    if n >= 2:
                        pe.wait_ge(f_out, n - 1)
                    nc.tensor.matmul(qp[n % 2][:], w[:, i, :], K.hT[:, c * CH:(c + 1) * CH],
                                     start=True, stop=True).then_inc(q_mm, 1)
                    if i == 1:
                        if c >= 2:
                            pe.wait_ge(v_out, c - 1)
                        for t in range(CPT):
                            m = nc.tensor.matmul(vp[c % 2][:, t, :], K.hT[:, c * CH + t * P:c * CH + (t + 1) * P],
                                                 w[:, 2, :], start=True, stop=True)
                        m.then_inc(v_mm, 1)

            @block.scalar
            def _(act):
                def affine(b):
                    N.affine(act, banks, b, K.mod_cols[:, 1, CA, b:b + 1], K.mod_cols[:, 1, SA, b:b + 1])

                act.wait_ge(b_s, 1)
                N.normalised_even(act, 0)
                affine(0)
                for n, (c, i) in enumerate(units):
                    b, first = divmod(2 * c + i, 2 * T // CH)
                    if first == 0:
                        if b >= 1:
                            affine(b)
                        if b + 1 < B:
                            N.normalised_even(act, b + 1)
                    act.wait_ge(q_mm, n + 1)
                    if n >= 3:
                        act.wait_ge(split, 4 * (n - 2))
                    nc.scalar.activation(f[:, n % 3, :], qp[n % 2][:], ACT.Identity, bias=bqs[:, i:i + 1],
                                         scale=HD1 ** -0.5 if i == 0 else 1.0).then_inc(f_out, 1)
                    if (c, i) == (NCH // 2, 1):
                        for q in stored:
                            act.wait_ge(q, 16 * T // CH)
                        first_load(act)

            @block.vector
            def _(dve):
                v = nc.vector
                dve.wait_ge(w_in, 16 * 6)
                v.tensor_copy(bqs[:, 1:2], bqk[:, 1:2])
                v.tensor_scalar(bqs[:, 0:1], bqk[:, 0:1], HD1 ** -0.5, None, ALU.mult).then_inc(b_s, 1)
                for b in range(B):
                    N.statistics(dve, b)
                for b in range(B):
                    N.normalised_odd(dve, b)
                count = 0
                for n, (c, i) in enumerate(units):
                    dve.wait_ge(f_out, n + 1)
                    if n >= 2:
                        dve.wait_ge(stored[i], 16 * (c + max(0, c - (B - 1) * T // CH)))
                        dve.wait_ge(split, count)
                    count = split3(v, dve, split, count, f[:, n % 3, :], [pa[:, n % 2, j, :] for j in range(3)],
                                   r[:, n % 2, :])
                    if i == 1:
                        dve.wait_ge(v_mm, c + 1)
                        v.tensor_tensor(v_nat[:, c * CPT:(c + 1) * CPT, :], vp[c % 2][:], bc(bv[:], 1, CPT),
                                        ALU.add).then_inc(v_out, 1)


ATT_SEMS = ("loaded0", "loaded1", "loaded2", "loaded3", "m1_mm", "maxed", "m_turned", "m_neg", "m_split",
            "m_stored", "m_loaded",
            "s2_mm", "exp", "v_aug", "pv_mm", "o_out", "o_turned", "o_done", "o_rsum")


def full_attention_stage(nc, K, A, wo):
    parts = nc.dram_tensor("qk_parts_dram", [2, 3, P, (B + 1) * T], BF16, kind="Internal").ap()
    mdram = nc.dram_tensor("neg_max_dram", [2, 3, 4 * TPB * P], BF16, kind="Internal").ap()
    with ExitStack() as st:
        v_nat = K.sb("v_nat", [P, NT, D], ctx=st)
        qs = K.sb("q_stack", [P, 4, 4, T], BF16, ctx=st)
        ks = K.sb("k_stack", [P, 4, 4, T], BF16, ctx=st)
        va = K.sb("v_aug", [P, 2, TPB, 4, 32], ctx=st)
        (ops_set,) = K.sems(st, "att1z", "operands_set")
        flat = "p a h t -> p (a h t)"

        def load(eng, sem, ring, batch, quad):
            for i, (dst, order) in enumerate(((qs, Q_PART), (ks, K_PART))):
                for slot, part in enumerate(order):
                    src = parts[i, part, quad * 32:(quad + 1) * 32, bass.ds(batch * T, T)]
                    eng.dma_start(dst[slot * HD1:(slot + 1) * HD1, ring], src.rearrange("(h d) t -> d h t", d=HD1)
                                  ).then_inc(sem, 16)
            eng.dma_start(qs[MROW:MROW + 3, ring], ks[KROWS - 3:KROWS, ring]).then_inc(sem, 16)

        LOADS = 16 * (2 * len(Q_PART) + 1)

        FILLS = 5

        def set_up(pool, part):
            g, ring = nc.gpsimd, slice(2 * part, 2 * part + 2)
            fills = ((qs[0:KROWS, ring].rearrange(flat).bitcast(F32), 0.0),
                     (ks[64:KROWS, ring].rearrange(flat).bitcast(F32), 0.0),
                     (ks[32:64, ring].rearrange(flat), 1.0), (va[:, part].rearrange("p t h c -> p (t h c)"), 0.0),
                     (va[:, part, :, :, HD1:HD1 + 1].rearrange("p t h c -> p (t h) c"), 1.0))
            for n, (dst, value) in enumerate(fills):
                g.memset(dst, value).then_inc(ops_set, 1)
                pool.wait_ge(ops_set, FILLS * part + n + 1)

        sm0 = dict(zip(ATT_SEMS, K.sems(st, "att1p", *ATT_SEMS)))

        def first_load(act):
            act.wait_ge(ops_set, FILLS)
            load(act, sm0["loaded0"], 0, 0, 0)

        qkv1_stage(nc, K, A, v_nat, parts, set_up, first_load)
        pr = K.sb("probs1", [P, 2, 4, CH], ctx=st)
        osb = K.sb("o_sb", [P, 2, CH], ctx=st)
        mx = K.sb("q_max", [P, 2, 4 * TPB], ctx=st)
        nm = K.sb("neg_max", [4 * TPB, P], ctx=st)
        nr = K.sb("neg_max_rest", [4 * TPB, P], ctx=st)
        mp = K.sb("neg_max_parts", [4 * TPB, 2, 3, P], BF16, ctx=st)
        ro = K.sb("o_rsum", [P, 2, CPT, 4], ctx=st)
        s1 = [K.ps(f"s1_ps{i}", [P, T], st) for i in range(2)]
        s2 = [K.ps(f"s2_ps{i}", [P, CH], st) for i in range(2)]
        op = K.ps("o1_ps", [P, CH], st)
        mi = K.ps("misc_ps", [P, CPT, P], st)
        UNITS = 4 * TPB
        LEAD = 8

        def first_pass(pe, sm, k, ring, n):
            h, qt = divmod(n, TPB)
            if k >= 2:
                pe.wait_ge(sm["maxed"], k - 1)
            for c in range(2):
                m = nc.tensor.matmul(s1[k % 2][:, c * CH:(c + 1) * CH], qs[0:KROWS, ring, h, qt * P:(qt + 1) * P],
                                     ks[0:KROWS, ring, h, c * CH:(c + 1) * CH], start=True, stop=True)
            m.then_inc(sm["m1_mm"], 1)

        def reduce_max(dve, sm, k, ring, n):
            dve.wait_ge(sm["m1_mm"], k + 1)
            nc.vector.tensor_reduce(mx[:, ring % 2, n:n + 1], s1[k % 2][:], AX.X, ALU.max).then_inc(sm["maxed"], 1)

        def turn_max(pe, sm, ring, units):
            pe.wait_ge(sm["maxed"], units)
            nc.tensor.transpose(mi[0:UNITS, 0, :], mx[:, ring % 2, :], K.ident[:]).then_inc(sm["m_turned"], 1)

        def negate_max(dve, sm, slot):
            dve.wait_ge(sm["m_turned"], slot + 1)
            if slot >= 1:
                dve.wait_ge(sm["m_split"], 4 * slot)
            nc.vector.tensor_scalar(nm[:], mi[0:UNITS, 0, :], -1.0, None, ALU.mult).then_inc(sm["m_neg"], 1)

        def split_max(pool, sm, ring, slot):
            pool.wait_ge(sm["m_neg"], slot + 1)
            if slot >= 2:
                pool.wait_ge(sm["m_stored"], 16 * (slot - 1))
            split3(nc.gpsimd, pool, sm["m_split"], 4 * slot, nm[:], [mp[:, ring % 2, j, :] for j in range(3)], nr[:])

        def move_max(sp, sm, ring, slot, units):
            sp.wait_ge(sm["m_split"], 4 * (slot + 1))
            if slot >= 1:
                sp.wait_ge(sm["m_loaded"], 16 * slot)
            sp.dma_start(mdram[ring % 2].rearrange("a (c q) -> c a q", q=P), mp[:, ring % 2]
                         ).then_inc(sm["m_stored"], 16)
            sp.wait_ge(sm["m_stored"], 16 * (slot + 1))
            sp.wait_ge(sm["maxed"], units)
            sp.dma_start(qs[MROW:MROW + 3, ring], mdram[ring % 2].rearrange("a (h t) -> a h t", h=4)
                         ).then_inc(sm["m_loaded"], 16)

        ahead = [(0, n) for n in range(UNITS)] + [(1, n) for n in range(LEAD)]
        with nc.Block() as block:
            @block.gpsimd
            def _(pool):
                wo.gate(pool)
                split_max(pool, sm0, 0, 0)

            @block.sync
            def _(sp):
                load(sp, sm0["loaded1"], 1, 0, 1)
                wo.load(sp)
                move_max(sp, sm0, 0, 0, UNITS)
                sp.wait_ge(sm0["loaded1"], LOADS)
                sp.wait_ge(sm0["m_loaded"], 16)

            @block.tensor
            def _(pe):
                for k, (ring, n) in enumerate(ahead):
                    if n == 0:
                        pe.wait_ge(sm0[f"loaded{ring}"], LOADS)
                    first_pass(pe, sm0, k, ring, n)
                    if k == UNITS + 1:
                        turn_max(pe, sm0, 0, UNITS)

            @block.vector
            def _(dve):
                for k, (ring, n) in enumerate(ahead):
                    reduce_max(dve, sm0, k, ring, n)
                    if k == UNITS:
                        negate_max(dve, sm0, 0)

        sm_list, clear = K.att_sems
        sm = dict(zip(ATT_SEMS, sm_list))
        STEPS = 2 * TPB
        REST = UNITS - LEAD

        def unit(s, u):
            return ((s + 1) % 4, u + LEAD) if u < REST else ((s + 2) % 4, u - REST)

        TURN_MAX = REST // 2
        TURN_OUT = 1
        with nc.Fori(0, B) as b:
            with nc.Block() as block:
                @block.sync
                def _(sp):
                    for s in range(QUADS):
                        if s >= 2:
                            sp.wait_ge(sm["s2_mm"], 4 * STEPS * (s - 1))
                        nq = s + 2
                        load(sp, sm[f"loaded{nq % 4}"], nq % 4, b + nq // 4, nq % 4)
                        move_max(sp, sm, (s + 1) % 4, s, UNITS * s + REST)
                    for n in range(QUADS):
                        sp.wait_ge(sm[f"loaded{n}"], LOADS)
                    sp.wait_ge(sm["m_loaded"], 16 * QUADS)

                @block.gpsimd
                def _(pool):
                    for s in range(QUADS):
                        if s >= 1:
                            split_max(pool, sm, s % 4, s - 1)
                        if s >= 2:
                            pool.wait_ge(sm["pv_mm"], STEPS * (s - 1))
                        nc.gpsimd.tensor_copy(
                            va[:, s % 2, :, :, 0:HD1],
                            v_nat[:, bass.ds(b * TPB, TPB), s * 32:(s + 1) * 32].rearrange("p t (h d) -> p t h d", d=HD1)
                        ).then_inc(sm["v_aug"], 1)
                        if s == 0:
                            wo.add_bias(b)
                    split_max(pool, sm, QUADS % 4, QUADS - 1)

                @block.tensor
                def _(pe):
                    def scores(k, h):
                        s, i = divmod(k, STEPS)
                        half, kt = divmod(i, TPB)
                        if i == 0 and s >= 1 and h == 0:
                            pe.wait_ge(sm["m_loaded"], 16 * s)
                        n = 4 * k + h
                        if n >= 2:
                            pe.wait_ge(sm["exp"], n - 1)
                        nc.tensor.matmul(s2[n % 2][:], ks[0:KROWS, s, h, kt * P:(kt + 1) * P],
                                         qs[0:KROWS, s, h, half * CH:(half + 1) * CH],
                                         start=True, stop=True).then_inc(sm["s2_mm"], 1)

                    def product(k):
                        s, i = divmod(k, STEPS)
                        kt = i % TPB
                        if i == 0:
                            pe.wait_ge(sm["v_aug"], s + 1)
                        pe.wait_ge(sm["exp"], 4 * (k + 1))
                        if kt == 0 and k >= TPB:
                            pe.wait_ge(sm["o_out"], k // TPB)
                        for h in range(4):
                            m = nc.tensor.matmul(op[32 * h:32 * h + 32, :], va[:, s % 2, kt, h, :], pr[:, k % 2, h, :],
                                                 start=(kt == 0), stop=(kt == TPB - 1))
                        m.then_inc(sm["pv_mm"], 1)

                    def turn_output(m, splits):
                        pe.wait_ge(sm["o_out"], m + 1)
                        if splits >= 1:
                            pe.wait_ge(sm["m_neg"], splits)
                        if m >= 1:
                            pe.wait_ge(sm["o_done"], m)
                        for t in range(CPT):
                            x = nc.tensor.transpose(mi[:, t, :], osb[:, m % 2, t * P:(t + 1) * P], K.ident[:])
                        x.then_inc(sm["o_turned"], 1)

                    for k in range(STEPS * QUADS):
                        s, i = divmod(k, STEPS)
                        scores(k, 0)
                        scores(k, 1)
                        if k >= 1:
                            product(k - 1)
                        scores(k, 2)
                        scores(k, 3)
                        if i == TURN_MAX:
                            pe.wait_ge(sm[f"loaded{(s + 2) % 4}"], LOADS)
                        first_pass(pe, sm, 2 * k, *unit(s, 2 * i))
                        if i == TURN_MAX:
                            pe.wait_ge(sm["o_done"], 2 * s + 1)
                            turn_max(pe, sm, (s + 1) % 4, UNITS * s + REST)
                        first_pass(pe, sm, 2 * k + 1, *unit(s, 2 * i + 1))
                        if i % TPB == TURN_OUT and k >= TPB:
                            turn_output(k // TPB - 1, s)
                    product(STEPS * QUADS - 1)
                    turn_output(2 * QUADS - 1, QUADS)

                @block.scalar
                def _(act):
                    def output(m):
                        act.wait_ge(sm["pv_mm"], TPB * (m + 1))
                        if m >= 2:
                            act.wait_ge(sm["o_turned"], m - 1)
                        nc.scalar.copy(osb[:, m % 2, :], op[:]).then_inc(sm["o_out"], 1)

                    for k in range(STEPS * QUADS):
                        for h in range(4):
                            act.wait_ge(sm["s2_mm"], 4 * k + h + 1)
                            if h == 0 and k >= 2:
                                act.wait_ge(sm["pv_mm"], k - 1)
                            nc.scalar.activation(pr[:, k % 2, h, :], s2[(4 * k + h) % 2][:], ACT.Exp
                                                 ).then_inc(sm["exp"], 1)
                            if h == 1 and k % TPB == 0 and k >= TPB:
                                output(k // TPB - 1)
                    output(2 * QUADS - 1)

                @block.vector
                def _(dve):
                    v = nc.vector

                    def divide(m):
                        s, half = divmod(m, 2)
                        dve.wait_ge(sm["o_turned"], m + 1)
                        heads = mi[:].rearrange("p t (h c) -> p t h c", c=32)
                        v.reciprocal(ro[:, m % 2], heads[:, :, :, HD1]).then_inc(sm["o_rsum"], 1)
                        dve.wait_ge(sm["o_rsum"], m + 1)
                        v.tensor_tensor(
                            K.nat[:, bass.ds(b * TPB + half * CPT, CPT), s * 32:(s + 1) * 32]
                            .rearrange("p t (h d) -> p t h d", d=HD1),
                            heads[:, :, :, 0:HD1], bc(ro[:, m % 2], 3, HD1), ALU.mult).then_inc(sm["o_done"], 1)

                    for s in range(QUADS):
                        for u in range(UNITS):
                            ring, n = unit(s, u)
                            if n == 0 and s >= 1:
                                dve.wait_ge(sm["m_turned"], s)
                            reduce_max(dve, sm, UNITS * s + u, ring, n)
                            if u == 2 * TURN_MAX:
                                negate_max(dve, sm, s)
                            i, odd = divmod(u, 2)
                            if i % TPB == TURN_OUT + 1 and odd == 1 and 2 * s + i // TPB >= 1:
                                divide(2 * s + i // TPB - 1)
                    divide(2 * QUADS - 1)
            nc.all_engine_barrier(sems_to_clear=clear)


class GatedProjection:

    def __init__(self, nc, K, name, w_in, bias_in, st):
        self.nc, self.K, self.w_in, self.bias_in = nc, K, w_in, bias_in
        self.w = K.sb(name + "_w", [P, D], ctx=st)
        self.bias = K.sb(name + "_bias", [P, D], ctx=st)
        self.wg = K.sb(name + "_w_gated", [P, B, D], ctx=st)
        self.bg = K.sb(name + "_bias_gated", [P, B, D], ctx=st)
        (self.loaded, self.gated, self.turned, self.t_out, self.y_mm, self.added) = K.sems(
            st, name, "w_in", "gated", "turned", "turned_out", "y_mm", "added")
        self.name = name

    def buffers(self, st):
        K, name = self.K, self.name
        self.aT = K.sb(name + "_aT", [P, NCH, CH], ctx=st)
        self.tp = [K.ps(f"{name}_tps{i}", [P, CPT, P], st) for i in range(2)]
        self.yp = [K.ps(f"{name}_yps{i}", [P, CPT, D], st) for i in range(2)]

    def load(self, sp):
        sp.dma_start(self.w[:], self.w_in).then_inc(self.loaded, 16)
        sp.dma_start(self.bias[:], self.bias_in.partition_broadcast(P)).then_inc(self.loaded, 16)

    def gate(self, pool):
        g = self.nc.gpsimd
        pool.wait_ge(self.loaded, 32)
        for b in range(B):
            ga = self.K.mod_rows[:, 1, b, GA, :]
            g.tensor_tensor(self.wg[:, b, :], self.w[:], ga, ALU.mult).then_inc(self.gated, 1)
            g.tensor_tensor(self.bg[:, b, :], self.bias[:], ga, ALU.mult).then_inc(self.gated, 1)

    def add_bias(self, b):
        h = self.K.x[:, bass.ds(b * TPB, TPB), :]
        bias = self.bg[:, bass.ds(b, 1), :].rearrange("p a d -> p (a d)")
        self.nc.gpsimd.tensor_tensor(h, h, bc(bias, 1, TPB), ALU.add)

    def products(self, pe):
        pe_, K = self.nc.tensor, self.K
        for c in range(NCH + 1):
            if c < NCH:
                if c >= 2:
                    pe.wait_ge(self.t_out, c - 1)
                for t in range(CPT):
                    m = pe_.transpose(self.tp[c % 2][:, t, :], K.nat[:, c * CPT + t, :], K.ident[:])
                m.then_inc(self.turned, 1)
            if c >= 1:
                k = c - 1
                b = k * CH // T
                pe.wait_ge(self.t_out, k + 1)
                if k >= 2:
                    pe.wait_ge(self.added, k - 1)
                for t in range(CPT):
                    m = pe_.matmul(self.yp[k % 2][:, t, :], self.aT[:, k, t * P:(t + 1) * P], self.wg[:, b, :],
                                   start=True, stop=True)
                m.then_inc(self.y_mm, 1)

    def turned_out(self, act):
        for c in range(NCH):
            act.wait_ge(self.turned, c + 1)
            self.nc.scalar.copy(self.aT[:, c, :], self.tp[c % 2][:].rearrange("p t d -> p (t d)")
                                ).then_inc(self.t_out, 1)

    def add(self, dve, b):
        for c in range(2 * b, 2 * b + 2):
            dve.wait_ge(self.y_mm, c + 1)
            h = self.K.x[:, c * CPT:(c + 1) * CPT, :]
            self.nc.vector.tensor_tensor(h, h, self.yp[c % 2][:], ALU.add).then_inc(self.added, 1)

    def wait_added(self, eng, b):
        eng.wait_ge(self.added, 2 * (b + 1))


def project_stage(nc, K, name, src, w_in_ap):
    with ExitStack() as st:
        w = K.sb(name + "_w", [P, D], ctx=st)
        aT = K.sb(name + "_aT", [P, NCH, CH], ctx=st)
        tp = [K.ps(f"{name}_tps{i}", [P, CPT, P], st) for i in range(4)]
        yp = [K.ps(f"{name}_yps{i}", [P, CPT, D], st) for i in range(4)]
        (w_in, turned, t_out, y_mm, y_out) = K.sems(st, name, "w_in", "turned", "turned_out", "y_mm", "y_out")
        with nc.Block() as block:
            @block.sync
            def _(sp):
                sp.dma_start(w[:], w_in_ap).then_inc(w_in, 16)

            @block.tensor
            def _(pe):
                pe.wait_ge(w_in, 16)
                for c in range(NCH + 1):
                    if c < NCH:
                        if c >= 4:
                            pe.wait_ge(t_out, c - 3)
                        for t in range(CPT):
                            m = nc.tensor.transpose(tp[c % 4][:, t, :], src[:, c * CPT + t, :], K.ident[:])
                        m.then_inc(turned, 1)
                    if c >= 1:
                        k = c - 1
                        pe.wait_ge(t_out, k + 1)
                        if k >= 4:
                            pe.wait_ge(y_out, k - 3)
                        for t in range(CPT):
                            m = nc.tensor.matmul(yp[k % 4][:, t, :], aT[:, k, t * P:(t + 1) * P], w[:],
                                                 start=True, stop=True)
                        m.then_inc(y_mm, 1)

            @block.scalar
            def _(act):
                for c in range(NCH):
                    act.wait_ge(turned, c + 1)
                    nc.scalar.copy(aT[:, c, :], tp[c % 4][:].rearrange("p t d -> p (t d)")).then_inc(t_out, 1)

            @block.vector
            def _(dve):
                for c in range(NCH):
                    dve.wait_ge(y_mm, c + 1)
                    h = K.nat[:, c * CPT:(c + 1) * CPT, :]
                    nc.vector.tensor_tensor(h, h, yp[c % 4][:], ALU.add).then_inc(y_out, 1)


def cross_attention_stage(nc, K, A, attended):
    QW, KW = H1 * HD1, KV2 * HD1
    pairs = [(s, t) for s in range(B) for t in range(s + 1)]
    first = [sum(range(s + 1)) for s in range(B)]
    NP = len(pairs)
    R = H1 // KV2
    with ExitStack() as st:
        w = K.sb("x_wT", [P, QKV2], ctx=st)
        q = K.sb("x_q", [P, NT, QW], ctx=st)
        k = K.sb("x_k", [P, NT, KW], ctx=st)
        vv = K.sb("x_v", [P, NT, KW], ctx=st)
        pd = K.sb("x_prod", [P, 2, TPB, QW], ctx=st)
        sc = K.sb("x_scores", [P, NP, TPB * H1], ctx=st)
        mx = K.sb("x_max", [P, B, TPB * H1], ctx=st)
        sm = K.sb("x_sum", [P, B, TPB * H1], ctx=st)
        yp = [K.ps(f"x_ps{i}", [P, CH], st) for i in range(4)]
        (w_in, mm, qkv_out, pdone, sdone, smx, exped, nrm, pv, summed) = K.sems(
            st, "cross", "w_in", "qkv_mm", "qkv_out", "product", "score", "softmax", "exp", "norm", "pv", "summed")
        with nc.Block() as block:
            @block.sync
            def _(sp):
                sp.dma_start(w[:], A["L1_ffn_qkvT"]).then_inc(w_in, 16)
                sp.wait_ge(w_in, 16)

            @block.tensor
            def _(pe):
                pe.wait_ge(w_in, 16)
                for n in range(NT // 2):
                    if n >= 4:
                        pe.wait_ge(qkv_out, n - 3)
                    for i in range(2):
                        t = 2 * n + i
                        m = nc.tensor.matmul(yp[n % 4][:, i * QKV2:(i + 1) * QKV2], K.hT[:, t * P:(t + 1) * P], w[:],
                                             start=True, stop=True)
                    m.then_inc(mm, 1)

            @block.scalar
            def _(act):
                for n in range(NT // 2):
                    act.wait_ge(mm, n + 1)
                    y = yp[n % 4][:, 0:2 * QKV2].rearrange("p (t c) -> p t c", t=2)
                    t2 = slice(2 * n, 2 * n + 2)
                    nc.scalar.copy(q[:, t2, :], y[:, :, 0:QW])
                    nc.scalar.copy(k[:, t2, :], y[:, :, QW:QW + KW])
                    nc.scalar.copy(vv[:, t2, :], y[:, :, QW + KW:QKV2]).then_inc(qkv_out, 1)
                act.wait_ge(smx, 2 * NP)
                nc.scalar.activation(sc[:], sc[:], ACT.Exp, scale=HD1 ** -0.5).then_inc(exped, 1)

            def grouped(ap):
                return ap.rearrange("p t (g r d) -> p (t g) r d", r=R, d=HD1)

            def shared(ap):
                return bc(ap.rearrange("p t (g d) -> p (t g) d", d=HD1), 2, R)

            def tiles(s):
                return slice(s * TPB, (s + 1) * TPB)

            @block.vector
            def _(dve):
                v = nc.vector
                for n, (s, t) in enumerate(pairs):
                    dve.wait_ge(qkv_out, (max(s, t) + 1) * TPB // 2)
                    if n >= 2:
                        dve.wait_ge(sdone, n - 1)
                    v.tensor_tensor(grouped(pd[:, n % 2]), grouped(q[:, tiles(s), :]), shared(k[:, tiles(t), :]),
                                    ALU.mult).then_inc(pdone, 1)
                    dve.wait_ge(pdone, n + 1)
                    v.tensor_reduce(sc[:, n, :], pd[:, n % 2].rearrange("p t (h d) -> p (t h) d", d=HD1), AX.X,
                                    ALU.add).then_inc(sdone, 1)
                dve.wait_ge(sdone, NP)
                count = 0
                for s in range(B):
                    f = first[s]
                    v.tensor_copy(mx[:, s, :], sc[:, f, :]).then_inc(smx, 1)
                    count += 1
                    for t in range(1, s + 1):
                        dve.wait_ge(smx, count)
                        v.tensor_tensor(mx[:, s, :], mx[:, s, :], sc[:, f + t, :], ALU.max).then_inc(smx, 1)
                        count += 1
                    dve.wait_ge(smx, count)
                for n, (s, t) in enumerate(pairs):
                    v.tensor_tensor(sc[:, n, :], sc[:, n, :], mx[:, s, :], ALU.subtract).then_inc(smx, 1)
                    count += 1
                assert count == 2 * NP
                dve.wait_ge(exped, 1)
                count = 0
                for s in range(B):
                    f = first[s]
                    v.tensor_copy(sm[:, s, :], sc[:, f, :]).then_inc(nrm, 1)
                    count += 1
                    for t in range(1, s + 1):
                        dve.wait_ge(nrm, count)
                        v.tensor_tensor(sm[:, s, :], sm[:, s, :], sc[:, f + t, :], ALU.add).then_inc(nrm, 1)
                        count += 1
                dve.wait_ge(nrm, count)
                v.reciprocal(mx[:], sm[:]).then_inc(nrm, 1)
                count += 1
                dve.wait_ge(nrm, count)
                for n, (s, t) in enumerate(pairs):
                    v.tensor_tensor(sc[:, n, :], sc[:, n, :], mx[:, s, :], ALU.mult).then_inc(nrm, 1)
                    count += 1
                dve.wait_ge(nrm, count)
                for n, (s, t) in enumerate(pairs):
                    weight = bc(sc[:, n, :].rearrange("p (m r) -> p m r", r=R), 3, HD1)
                    if n >= 2:
                        added = sum(t_ > 0 for _, t_ in pairs[:n - 1])
                        if added:
                            dve.wait_ge(summed, added)
                    v.tensor_tensor(grouped(attended[:, tiles(s), :] if t == 0 else pd[:, n % 2]),
                                    shared(vv[:, tiles(t), :]), weight, ALU.mult).then_inc(pv, 1)

            @block.gpsimd
            def _(pool):
                done = 0
                for n, (s, t) in enumerate(pairs):
                    if t:
                        pool.wait_ge(pv, n + 1)
                        if t >= 2:
                            pool.wait_ge(summed, done)
                        o = attended[:, tiles(s), :]
                        nc.gpsimd.tensor_tensor(o, o, pd[:, n % 2], ALU.add).then_inc(summed, 1)
                        done += 1


def build(nc, A, out):
    with ExitStack() as ctx:
        K = Core(nc, ctx)
        K.win_sems = K.loop_sems(
            "win", "h_in", "proj_mm", "act_out", "q_out", "v_shift_even", "v_shift_odd", "score_mm", "biased", "exp",
            "rsum", "normed", "turned", "probsT_out", "pv_mm", "o_out", "wo_mm", "wo_gated")
        K.moe_sems = K.loop_sems("moe", "h_hi", "h_lo", "hidden_mm", "gelu", "hidden_hi", "hidden_lo", "weights_mm",
                                  "weights_out", "y_mm", "y_weighed", "y_summed", "x_out")
        K.att_sems = K.loop_sems("att1", *ATT_SEMS)
        K.x = K.sb("x", [P, NT, D])
        K.nat = K.sb("nat", [P, NT, D])
        K.hT = K.sb("hT", [P, B * T + CH])
        K.w = K.sb("expert_w", [P, NT, E])
        K.mod_cols = K.sb("mod_cols", [P, 2, 6, B])
        K.mod_rows = K.sb("mod_rows", [P, 2, B, 6, D])
        K.ident = K.sb("ident", [P, P])
        K.neghalf = K.sb("neghalf", [P, NT])

        with ExitStack() as st:
            gram = K.sb("gram", [P, 2, D], ctx=st)
            start_stage(nc, K, A, gram)
            window_attention_stage(nc, K, A, gram)
        with ExitStack() as st:
            M = Experts(K, "moe0", F0, A["L0_ffn_W1T"], A["L0_ffn_W2T"], A["L0_ffn_b1c"], A["L0_ffn_WgT"],
                        A["L0_ffn_bg"], st)
            double_norm_stage(nc, K, A, "n0b", 0, CB, SB, ("L0_ffn_gamma", "L0_ffn_beta"), M)
            routing_stage(nc, K, A, "rt0", A["L0_ffn_b2"], True, M)
            expert_stage(nc, K, "moe0", M, ACT.Gelu, 0)
        with ExitStack() as st:
            wo = GatedProjection(nc, K, "wo1", A["L1_attn_WoT"], A["L1_attn_bo"], st)
            full_attention_stage(nc, K, A, wo)
            double_norm_stage(nc, K, A, "n1b", 1, CB, SB, ("L1_ffn_ln1_weight", "L1_ffn_ln1_bias"), before=wo)
        with ExitStack() as st:
            attended = K.sb("attended", [P, NT, D], ctx=st)
            cross_attention_stage(nc, K, A, attended)
            project_stage(nc, K, "pj1", attended, A["L1_ffn_projT"])
        with ExitStack() as st:
            M = Experts(K, "moe1", F1, A["L1_ffn_moe_w1"], A["L1_ffn_moe_w2"], None, A["L1_ffn_routerT"], None, st)
            last_norm_stage(nc, K, A, "n1d", ("L1_ffn_ln2_weight", "L1_ffn_ln2_bias"), M)
            routing_stage(nc, K, A, "rt1", None, False, M)
            expert_stage(nc, K, "moe1", M, ACT.Gelu_apprx_tanh, 1, out)


def constants():
    slopes = np.array([2.0 ** (-0.5 * (i + 1)) for i in range(H0)])
    r = np.arange(BLK)[:, None]
    c = np.arange(P)[None, :]
    dist = c - BLK - r
    neg = np.empty((2, BLK, PAIRS, 2, P), np.float32)
    for h in range(H0):
        for v in range(2):
            ok = (dist <= 0) & (dist >= -WIN) & ((c >= BLK) | (v == 0))
            neg[h % 2, :, h // 2, v, :] = np.where(ok, -slopes[h] * dist, 1e30)
    lower = (np.arange(E)[None, :] < np.arange(E)[:, None]).astype(np.float32).reshape(1, -1)
    lower = np.broadcast_to(lower, (P, E * E))
    select = np.zeros((KROWS, E, P), np.float32)
    for row in range(3 * E):
        select[row, row % E, :] = 1.0
    return {"identity": np.eye(P, dtype=np.float32), "neg_bias": neg.reshape(P, PAIRS, 2, P),
            "lower": np.ascontiguousarray(lower), "select": select.reshape(KROWS, E * P)}


AS_IS = ("L0_attn_x", "L0_attn_wq", "L0_attn_wk", "L0_ffn_gamma", "L0_ffn_beta",
         "L0_ffn_bg", "L0_ffn_b2", "L0_wmod", "L1_attn_bq", "L1_attn_bk", "L1_attn_bv", "L1_attn_bo",
         "L1_ffn_ln1_weight", "L1_ffn_ln1_bias", "L1_ffn_ln2_weight", "L1_ffn_ln2_bias", "L1_ffn_moe_w1",
         "L1_ffn_moe_w2", "L1_wmod")
TURNED = {"L0_attn_wqT": "L0_attn_wq", "L0_attn_wkT": "L0_attn_wk", "L0_attn_wvT": "L0_attn_wv",
          "L0_attn_woT": "L0_attn_wo", "L0_ffn_WgT": "L0_ffn_Wg", "L0_ffn_W1T": "L0_ffn_W1", "L0_ffn_W2T": "L0_ffn_W2",
          "L0_c": "L0_c", "L1_c": "L1_c", "L1_attn_WqT": "L1_attn_Wq", "L1_attn_WkT": "L1_attn_Wk",
          "L1_attn_WvT": "L1_attn_Wv", "L1_attn_WoT": "L1_attn_Wo", "L1_ffn_qkvT": "L1_ffn_qkv_weight",
          "L1_ffn_projT": "L1_ffn_proj_weight", "L1_ffn_routerT": "L1_ffn_router_weight"}


def kernel(**inputs):
    import numpy as _np
    import concourse.bacc as _bacc
    from concourse import mybir as _mybir
    from concourse.bass_utils import run_bass_kernel_spmd as _run

    data = {n: _np.asarray(inputs[n]) for n in AS_IS}
    for n, of in TURNED.items():
        data[n] = _np.swapaxes(_np.asarray(inputs[of]), -1, -2)
    data["L0_ffn_b1c"] = _np.asarray(inputs["L0_ffn_b1"]).reshape(E * F0 // P, P).T
    for n in "qk":
        data[f"L0_attn_{n}_norm_c"] = _np.asarray(inputs[f"L0_attn_{n}_norm_w"]).reshape(PAIRS, P).T
    data.update(constants())
    nc = _bacc.Bacc("TRN2", target_bir_lowering=False, num_devices=1)
    arrays, A = {}, {}
    for n, a in data.items():
        a = _np.ascontiguousarray(a)
        arrays[f"in_{n}"] = a
        A[n] = nc.dram_tensor(f"in_{n}", a.shape, _mybir.dt.from_np(a.dtype), kind="ExternalInput").ap()
    out = nc.dram_tensor("out_x", (B, T, D), F32, kind="ExternalOutput").ap()
    build(nc, A, out)
    r = _run(nc, [arrays], core_ids=[0])
    return r.results[0]["out_x"]
```
